# Optimizing a Trainium2 kernel written in Bass

```python
import numpy as np
import jax
import jax.numpy as jnp

def _softmax(x, axis=-1):
    return jax.nn.softmax(x, axis=axis)

def _gelu(x):
    return jax.nn.gelu(x, approximate=True)

def _silu(x):
    return jax.nn.silu(x)

def _sigmoid(x):
    return jax.nn.sigmoid(x)

def _layernorm(x, axis=-1, eps=1e-05):
    m = jnp.mean(x, axis=axis, keepdims=True)
    v = jnp.var(x, axis=axis, keepdims=True)
    return (x - m) / jnp.sqrt(v + eps)

def _scatter_add(tgt, idx, src, axis=0):
    return tgt.at[idx].add(src)

def _segment_sum(src, seg, n):
    return jax.ops.segment_sum(src, seg, n)
kernel_name = 'mk_decoder_preln_d1_seqx_r4_3ada2b'

def setup_inputs(seed: int=0):
    np.random.seed(seed)
    _w = jnp.asarray

    def _rec_inputs():
        import jax
        import jax.numpy as jnp
        _rk = jax.random.key(seed)
        x = -0.0002928 + 1 * jax.random.normal(jax.random.fold_in(_rk, 1), (32, 100, 512), jnp.float32)
        _lenS = 100 - jax.random.randint(jax.random.fold_in(_rk, 7), (32,), 0, max(1, 100 // 4) + 1, jnp.int32)
        _lenS2 = 361 - jax.random.randint(jax.random.fold_in(_rk, 8), (32,), 0, max(1, 361 // 4) + 1, jnp.int32)
        _ctx_2048P = jax.random.normal(jax.random.fold_in(_rk, 11), (32, 16, 512), jnp.float32)
        _ctx_2048c = jax.random.dirichlet(jax.random.fold_in(_rk, 511), 0.3 * jnp.ones((16,), jnp.float32), (32, 361))
        _ctx_2048t = jnp.einsum('bsk,bkd->bsd', _ctx_2048c, _ctx_2048P)
        _ctx_2048t = _ctx_2048t * jax.lax.rsqrt(jnp.mean(jnp.square(_ctx_2048t)) + 1e-12) * 0.953939
        ctx_2048 = 4.13588e-05 + 0.999923 * (_ctx_2048t + 0.3 * jax.random.normal(jax.random.fold_in(_rk, 611), (32, 361, 512), jnp.float32))
        _validS = jnp.arange(100)[None, :] < _lenS[:, None]
        _validS2 = jnp.arange(361)[None, :] < _lenS2[:, None]
        _causal = jnp.tril(jnp.ones((100, 100), dtype=bool))
        mask_1xSxS2_ff0 = jnp.where(jnp.ones((1, 100, 361), dtype=bool), 0.0, -1000000000.0).astype(jnp.float32)
        return (x, ctx_2048, mask_1xSxS2_ff0)
    x, ctx_2048, mask_1xSxS2_ff0 = _rec_inputs()

    def _L0_attn_setup():
        import jax, jax.numpy as jnp
        import numpy as np
        from jax import lax
        BATCH = 2
        SEQ = 512
        HID = 512
        EXPAND = 2
        INTER = EXPAND * HID
        HEADS = 64
        PDIM = INTER // HEADS
        NSTATE = 128
        G = 1
        HPG = HEADS // G
        KCONV = 4
        GTS = G * NSTATE
        CONV_DIM = INTER + 2 * GTS
        PROJ_DIM = 2 * INTER + 2 * GTS + HEADS
        EPS = 1e-05
        MUP = (0.25, 0.5, 0.5, 0.5, 1.0)

        def _mup_vector():
            return jnp.concatenate([jnp.full((INTER,), MUP[0], jnp.float32), jnp.full((INTER,), MUP[1], jnp.float32), jnp.full((GTS,), MUP[2], jnp.float32), jnp.full((GTS,), MUP[3], jnp.float32), jnp.full((HEADS,), MUP[4], jnp.float32)])

        def _forward(hidden_states, in_proj_w, conv_w, conv_b, A_log, D, dt_bias, norm_w, out_proj_w):
            b, l, _ = hidden_states.shape
            proj = hidden_states @ in_proj_w * _mup_vector()
            z = proj[..., :INTER]
            xBC = proj[..., INTER:INTER + CONV_DIM]
            dt = proj[..., INTER + CONV_DIM:]
            xBC_cl = jnp.swapaxes(xBC, 1, 2)
            conv = lax.conv_general_dilated(xBC_cl, conv_w[:, None, :], window_strides=(1,), padding=((KCONV - 1, 0),), feature_group_count=CONV_DIM)
            xBC = jax.nn.silu(jnp.swapaxes(conv + conv_b[None, :, None], 1, 2))
            x = xBC[..., :INTER].reshape(b, l, G, HPG, PDIM)
            Bm = xBC[..., INTER:INTER + GTS].reshape(b, l, G, NSTATE)
            Cm = xBC[..., INTER + GTS:].reshape(b, l, G, NSTATE)
            dt = jax.nn.softplus(dt + dt_bias)
            A = -jnp.exp(A_log)
            dA = jnp.exp(dt * A).reshape(b, l, G, HPG)
            dtx = dt.reshape(b, l, G, HPG)[..., None] * x

            def step(state, inp):
                dA_t, dtx_t, B_t, C_t = inp
                state = state * dA_t[..., None, None] + jnp.einsum('bgcp,bgn->bgcpn', dtx_t, B_t)
                y_t = jnp.einsum('bgn,bgcpn->bgcp', C_t, state)
                return (state, y_t)
            inputs = (jnp.moveaxis(dA, 1, 0), jnp.moveaxis(dtx, 1, 0), jnp.moveaxis(Bm, 1, 0), jnp.moveaxis(Cm, 1, 0))
            state0 = jnp.zeros((b, G, HPG, PDIM, NSTATE), hidden_states.dtype)
            _, ys = lax.scan(step, state0, inputs)
            y = jnp.moveaxis(ys, 0, 1) + D.reshape(1, 1, G, HPG, 1) * x
            y = y.reshape(b, l, INTER)
            yg = y.reshape(b, l, G, INTER // G)
            var = jnp.mean(jnp.square(yg), axis=-1, keepdims=True)
            yn = (yg * lax.rsqrt(var + EPS)).reshape(b, l, INTER) * norm_w
            out = yn * jax.nn.silu(z)
            return out @ out_proj_w
        key = jax.random.key(seed)
        ks = jax.random.split(key, 8)
        hidden_states = jax.random.normal(ks[0], (BATCH, SEQ, HID), jnp.float32)
        in_proj_w = jax.random.normal(ks[1], (HID, PROJ_DIM), jnp.float32) * 0.02
        conv_w = jax.random.normal(ks[2], (CONV_DIM, KCONV), jnp.float32) * 0.2
        conv_b = jnp.zeros((CONV_DIM,), jnp.float32)
        A_log = jnp.log(jnp.arange(1, HEADS + 1, dtype=jnp.float32))
        D = jnp.ones((HEADS,), jnp.float32)
        dt_bias = jax.random.uniform(ks[3], (HEADS,), jnp.float32)
        norm_w = jnp.ones((INTER,), jnp.float32)
        out_proj_w = jax.random.normal(ks[4], (INTER, HID), jnp.float32) * 0.02
        return dict(hidden_states=hidden_states, in_proj_w=in_proj_w, conv_w=conv_w, conv_b=conv_b, A_log=A_log, D=D, dt_bias=dt_bias, norm_w=norm_w, out_proj_w=out_proj_w)
    _L0_attn_all = _L0_attn_setup()
    _L0_attn_in = {k: v for k, v in _L0_attn_all.items() if k in ('in_proj_w', 'conv_w', 'conv_b', 'A_log', 'D', 'dt_bias', 'norm_w', 'out_proj_w')}
    del _L0_attn_all

    def _L0_xattn_setup():
        import jax, jax.numpy as jnp
        import numpy as np
        H = 512
        NH = 16
        NKV = 4
        HD = 128
        GROUPS = NH // NKV
        EPS = 1e-06
        B, S, SE = (1, 512, 1024)

        def _rmsnorm(x, w, eps=EPS):
            xf = x.astype(jnp.float32)
            var = jnp.mean(xf * xf, axis=-1, keepdims=True)
            return (xf * jax.lax.rsqrt(var + eps)).astype(x.dtype) * w
        key = jax.random.key(seed)
        ks = jax.random.split(key, 12)
        sc = 0.02
        return {'hidden_states': jax.random.normal(ks[0], (B, S, H), jnp.float32), 'encoder_hidden_states': jax.random.normal(ks[1], (B, SE, H), jnp.float32), 'attention_mask': jnp.zeros((B, S, SE), jnp.float32), 'Wq': jax.random.normal(ks[2], (H, NH * HD), jnp.float32) * sc, 'bq': jax.random.normal(ks[3], (NH * HD,), jnp.float32) * sc, 'Wk': jax.random.normal(ks[4], (H, NKV * HD), jnp.float32) * sc, 'bk': jax.random.normal(ks[5], (NKV * HD,), jnp.float32) * sc, 'Wv': jax.random.normal(ks[6], (H, NKV * HD), jnp.float32) * sc, 'bv': jax.random.normal(ks[7], (NKV * HD,), jnp.float32) * sc, 'Wo': jax.random.normal(ks[8], (NH * HD, H), jnp.float32) * sc, 'qn_w': jnp.ones((HD,), jnp.float32), 'kn_w': jnp.ones((HD,), jnp.float32)}
    _L0_xattn_all = _L0_xattn_setup()
    _L0_xattn_in = {k: v for k, v in _L0_xattn_all.items() if k in ('Wq', 'bq', 'Wk', 'bk', 'Wv', 'bv', 'Wo', 'qn_w', 'kn_w')}
    del _L0_xattn_all

    def _L0_ffn_setup():
        import jax, jax.numpy as jnp
        import numpy as np
        H = 512
        I = 352
        E = 16
        K = 2
        N_SHARED = 2
        IS = I * N_SHARED
        ROUTED_SCALE = 1.0
        CAPACITY = 256

        def _moe_forward(hidden_states, gate_w, w_gate, w_up, w_down, ws_gate, ws_up, ws_down):
            B, S, _ = hidden_states.shape
            x = hidden_states.reshape(-1, H)
            T = x.shape[0]
            logits = jnp.einsum('th,eh->te', x.astype(jnp.float32), gate_w.astype(jnp.float32))
            scores = jax.nn.softmax(logits, axis=-1)
            topk_w, topk_idx = jax.lax.top_k(scores, K)
            topk_w = (topk_w * ROUTED_SCALE).astype(x.dtype)
            flat_idx = topk_idx.reshape(-1)
            order = jnp.argsort(flat_idx)
            sorted_e = flat_idx[order]
            sorted_t = order // K
            counts = jnp.bincount(flat_idx, length=E)
            starts = jnp.cumsum(counts) - counts
            pos = jnp.arange(T * K) - starts[sorted_e]
            buf = jnp.zeros((E, CAPACITY, H), x.dtype).at[sorted_e, pos].set(x[sorted_t], mode='drop')
            g = jax.nn.silu(jnp.einsum('ech,ehi->eci', buf, w_gate))
            u = jnp.einsum('ech,ehi->eci', buf, w_up)
            expert_out = jnp.einsum('eci,eih->ech', g * u, w_down)
            gathered = expert_out[sorted_e, pos]
            out_flat = jnp.zeros((T * K, H), x.dtype).at[order].set(gathered)
            y = (out_flat.reshape(T, K, H) * topk_w[..., None]).sum(axis=1)
            sh = jnp.einsum('ti,ih->th', jax.nn.silu(x @ ws_gate) * (x @ ws_up), ws_down)
            return (y + sh).reshape(B, S, H)
        key = jax.random.key(seed)
        ks = jax.random.split(key, 8)
        B, S = (2, 256)
        scale = 0.02
        return {'hidden_states': jax.random.normal(ks[0], (B, S, H), jnp.float32), 'gate_w': jax.random.normal(ks[1], (E, H), jnp.float32) * scale, 'w_gate': jax.random.normal(ks[2], (E, H, I), jnp.float32) * scale, 'w_up': jax.random.normal(ks[3], (E, H, I), jnp.float32) * scale, 'w_down': jax.random.normal(ks[4], (E, I, H), jnp.float32) * scale, 'ws_gate': jax.random.normal(ks[5], (H, IS), jnp.float32) * scale, 'ws_up': jax.random.normal(ks[6], (H, IS), jnp.float32) * scale, 'ws_down': jax.random.normal(ks[7], (IS, H), jnp.float32) * scale}
    _L0_ffn_all = _L0_ffn_setup()
    _L0_ffn_in = {k: v for k, v in _L0_ffn_all.items() if k in ('gate_w', 'w_gate', 'w_up', 'w_down', 'ws_gate', 'ws_up', 'ws_down')}
    del _L0_ffn_all
    return {'x': x, 'ctx_2048': ctx_2048, 'mask_1xSxS2_ff0': mask_1xSxS2_ff0, 'L0_attn_in_proj_w': _L0_attn_in['in_proj_w'], 'L0_attn_conv_w': _L0_attn_in['conv_w'], 'L0_attn_conv_b': _L0_attn_in['conv_b'], 'L0_attn_A_log': _L0_attn_in['A_log'], 'L0_attn_D': _L0_attn_in['D'], 'L0_attn_dt_bias': _L0_attn_in['dt_bias'], 'L0_attn_norm_w': _L0_attn_in['norm_w'], 'L0_attn_out_proj_w': _L0_attn_in['out_proj_w'], 'L0_xattn_Wq': _L0_xattn_in['Wq'], 'L0_xattn_bq': _L0_xattn_in['bq'], 'L0_xattn_Wk': _L0_xattn_in['Wk'], 'L0_xattn_bk': _L0_xattn_in['bk'], 'L0_xattn_Wv': _L0_xattn_in['Wv'], 'L0_xattn_bv': _L0_xattn_in['bv'], 'L0_xattn_Wo': _L0_xattn_in['Wo'], 'L0_xattn_qn_w': _L0_xattn_in['qn_w'], 'L0_xattn_kn_w': _L0_xattn_in['kn_w'], 'L0_ffn_gate_w': _L0_ffn_in['gate_w'], 'L0_ffn_w_gate': _L0_ffn_in['w_gate'], 'L0_ffn_w_up': _L0_ffn_in['w_up'], 'L0_ffn_w_down': _L0_ffn_in['w_down'], 'L0_ffn_ws_gate': _L0_ffn_in['ws_gate'], 'L0_ffn_ws_up': _L0_ffn_in['ws_up'], 'L0_ffn_ws_down': _L0_ffn_in['ws_down']}

def reference(x, ctx_2048, mask_1xSxS2_ff0, L0_attn_in_proj_w, L0_attn_conv_w, L0_attn_conv_b, L0_attn_A_log, L0_attn_D, L0_attn_dt_bias, L0_attn_norm_w, L0_attn_out_proj_w, L0_xattn_Wq, L0_xattn_bq, L0_xattn_Wk, L0_xattn_bk, L0_xattn_Wv, L0_xattn_bv, L0_xattn_Wo, L0_xattn_qn_w, L0_xattn_kn_w, L0_ffn_gate_w, L0_ffn_w_gate, L0_ffn_w_up, L0_ffn_w_down, L0_ffn_ws_gate, L0_ffn_ws_up, L0_ffn_ws_down):
    import jax
    import jax.numpy as jnp

    def _L0_attn_ref(hidden_states, in_proj_w, conv_w, conv_b, A_log, D, dt_bias, norm_w, out_proj_w):
        import jax, jax.numpy as jnp
        import numpy as np
        from jax import lax
        BATCH = 2
        SEQ = 512
        HID = 512
        EXPAND = 2
        INTER = EXPAND * HID
        HEADS = 64
        PDIM = INTER // HEADS
        NSTATE = 128
        G = 1
        HPG = HEADS // G
        KCONV = 4
        GTS = G * NSTATE
        CONV_DIM = INTER + 2 * GTS
        PROJ_DIM = 2 * INTER + 2 * GTS + HEADS
        EPS = 1e-05
        MUP = (0.25, 0.5, 0.5, 0.5, 1.0)

        def _mup_vector():
            return jnp.concatenate([jnp.full((INTER,), MUP[0], jnp.float32), jnp.full((INTER,), MUP[1], jnp.float32), jnp.full((GTS,), MUP[2], jnp.float32), jnp.full((GTS,), MUP[3], jnp.float32), jnp.full((HEADS,), MUP[4], jnp.float32)])

        def _forward(hidden_states, in_proj_w, conv_w, conv_b, A_log, D, dt_bias, norm_w, out_proj_w):
            b, l, _ = hidden_states.shape
            proj = hidden_states @ in_proj_w * _mup_vector()
            z = proj[..., :INTER]
            xBC = proj[..., INTER:INTER + CONV_DIM]
            dt = proj[..., INTER + CONV_DIM:]
            xBC_cl = jnp.swapaxes(xBC, 1, 2)
            conv = lax.conv_general_dilated(xBC_cl, conv_w[:, None, :], window_strides=(1,), padding=((KCONV - 1, 0),), feature_group_count=CONV_DIM)
            xBC = jax.nn.silu(jnp.swapaxes(conv + conv_b[None, :, None], 1, 2))
            x = xBC[..., :INTER].reshape(b, l, G, HPG, PDIM)
            Bm = xBC[..., INTER:INTER + GTS].reshape(b, l, G, NSTATE)
            Cm = xBC[..., INTER + GTS:].reshape(b, l, G, NSTATE)
            dt = jax.nn.softplus(dt + dt_bias)
            A = -jnp.exp(A_log)
            dA = jnp.exp(dt * A).reshape(b, l, G, HPG)
            dtx = dt.reshape(b, l, G, HPG)[..., None] * x

            def step(state, inp):
                dA_t, dtx_t, B_t, C_t = inp
                state = state * dA_t[..., None, None] + jnp.einsum('bgcp,bgn->bgcpn', dtx_t, B_t)
                y_t = jnp.einsum('bgn,bgcpn->bgcp', C_t, state)
                return (state, y_t)
            inputs = (jnp.moveaxis(dA, 1, 0), jnp.moveaxis(dtx, 1, 0), jnp.moveaxis(Bm, 1, 0), jnp.moveaxis(Cm, 1, 0))
            state0 = jnp.zeros((b, G, HPG, PDIM, NSTATE), hidden_states.dtype)
            _, ys = lax.scan(step, state0, inputs)
            y = jnp.moveaxis(ys, 0, 1) + D.reshape(1, 1, G, HPG, 1) * x
            y = y.reshape(b, l, INTER)
            yg = y.reshape(b, l, G, INTER // G)
            var = jnp.mean(jnp.square(yg), axis=-1, keepdims=True)
            yn = (yg * lax.rsqrt(var + EPS)).reshape(b, l, INTER) * norm_w
            out = yn * jax.nn.silu(z)
            return out @ out_proj_w
        return _forward(hidden_states, in_proj_w, conv_w, conv_b, A_log, D, dt_bias, norm_w, out_proj_w)

    def _L0_xattn_ref(hidden_states, encoder_hidden_states, attention_mask, Wq, bq, Wk, bk, Wv, bv, Wo, qn_w, kn_w):
        import jax, jax.numpy as jnp
        import numpy as np
        H = 512
        NH = 16
        NKV = 4
        HD = 128
        GROUPS = NH // NKV
        EPS = 1e-06
        B, S, SE = (1, 512, 1024)

        def _rmsnorm(x, w, eps=EPS):
            xf = x.astype(jnp.float32)
            var = jnp.mean(xf * xf, axis=-1, keepdims=True)
            return (xf * jax.lax.rsqrt(var + eps)).astype(x.dtype) * w
        b, s, _ = hidden_states.shape
        se = encoder_hidden_states.shape[1]
        q = (hidden_states @ Wq + bq).reshape(b, s, NH, HD).transpose(0, 2, 1, 3)
        k = (encoder_hidden_states @ Wk + bk).reshape(b, se, NKV, HD).transpose(0, 2, 1, 3)
        v = (encoder_hidden_states @ Wv + bv).reshape(b, se, NKV, HD).transpose(0, 2, 1, 3)
        k = jnp.repeat(k, GROUPS, axis=1)
        v = jnp.repeat(v, GROUPS, axis=1)
        q = _rmsnorm(q, qn_w)
        k = _rmsnorm(k, kn_w)
        scale = 1.0 / np.sqrt(HD).astype(np.float32)
        scores = jnp.einsum('bhsd,bhed->bhse', q, k) * scale
        scores = scores + attention_mask[:, None, :, :]
        probs = jax.nn.softmax(scores.astype(jnp.float32), axis=-1).astype(q.dtype)
        out = jnp.einsum('bhse,bhed->bhsd', probs, v)
        out = out.transpose(0, 2, 1, 3).reshape(b, s, NH * HD)
        return out @ Wo

    def _L0_ffn_ref(hidden_states, gate_w, w_gate, w_up, w_down, ws_gate, ws_up, ws_down):
        import jax, jax.numpy as jnp
        import numpy as np
        H = 512
        I = 352
        E = 16
        K = 2
        N_SHARED = 2
        IS = I * N_SHARED
        ROUTED_SCALE = 1.0
        CAPACITY = 256

        def _moe_forward(hidden_states, gate_w, w_gate, w_up, w_down, ws_gate, ws_up, ws_down):
            B, S, _ = hidden_states.shape
            x = hidden_states.reshape(-1, H)
            T = x.shape[0]
            logits = jnp.einsum('th,eh->te', x.astype(jnp.float32), gate_w.astype(jnp.float32))
            scores = jax.nn.softmax(logits, axis=-1)
            topk_w, topk_idx = jax.lax.top_k(scores, K)
            topk_w = (topk_w * ROUTED_SCALE).astype(x.dtype)
            flat_idx = topk_idx.reshape(-1)
            order = jnp.argsort(flat_idx)
            sorted_e = flat_idx[order]
            sorted_t = order // K
            counts = jnp.bincount(flat_idx, length=E)
            starts = jnp.cumsum(counts) - counts
            pos = jnp.arange(T * K) - starts[sorted_e]
            buf = jnp.zeros((E, CAPACITY, H), x.dtype).at[sorted_e, pos].set(x[sorted_t], mode='drop')
            g = jax.nn.silu(jnp.einsum('ech,ehi->eci', buf, w_gate))
            u = jnp.einsum('ech,ehi->eci', buf, w_up)
            expert_out = jnp.einsum('eci,eih->ech', g * u, w_down)
            gathered = expert_out[sorted_e, pos]
            out_flat = jnp.zeros((T * K, H), x.dtype).at[order].set(gathered)
            y = (out_flat.reshape(T, K, H) * topk_w[..., None]).sum(axis=1)
            sh = jnp.einsum('ti,ih->th', jax.nn.silu(x @ ws_gate) * (x @ ws_up), ws_down)
            return (y + sh).reshape(B, S, H)
        return _moe_forward(hidden_states, gate_w, w_gate, w_up, w_down, ws_gate, ws_up, ws_down)
    x = x + _L0_attn_ref(_layernorm(x, axis=-1), L0_attn_in_proj_w, L0_attn_conv_w, L0_attn_conv_b, L0_attn_A_log, L0_attn_D, L0_attn_dt_bias, L0_attn_norm_w, L0_attn_out_proj_w)
    x = x + _L0_xattn_ref(_layernorm(x, axis=-1), ctx_2048, mask_1xSxS2_ff0, L0_xattn_Wq, L0_xattn_bq, L0_xattn_Wk, L0_xattn_bk, L0_xattn_Wv, L0_xattn_bv, L0_xattn_Wo, L0_xattn_qn_w, L0_xattn_kn_w)
    x = x + _L0_ffn_ref(_layernorm(x, axis=-1), L0_ffn_gate_w, L0_ffn_w_gate, L0_ffn_w_up, L0_ffn_w_down, L0_ffn_ws_gate, L0_ffn_ws_up, L0_ffn_ws_down)
    return x

_drawn_inputs = setup_inputs


def setup_inputs(seed=0):
    import zlib

    import numpy as np

    out = dict(_drawn_inputs(seed))
    spreads = {'L0_attn_conv_b': (0.0, 0.1),
     'L0_attn_D': (1.0, 0.6),
     'L0_attn_norm_w': (1.0, 0.6),
     'L0_xattn_qn_w': (1.0, 0.6),
     'L0_xattn_kn_w': (1.0, 0.6)}
    factors = {'L0_attn_A_log': 8.0,
     'L0_attn_dt_bias': 8.0,
     'L0_xattn_bq': 8.0,
     'L0_xattn_bk': 8.0,
     'L0_xattn_bv': 3.086,
     'L0_ffn_gate_w': 8.0,
     'L0_ffn_w_gate': 8.0,
     'L0_ffn_w_up': 7.961,
     'L0_ffn_w_down': 7.855,
     'L0_ffn_ws_gate': 8.0,
     'L0_ffn_ws_up': 8.0,
     'L0_ffn_ws_down': 8.0}
    for name, (base, spread) in spreads.items():
        noise = np.random.default_rng([zlib.crc32(name.encode()), seed]).standard_normal(out[name].shape)
        drawn = base * np.exp(spread * noise) if base else spread * noise
        out[name] = jnp.asarray(drawn.astype(out[name].dtype))
    for name, factor in factors.items():
        out[name] = (out[name] * factor).astype(out[name].dtype)
    return out
```

```python
from contextlib import ExitStack

import concourse.bass as bass
from concourse import mybir

F32 = mybir.dt.float32
BF16 = mybir.dt.bfloat16
I32 = mybir.dt.int32
U32 = mybir.dt.uint32
ALU = mybir.AluOpType
ACT = mybir.ActivationFunctionType

P = 128
B = 32
T = 100
H = 512
KT = H // P


TABLES = "natural_log_exp_and_others"

E_MAX = 2.0 ** 63


def at_least(eng, sem, value):
    if not isinstance(value, int) or value > 0:
        eng.wait_ge(sem, value)


CELLS = 16


def hold_vector(eng, cells):
    n = cells[1].pop(0)
    cells[1].append(n)
    eng.memset(cells[0][0:1, n:n + 1], 0.0)


def hold_pool(eng, cells, held, times):
    at_least(eng, held, times)
    eng.tensor_tensor(cells[0:1, 2:3], cells[0:1, 0:1], cells[0:1, 1:2], ALU.add).then_inc(held, 1)


class Memory:

    def __init__(self, nc, stack, tag):
        self.nc, self.stack, self.tag, self.sems = nc, stack, tag, []
        stack.callback(self.clear)

    def clear(self):
        if self.sems:
            self.nc.clear_and_free_semaphores(self.sems)
            self.nc.all_engine_barrier()

    def sb(self, name, shape, dt=F32):
        return self.stack.enter_context(self.nc.sbuf_tensor(f"{self.tag}_{name}", shape, dt))

    def ps(self, name, shape, dt=F32):
        return self.stack.enter_context(self.nc.psum_tensor(f"{self.tag}_{name}", shape, dt))

    def sem(self, name):
        self.sems.append(self.nc.alloc_semaphore(name=f"{self.tag}_{name}"))
        return self.sems[-1]


INTER = 1024
NSTATE = 128
HEADS = 64
PD = INTER // HEADS
CONV = INTER + 2 * NSTATE
CT = CONV // P
XT = INTER // P
HH = HEADS // 2
PAIRS = B // 2
HB = 4
NBLK = HEADS // HB
LAG = 3
W2 = 2 * T


def phase_a(nc, x, w_in, conv_w, conv_b, a_log, d_skip, dt_bias, norm_w, w_out, x1):
    with ExitStack() as stack:
        m = Memory(nc, stack, "a")
        sb, ps, sem = m.sb, m.ps, m.sem
        win = sb("win", [P, KT, 2 * INTER + 2 * NSTATE + HEADS])
        wdt = sb("wdt", [P, KT, 2, 3, HH])
        wout = sb("wout", [P, XT, H])
        ident = sb("ident", [P, P])
        eye4 = sb("eye4", [T, HB, T])
        sel = sb("sel", [96, HH, T], BF16)
        cw = sb("cw", [P, CT, 4])
        cb = sb("cb", [P, CT])
        nw = sb("nw", [P, XT])
        a_neg = sb("a_neg", [96, 2])
        dtb = sb("dtb", [96, 2])
        dsk = sb("dsk", [T, HEADS])
        eps = sb("eps", [P, 1])
        cell = (sb("cells", [1, CELLS]), list(range(CELLS)))
        xl = sb("xl", [T, 2, 2, H])
        stats = sb("stats", [T, 2, 6])
        mv = sb("mv", [T, 2, 2])
        lnv = sb("lnv", [T, 2])
        rstd = sb("rstd", [T, 2])
        hn = sb("hn", [T, 2, H])
        hT = sb("hT", [P, KT, W2])
        acc = sb("acc", [P, 2, 2, W2])
        sg = sb("sg", [P, 2, 2 * W2])
        xc = sb("xc", [P, 2, CT, W2])
        szt = sb("szt", [T, 2, 512])
        sz = sb("sz", [T, 2, 2, INTER])
        dtu = sb("dtu", [96, 2, W2])
        dtm = sb("dtm", [96, 6, 2 * W2])
        dt = sb("dt", [96, 2, 2, W2])
        da = sb("da", [96, 2, 2, T])
        res = sb("res", [96, 2, 2, T])
        mid = sb("mid", [96, 2, 2, T], BF16)
        das = sb("das", [96, 2, 2, 2, T], BF16)
        gd = sb("gd", [T, 2, T + HEADS])
        xt = sb("xt", [T, INTER])
        dx = sb("dx", [T, 2, INTER])
        dtx = sb("dtx", [T, 2, INTER])
        lmat = sb("lmat", [T, 4, HB * T])
        mmat = sb("mmat", [T, 4, HB, T])
        y1 = sb("y1", [T, INTER])
        ysq = sb("ysq", [T, INTER])
        ss = sb("ss", [T, 2, 3])
        yz = sb("yz", [T, INTER])
        gT = sb("gT", [P, XT, T])
        xr = sb("xr", [T, 2, H])
        x1o = sb("x1o", [T, 2, H])

        pj = [ps(f"pj{n}", [P, 512]) for n in range(2)]
        sp_ = [ps(f"sp{n}", [P, 512]) for n in range(2)]
        bc = [ps(f"bc{n}", [P, 512]) for n in range(2)]
        yp = ps("yp", [P, 2, 512])

        s_win, s_wout, s_small = sem("win_loaded"), sem("wout_loaded"), sem("small_loaded")
        s_const, s_prep, s_aneg = sem("const_ready"), sem("prep_ready"), sem("a_neg_ready")
        s_wout_ready, s_wdt = sem("wout_ready"), sem("wdt_ready")
        s_xl = [sem("xl_loaded0"), sem("xl_loaded1")]
        s_xr = [sem("xr_loaded0"), sem("xr_loaded1")]
        s_st = [sem("x1_stored0"), sem("x1_stored1")]
        s_stats, s_mv, s_lnv, s_rstd, s_h = sem("stats"), sem("mv"), sem("lnv"), sem("rstd"), sem("h")
        s_pj, s_hT = sem("proj_in_psum"), sem("hT")
        s_tap0, s_taps, s_exp, s_e1, s_cl, s_rec, s_xc = (sem(n) for n in ("tap0", "taps", "cexp", "cmin", "cln", "csigm", "xc"))
        s_ze, s_z1, s_zl, s_zr, s_sz = (sem(n) for n in ("zexp", "zmin", "zln", "zsigm", "sz"))
        s_dtu, s_dn, s_dv, s_dw, s_dl, s_dr = (sem(n) for n in ("dt_u", "dt_neg", "dt_exp", "dt_w", "dt_ln", "dt_rec"))
        s_dpre, s_dm, s_dt, s_da, s_da0, s_split = (sem(n) for n in ("dt_pre", "dt_mul", "dt", "da", "da0", "da_split"))
        s_sp, s_gd, s_xt, s_dx, s_dtx = (sem(n) for n in ("ssm_in_psum", "gd", "xt", "dx", "dtx"))
        s_bc, s_L, s_M, s_y = (sem(n) for n in ("decay_bc", "L", "M", "y_heads"))
        s_y1, s_ssq, s_sln, s_rs, s_yz, s_gT, s_x1 = (sem(n) for n in ("y1", "ssq", "sln", "rs", "yz", "gT", "x1"))

        block = stack.enter_context(nc.Block())
        UP = 12
        U_HT, U_DT, U_CV, U_Z = 0, 2, 3, 8
        NCV = CT // 2

        def pj_free(eng, g, n):
            if n < 2:
                g, n = g - 1, n + UP
                if isinstance(g, int) and g < 0:
                    return
            u = n - 2
            if u < U_DT:
                eng.wait_ge(s_hT, 2 * g + u + 1)
            elif u == U_DT:
                eng.wait_ge(s_dtu, 2 * g + 2)
            elif u < U_Z:
                eng.wait_ge(s_taps, 6 * (NCV * g + u - U_CV) + 6)
            else:
                eng.wait_ge(s_sz, 4 * g + u - U_Z + 1)

        US = 6

        def sp_free(eng, s, n):
            if n < 2:
                s, n = s - 1, n + US
                if isinstance(s, int) and s < 0:
                    return
            u = n - 2
            if u == 0:
                eng.wait_ge(s_gd, s + 1)
            elif u in (1, 2):
                eng.wait_ge(s_dtx, 2 * s + u)
            elif u in (3, 4):
                at_least(eng, s_gT, 2 * (s - 1) + u - 2)
            else:
                at_least(eng, s_x1, s)

        PLAN = {(0, 1): ["ln"], (0, 4): ["hT"], (0, 6): ["dt"], (0, 7): ["dt2"], (0, 8): ["cv0"], (0, 9): ["dt3"],
                (0, 10): ["cw0"], (0, 11): ["cx0", "cv1"], (0, 12): ["dt4"], (0, 13): ["cw1"], (0, 14): ["cx1", "cv2", "dt5"],
                (0, 15): ["cw2"],
                (1, 1): ["cx2", "cv3"], (1, 2): ["cw3"], (1, 3): ["cx3"], (1, 4): ["cv4"], (1, 5): ["cw4"], (1, 6): ["cx4"],
                (1, 7): ["z0"], (1, 8): ["zz0"], (1, 9): ["z1"], (1, 10): ["zz1"], (1, 11): ["z2"],
                (1, 12): ["zz2"], (1, 13): ["z3"], (1, 14): ["zz3"]}
        ALL = [i for k in sorted(PLAN) for i in PLAN[k]]

        PROMPT = ("ln", "hT")

        def over_pairs(eng, projection, sequence, tail, late=0):
            for item in ALL:
                projection(item, 0, 0, 0)

            def pair(g, i, p, last=False):
                for j in range(2):
                    def between(b, j=j):
                        if not last:
                            prompt = [n for n in PLAN.get((j, b), []) if n in PROMPT]
                            others = [n for n in PLAN.get(divmod(NBLK * j + b - late, NBLK), []) if n not in PROMPT]
                            for item in prompt + others:
                                projection(item, g + 1, i + p, 1 - p)
                    sequence(g, i, p, j, between)

            pair(0, 0, 0)
            pair(1, 0, 1)
            with eng.Fori(1, PAIRS // 2 - 1) as i:
                pair(2 * i, i, 0)
                pair(2 * i + 1, i, 1)
            n = PAIRS // 2 - 1
            pair(2 * n, n, 0)
            pair(2 * n + 1, n, 1, last=True)
            tail(2 * n + 2, n + 1, 0, 0)

        @block.sync
        def _(eng):
            eng.dma_start(win[:, :, 2 * INTER + 2 * NSTATE:], w_in[:, 2 * INTER + 2 * NSTATE:].rearrange("(k p) n -> p k n", p=P),
                          allow_slow_non_contiguous=True).then_inc(s_win, 16)
            eng.dma_start(win[:, :, INTER:2 * INTER + 2 * NSTATE],
                          w_in[:, INTER:2 * INTER + 2 * NSTATE].rearrange("(k p) n -> p k n", p=P)).then_inc(s_win, 16)
            eng.dma_start(win[:, :, 0:INTER], w_in[:, 0:INTER].rearrange("(k p) n -> p k n", p=P)).then_inc(s_win, 16)
            eng.dma_start(wout[:, :, :], w_out.rearrange("(k p) n -> p k n", p=P)).then_inc(s_wout, 16)

            def projection(item, g, i, p):
                if item == "ln":
                    at_least(eng, s_h, 2 * (g - 1))
                    eng.dma_start(xl[:, p, :, :], x[bass.ds(2 * g, 2)].rearrange("j t d -> t j d")).then_inc(s_xl[p], 16)

            def tail(g, i, p, j):
                q = 1 - j
                s = 2 * g + j - 1
                eng.wait_ge(s_x1, s + 1)
                eng.dma_start(x1[bass.ds(s, 1)].rearrange("a t d -> t (a d)"), x1o[:, q, :]).then_inc(s_st[q], 16)

            def sequence(g, i, p, j, between):
                s = 2 * g + j
                at_least(eng, s_x1, s - 1)
                eng.dma_start(xr[:, j, :], x[bass.ds(s, 1)].rearrange("a t d -> t (a d)")).then_inc(s_xr[j], 16)
                for b in range(NBLK):
                    between(b)
                    if b == 7 and not (isinstance(s, int) and s == 0):
                        tail(g, i, p, j)

            over_pairs(eng, projection, sequence, tail)
            eng.wait_ge(s_st[0], 16 * (B // 2))
            eng.wait_ge(s_st[1], 16 * (B // 2))

        @block.gpsimd
        def _(eng):
            for r in range(3):
                for src, dst in ((a_log, a_neg), (dt_bias, dtb)):
                    eng.dma_start(dst[HH * r:HH * r + HH, :], src.rearrange("(h r) -> r h", h=2),
                                  allow_slow_non_contiguous=True).then_inc(s_small, 16)
            eng.dma_start(cw[:, :, :], conv_w.rearrange("(c p) k -> p c k", p=P), allow_slow_non_contiguous=True).then_inc(s_small, 16)
            eng.dma_start(cb[:, :], conv_b.rearrange("(c p) -> p c", p=P), allow_slow_non_contiguous=True).then_inc(s_small, 16)
            eng.dma_start(nw[:, :], norm_w.rearrange("(c p) -> p c", p=P), allow_slow_non_contiguous=True).then_inc(s_small, 16)
            eng.dma_start(dsk[:, :], d_skip.rearrange("(a h) -> a h", a=1).to_broadcast([T, HEADS]),
                          allow_slow_non_contiguous=True).then_inc(s_small, 16)
            eng.memset(ident[:, :], 0.0).then_inc(s_const, 1)
            eng.memset(eye4[:, :, :], 0.0).then_inc(s_const, 1)
            eng.memset(sel[:, :, :], 0.0).then_inc(s_const, 1)
            eng.wait_ge(s_const, 3)
            eng.affine_select(out=ident[:, :], in_=ident[:, :], compare_op=ALU.not_equal, fill=1.0, base=0,
                              pattern=[[-1, P]], channel_multiplier=1).then_inc(s_const, 1)
            eng.affine_select(out=eye4[:, :, :], in_=eye4[:, :, :], compare_op=ALU.not_equal, fill=1.0, base=0,
                              pattern=[[0, HB], [-1, T]], channel_multiplier=1).then_inc(s_const, 1)
            for r in range(3):
                if r:
                    eng.wait_ge(s_const, 5 + r)
                eng.affine_select(out=sel[:, :, :], in_=sel[:, :, :], compare_op=ALU.not_equal, fill=1.0,
                                  base=-HH * r, pattern=[[-1, HH], [0, T]], channel_multiplier=1).then_inc(s_const, 1)
            eng.wait_ge(s_win, 48)
            for h in range(2):
                for r in range(3):
                    eng.tensor_copy(wdt[:, :, h, r, :], win[:, :, 2 * INTER + 2 * NSTATE + HH * h:][:, :, 0:HH]).then_inc(s_wdt, 1)

            def projection(item, g, i, p):
                if item == "dt3":
                    eng.wait_ge(s_dw, 3 * g + 3)
                    eng.tensor_tensor(dtm[:, 3, :], dtm[:, 3, :], dtm[:, 4, :], ALU.add).then_inc(s_dpre, 1)
                    eng.wait_ge(s_dl, g + 1)
                    eng.tensor_tensor(dtm[:, 4, :], dtm[:, 5, :], dtm[:, 4, :], ALU.add).then_inc(s_dpre, 1)
                    eng.wait_ge(s_dpre, 2 * g + 2)
                    eng.tensor_tensor(dtm[:, 4, :], dtm[:, 4, :], dtm[:, 1, :], ALU.mult).then_inc(s_dm, 1)
                    eng.wait_ge(s_dm, 2 * g + 1)
                    eng.wait_ge(s_dr, g + 1)
                    eng.tensor_tensor(dtm[:, 4, :], dtm[:, 4, :], dtm[:, 3, :], ALU.mult).then_inc(s_dm, 1)
                elif item.startswith("cx"):
                    c = int(item[2:])
                    k = NCV * g + c
                    q = (p + c) % 2
                    eng.wait_ge(s_rec, k + 1)
                    at_least(eng, s_sp, US * 2 * (g - 1))
                    eng.tensor_tensor(xc[:, p, 2 * c:2 * c + 2, :].rearrange("p a b -> p (a b)"),
                                      acc[:, q, :, :].rearrange("p a b -> p (a b)"), sg[:, q, :], ALU.mult).then_inc(s_xc, 1)

            def sequence(g, i, p, j, between):
                s = 2 * g + j
                for c in range(2):
                    eng.wait_ge(s_xt, 2 * s + c + 1)
                    at_least(eng, s_y1, s - 1)
                    eng.tensor_tensor(dx[:, j, 512 * c:512 * c + 512].rearrange("t (h q) -> t h q", q=PD),
                                      xt[:, 512 * c:512 * c + 512].rearrange("t (h q) -> t h q", q=PD),
                                      dsk[:, 32 * c:32 * c + 32].rearrange("t (h a) -> t h a", a=1).to_broadcast([T, 32, PD]), ALU.mult).then_inc(s_dx, 1)
                for b in range(NBLK):
                    n = NBLK * s + b
                    eng.wait_ge(s_L, n + 1)
                    at_least(eng, s_y, n - 3)
                    eng.tensor_tensor(mmat[:, b % 4, :, :], lmat[:, b % 4, :].rearrange("s (h t) -> s h t", h=HB),
                                      gd[:, j, 0:T].rearrange("s (a t) -> s a t", a=1).to_broadcast([T, HB, T]), ALU.mult).then_inc(s_M, 1)
                    if b == 1 and not (isinstance(s, int) and s == 0):
                        gate(g, i, p, j)
                    between(b)

            def gate(g, i, p, j):
                s = 2 * g + j - 1
                eng.wait_ge(s_y1, s + 1)
                at_least(eng, s_gT, 2 * s)
                eng.tensor_tensor(yz[:, :], y1[:, :], sz[:, p if j else 1 - p, 1 - j, :], ALU.mult).then_inc(s_yz, 1)

            eng.wait_ge(s_small, 160)
            over_pairs(eng, projection, sequence, gate, late=1)

        @block.scalar
        def _(eng):
            eng.preload_act_table_set(TABLES)
            eng.wait_ge(s_small, 160)
            eng.activation(a_neg[:, :], a_neg[:, :], ACT.Exp).then_inc(s_aneg, 1)
            eng.wait_ge(s_aneg, 1)
            eng.mul(a_neg[:, :], a_neg[:, :], -1.0).then_inc(s_aneg, 1)
            eng.wait_ge(s_aneg, 2)
            eng.wait_ge(s_prep, 3)

            def projection(item, g, i, p):
                if item == "ln":
                    eng.wait_ge(s_mv, 2 * g + 2)
                    eng.activation(lnv[:, :], mv[:, :, 1], ACT.Ln, bias=eps[0:T, :]).then_inc(s_lnv, 1)
                    eng.wait_ge(s_lnv, g + 1)
                    eng.activation(rstd[:, :], lnv[:, :], ACT.Exp, scale=-0.5).then_inc(s_rstd, 1)
                elif item == "hT":
                    at_least(eng, s_pj, UP * g)
                    for j in range(2):
                        eng.wait_ge(s_pj, UP * g + j + 1)
                        eng.copy(hT[:, :, T * j:T * j + T], pj[j][:, 0:KT * T].rearrange("p (k t) -> p k t", k=KT)).then_inc(s_hT, 1)
                elif item == "dt2":
                    eng.wait_ge(s_dn, g + 1)
                    eng.activation(dtm[:, 1, :], dtm[:, 0, :], ACT.Exp).then_inc(s_dv, 1)
                elif item == "dt3":
                    eng.wait_ge(s_dw, 3 * g + 1)
                    eng.activation(dtm[:, 5, :], dtm[:, 2, :], ACT.Ln).then_inc(s_dl, 1)
                elif item == "dt4":
                    eng.wait_ge(s_dt, g + 1)
                    at_least(eng, s_split, 5 * g)
                    for h in range(2):
                        eng.activation(da[:, h, :, :].rearrange("p j t -> p (j t)"), dt[:, p, h, :], ACT.Exp, scale=a_neg[:, h:h + 1]).then_inc(s_da, 1)
                elif item.startswith("cv"):
                    c = int(item[2:])
                    k = NCV * g + c
                    q = (p + c) % 2
                    eng.wait_ge(s_pj, UP * g + U_CV + c + 1)
                    at_least(eng, s_xc, k - 1)
                    for a in range(2):
                        t = 2 * c + a
                        eng.activation(acc[:, q, a, :], pj[(U_CV + c) % 2][:, W2 * a:W2 * a + W2], ACT.Identity,
                                       scale=cw[:, t, 3:4], bias=cb[:, t:t + 1]).then_inc(s_tap0, 1)
                elif item.startswith("cw"):
                    c = int(item[2:])
                    k = NCV * g + c
                    q = (p + c) % 2
                    eng.wait_ge(s_taps, 6 * k + 6)
                    eng.activation(sg[:, q, :], acc[:, q, :, :].rearrange("p a b -> p (a b)"), ACT.Exp, scale=-1.0).then_inc(s_exp, 1)
                elif item.startswith("cx"):
                    c = int(item[2:])
                    k = NCV * g + c
                    q = (p + c) % 2
                    eng.wait_ge(s_e1, k + 1)
                    eng.activation(sg[:, q, :], sg[:, q, :], ACT.Ln, bias=1.0).then_inc(s_cl, 1)
                    eng.wait_ge(s_cl, k + 1)
                    eng.activation(sg[:, q, :], sg[:, q, :], ACT.Exp, scale=-1.0).then_inc(s_rec, 1)
                elif item.startswith("zz"):
                    c = int(item[2:])
                    k = 4 * g + c
                    eng.wait_ge(s_z1, k + 1)
                    eng.activation(szt[:, c % 2, :], szt[:, c % 2, :], ACT.Ln, bias=1.0).then_inc(s_zl, 1)
                    eng.wait_ge(s_zl, k + 1)
                    eng.activation(szt[:, c % 2, :], szt[:, c % 2, :], ACT.Exp, scale=-1.0).then_inc(s_zr, 1)
                elif item[0] == "z":
                    c = int(item[1:])
                    k = 4 * g + c
                    eng.wait_ge(s_pj, UP * g + U_Z + c + 1)
                    at_least(eng, s_sz, k - 1)
                    eng.activation(szt[:, c % 2, :], pj[(U_Z + c) % 2][0:T, :], ACT.Exp, scale=-0.25).then_inc(s_ze, 1)

            def tail(g, i, p, j):
                s = 2 * g + j - 1
                for c in range(2):
                    eng.wait_ge(s_sp, US * (s + 1) + 3 + c + 1)
                    eng.copy(gT[:, 4 * c:4 * c + 4, :], sp_[(3 + c) % 2][:, 0:4 * T].rearrange("p (k t) -> p k t", k=4)).then_inc(s_gT, 1)

            def sequence(g, i, p, j, between):
                s = 2 * g + j
                eng.wait_ge(s_sp, US * s + 1)
                at_least(eng, s_M, NBLK * (s - 1))
                eng.copy(gd[:, j, :], sp_[0][0:T, 0:T + HEADS]).then_inc(s_gd, 1)
                for c in range(2):
                    eng.wait_ge(s_sp, US * s + c + 2)
                    at_least(eng, s_dx, 2 * s)
                    eng.copy(xt[:, 512 * c:512 * c + 512], sp_[(1 + c) % 2][0:T, :]).then_inc(s_xt, 1)
                for b in range(NBLK):
                    if b == 1 and not (isinstance(s, int) and s == 0):
                        norm(g, i, p, j)
                    if b == 4 and not (isinstance(s, int) and s == 0):
                        tail(g, i, p, j)
                    between(b)

            def norm(g, i, p, j):
                s = 2 * g + j - 1
                q = 1 - j
                eng.wait_ge(s_y1, s + 1)
                eng.activation(ysq[:, :], y1[:, :], ACT.Square, accum_out=ss[:, q, 0:1]).then_inc(s_ssq, 1)
                eng.wait_ge(s_ssq, s + 1)
                eng.activation(ss[:, q, 1:2], ss[:, q, 0:1], ACT.Ln, scale=1.0 / INTER, bias=eps[0:T, :]).then_inc(s_sln, 1)
                eng.wait_ge(s_sln, s + 1)
                at_least(eng, s_x1, s - 1)
                eng.activation(ss[:, q, 2:3], ss[:, q, 1:2], ACT.Exp, scale=-0.5).then_inc(s_rs, 1)

            def last(g, i, p, j):
                norm(g, i, p, j)
                tail(g, i, p, j)

            over_pairs(eng, projection, sequence, last)

        @block.vector
        def _(eng):
            eng.memset(eps[:, :], 1e-5).then_inc(s_prep, 1)
            eng.wait_ge(s_small, 160)
            eng.tensor_scalar(cw[:, :, :], cw[:, :, :], 0.5, None, ALU.mult).then_inc(s_prep, 1)
            eng.memset(ss[:, :, :], 0.0).then_inc(s_prep, 1)
            eng.wait_ge(s_prep, 3)
            eng.wait_ge(s_wout, 16)
            for c in range(XT):
                eng.tensor_scalar(wout[:, c, :], wout[:, c, :], nw[:, c:c + 1], None, ALU.mult).then_inc(s_wout_ready, 1)

            def projection(item, g, i, p):
                if item == "ln":
                    eng.wait_ge(s_xl[p], 16 * (i + 1))
                    for j in range(2):
                        eng.bn_stats(stats[:, j, :], xl[:, p, j, :]).then_inc(s_stats, 1)
                    for j in range(2):
                        eng.wait_ge(s_stats, 2 * g + j + 1)
                        hold_vector(eng, cell)
                        eng.bn_aggr(mv[:, j, :], stats[:, j, :]).then_inc(s_mv, 1)
                elif item == "hT":
                    eng.wait_ge(s_rstd, g + 1)
                    at_least(eng, s_hT, 2 * g)
                    for j in range(2):
                        eng.tensor_scalar(hn[:, j, :], xl[:, p, j, :], mv[:, j, 0:1], rstd[:, j:j + 1], ALU.subtract, ALU.mult).then_inc(s_h, 1)
                elif item == "dt":
                    eng.wait_ge(s_pj, UP * g + U_DT + 1)
                    for h in range(2):
                        eng.tensor_scalar(dtu[:, h, :], pj[U_DT % 2][0:96, W2 * h:W2 * h + W2], dtb[:, h:h + 1], None, ALU.add).then_inc(s_dtu, 1)
                    eng.wait_ge(s_dtu, 2 * g + 2)
                    u = dtu[:, :, :].rearrange("p h t -> p (h t)")
                    at_least(eng, s_dm, 2 * g)
                    eng.scalar_tensor_tensor(out=dtm[:, 0, :], in0=u, scalar=-1.0, in1=u, op0=ALU.mult, op1=ALU.min).then_inc(s_dn, 1)
                elif item == "dt3":
                    eng.wait_ge(s_dv, g + 1)
                    eng.tensor_scalar(dtm[:, 2, :], dtm[:, 1, :], 1.0, None, ALU.add).then_inc(s_dw, 1)
                    eng.wait_ge(s_dw, 3 * g + 1)
                    eng.tensor_scalar(dtm[:, 3, :], dtm[:, 2, :], -1.0, None, ALU.add).then_inc(s_dw, 1)
                    eng.wait_ge(s_dw, 3 * g + 2)
                    eng.tensor_scalar(dtm[:, 4, :], dtm[:, 3, :], 0.0, None, ALU.is_equal).then_inc(s_dw, 1)
                    eng.wait_ge(s_dpre, 2 * g + 1)
                    eng.reciprocal(dtm[:, 3, :], dtm[:, 3, :]).then_inc(s_dr, 1)
                elif item == "dt4":
                    eng.wait_ge(s_dm, 2 * g + 2)
                    at_least(eng, s_sp, US * 2 * (g - 1))
                    eng.scalar_tensor_tensor(out=dt[:, p, :, :].rearrange("p h t -> p (h t)"), in0=dtu[:, :, :].rearrange("p h t -> p (h t)"),
                                             scalar=0.0, in1=dtm[:, 4, :], op0=ALU.max, op1=ALU.add).then_inc(s_dt, 1)
                elif item == "dt5":
                    eng.wait_ge(s_da, 2 * g + 2)
                    eng.memset(da[:, :, :, 0:1], 0.0).then_inc(s_da0, 1)
                    eng.wait_ge(s_da0, g + 1)
                    at_least(eng, s_bc, NBLK * 2 * (g - 1))
                    eng.tensor_copy(das[:, p, :, :, :], da[:, :, :, :]).then_inc(s_split, 1)
                    eng.wait_ge(s_split, 5 * g + 1)
                    eng.tensor_tensor(res[:, :, :, :], da[:, :, :, :], das[:, p, :, :, :], ALU.subtract).then_inc(s_split, 1)
                    eng.wait_ge(s_split, 5 * g + 2)
                    eng.tensor_copy(mid[:, :, :, :], res[:, :, :, :]).then_inc(s_split, 1)
                    eng.wait_ge(s_split, 5 * g + 3)
                    eng.tensor_copy(das[32:64, p, :, :, :], mid[32:64, :, :, :]).then_inc(s_split, 1)
                    eng.tensor_tensor(das[64:96, p, :, :, :], res[64:96, :, :, :], mid[64:96, :, :, :], ALU.subtract).then_inc(s_split, 1)
                elif item.startswith("cv"):
                    c = int(item[2:])
                    k = NCV * g + c
                    q = (p + c) % 2
                    eng.wait_ge(s_tap0, 2 * k + 2)
                    n = 0
                    for d in (1, 2, 3):
                        for a in range(2):
                            if n >= 2:
                                eng.wait_ge(s_taps, 6 * k + n - 1)
                            o = acc[:, q, a, :].rearrange("p (j t) -> p j t", j=2)[:, :, d:T]
                            src = pj[(U_CV + c) % 2][:, W2 * a:W2 * a + W2].rearrange("p (j t) -> p j t", j=2)[:, :, 0:T - d]
                            eng.scalar_tensor_tensor(out=o, in0=src, scalar=cw[:, 2 * c + a, 3 - d:4 - d], in1=o,
                                                     op0=ALU.mult, op1=ALU.add).then_inc(s_taps, 1)
                            n += 1
                elif item.startswith("cw"):
                    c = int(item[2:])
                    k = NCV * g + c
                    q = (p + c) % 2
                    eng.wait_ge(s_exp, k + 1)
                    eng.tensor_scalar(sg[:, q, :], sg[:, q, :], E_MAX, None, ALU.min).then_inc(s_e1, 1)
                elif item[0] == "z" and item[1] != "z":
                    c = int(item[1:])
                    k = 4 * g + c
                    eng.wait_ge(s_ze, k + 1)
                    eng.tensor_scalar(szt[:, c % 2, :], szt[:, c % 2, :], E_MAX, None, ALU.min).then_inc(s_z1, 1)
                elif item.startswith("zz"):
                    c = int(item[2:])
                    k = 4 * g + c
                    eng.wait_ge(s_zr, k + 1)
                    at_least(eng, s_yz, 2 * (g - 1))
                    eng.scalar_tensor_tensor(out=sz[:, p, c // 2, 512 * (c % 2):512 * (c % 2) + 512], in0=pj[(U_Z + c) % 2][0:T, :],
                                             scalar=0.25, in1=szt[:, c % 2, :], op0=ALU.mult, op1=ALU.mult).then_inc(s_sz, 1)

            def tail(g, i, p, j):
                s = 2 * g + j - 1
                q = 1 - j
                eng.wait_ge(s_sp, US * (s + 1) + 6)
                eng.wait_ge(s_rs, s + 1)
                done = (s - q) // 2 if isinstance(s, int) else g - 1 if j == 0 else g
                eng.wait_ge(s_xr[q], 16 * (done + 1))
                at_least(eng, s_st[q], 16 * done)
                eng.scalar_tensor_tensor(out=x1o[:, q, :], in0=sp_[5 % 2][0:T, :], scalar=ss[:, q, 2:3], in1=xr[:, q, :],
                                         op0=ALU.mult, op1=ALU.add).then_inc(s_x1, 1)

            def sequence(g, i, p, j, between):
                s = 2 * g + j
                eng.wait_ge(s_gd, s + 1)
                for c in range(2):
                    eng.wait_ge(s_xt, 2 * s + c + 1)
                    at_least(eng, s_y, NBLK * (s - 1))
                    eng.tensor_tensor(dtx[:, j, 512 * c:512 * c + 512].rearrange("t (h q) -> t h q", q=PD),
                                      sp_[(1 + c) % 2][0:T, :].rearrange("t (h q) -> t h q", q=PD),
                                      gd[:, j, T + 32 * c:T + 32 * c + 32].rearrange("t (h a) -> t h a", a=1).to_broadcast([T, 32, PD]), ALU.mult).then_inc(s_dtx, 1)
                for b in range(NBLK):
                    n = NBLK * s + b
                    eng.wait_ge(s_bc, n + 1)
                    at_least(eng, s_M, n - 3)
                    eng.tensor_tensor_scan(lmat[:, b % 4, :], bc[b % 2][0:T, 0:HB * T], eye4[:, :, :].rearrange("s h t -> s (h t)"),
                                           0.0, ALU.mult, ALU.add).then_inc(s_L, 1)
                    if b == 1 and not (isinstance(s, int) and s == 0):
                        add_skip(g, i, p, j)
                    between(b)
                    if b == 10 and not (isinstance(s, int) and s == 0):
                        tail(g, i, p, j)

            def add_skip(g, i, p, j):
                s = 2 * g + j - 1
                eng.wait_ge(s_y, NBLK * s + NBLK)
                eng.wait_ge(s_dx, 2 * s + 2)
                at_least(eng, s_yz, s)
                at_least(eng, s_ssq, s)
                eng.tensor_tensor(y1[:, :], yp[0:T, :, :].rearrange("t a b -> t (a b)"), dx[:, 1 - j, :], ALU.add).then_inc(s_y1, 1)

            def last(g, i, p, j):
                add_skip(g, i, p, j)
                tail(g, i, p, j)

            over_pairs(eng, projection, sequence, last, late=1)

        @block.tensor
        def _(eng):
            eng.wait_ge(s_const, 8)
            eng.wait_ge(s_win, 48)
            eng.wait_ge(s_wdt, 6)
            eng.wait_ge(s_wout_ready, XT)
            def projection(item, g, i, p):
                if item == "hT":
                    for j in range(2):
                        eng.wait_ge(s_h, 2 * g + j + 1)
                        pj_free(eng, g, j)
                        for k in range(KT):
                            mm = eng.transpose(pj[j][:, T * k:T * k + T], hn[:, j, P * k:P * k + P], ident[0:T, 0:T])
                        mm.then_inc(s_pj, 1)
                elif item == "dt":
                    eng.wait_ge(s_hT, 2 * g + 2)
                    pj_free(eng, g, U_DT)
                    for h in range(2):
                        for k in range(KT):
                            mm = eng.matmul(pj[U_DT % 2][0:96, W2 * h:W2 * h + W2], wdt[:, k, h, :, :].rearrange("p r h -> p (r h)"), hT[:, k, :],
                                            start=(k == 0), stop=(k == KT - 1))
                    mm.then_inc(s_pj, 1)
                elif item.startswith("cv"):
                    c = int(item[2:])
                    pj_free(eng, g, U_CV + c)
                    for a in range(2):
                        n = INTER + P * (2 * c + a)
                        for k in range(KT):
                            mm = eng.matmul(pj[(U_CV + c) % 2][:, W2 * a:W2 * a + W2], win[:, k, n:n + P], hT[:, k, :],
                                            start=(k == 0), stop=(k == KT - 1))
                    mm.then_inc(s_pj, 1)
                elif item[0] == "z" and item[1] != "z":
                    c = int(item[1:])
                    j = c // 2
                    pj_free(eng, g, U_Z + c)
                    for k in range(KT):
                        mm = eng.matmul(pj[(U_Z + c) % 2][0:T, :], hT[:, k, T * j:T * j + T], win[:, k, 512 * (c % 2):512 * (c % 2) + 512],
                                        start=(k == 0), stop=(k == KT - 1))
                    mm.then_inc(s_pj, 1)

            def tail(g, i, p, j, wait=True):
                s = 2 * g + j - 1
                eng.wait_ge(s_yz, s + 1)
                for c in range(2):
                    if wait:
                        sp_free(eng, s + 1, 3 + c)
                    for k in range(4):
                        n = P * (4 * c + k)
                        mm = eng.transpose(sp_[(3 + c) % 2][:, T * k:T * k + T], yz[:, n:n + P], ident[0:T, 0:T])
                    mm.then_inc(s_sp, 1)

            def tail2(g, i, p, j):
                s = 2 * g + j - 1
                eng.wait_ge(s_gT, 2 * s + 2)
                for k in range(XT):
                    mm = eng.matmul(sp_[5 % 2][0:T, :], gT[:, k, :], wout[:, k, :], start=(k == 0), stop=(k == XT - 1))
                mm.then_inc(s_sp, 1)

            def sequence(g, i, p, j, between):
                s = 2 * g + j
                first = isinstance(s, int) and s == 0
                cols = slice(T * j, T * j + T)
                eng.wait_ge(s_xc, NCV * g + NCV)
                eng.wait_ge(s_dt, g + 1)
                sp_free(eng, s, 0)
                eng.matmul(sp_[0][0:T, 0:T], xc[:, p, XT, cols], xc[:, p, XT + 1, cols], start=True, stop=True)
                for h in range(2):
                    mm = eng.transpose(sp_[0][0:T, T + HH * h:T + HH * h + HH], dt[0:HH, p, h, cols], ident[0:HH, 0:HH])
                mm.then_inc(s_sp, 1)
                for c in range(2):
                    sp_free(eng, s, 1 + c)
                    for k in range(4):
                        mm = eng.transpose(sp_[(1 + c) % 2][0:T, P * k:P * k + P], xc[:, p, 4 * c + k, cols], ident[:, :])
                    mm.then_inc(s_sp, 1)
                eng.wait_ge(s_split, 5 * g + 5)

                def heads(b):
                    eng.wait_ge(s_M, NBLK * s + b + 1)
                    if b == 0:
                        eng.wait_ge(s_dtx, 2 * s + 2)
                        at_least(eng, s_y1, s)
                    for h in range(HB):
                        n = PD * (HB * b + h)
                        mm = eng.matmul(yp[0:T, n // 512, n % 512:n % 512 + PD], mmat[:, b % 4, h, :], dtx[:, j, n:n + PD], start=True, stop=True)
                    mm.then_inc(s_y, 1)

                for b in range(NBLK):
                    at_least(eng, s_L, NBLK * s + b - 1)
                    for h in range(HB):
                        hd = HB * b + h
                        mm = eng.matmul(bc[b % 2][0:T, T * h:T * h + T], sel[:, hd % HH, :], das[:, p, hd // HH, j, :], start=True, stop=True)
                    mm.then_inc(s_bc, 1)
                    if b >= LAG:
                        heads(b - LAG)
                    if b == 4:
                        if first:
                            eng.nop().then_inc(s_sp, 3)
                        else:
                            tail(g, i, p, j)
                    between(b)
                    if b == 8 and not first:
                        tail2(g, i, p, j)
                for b in range(NBLK - LAG, NBLK):
                    heads(b)

            def last(g, i, p, j):
                eng.wait_ge(s_gT, 2 * B - 2)
                eng.wait_ge(s_x1, B - 1)
                eng.nop().then_inc(s_sp, 3)
                tail(g, i, p, j, False)
                tail2(g, i, p, j)

            over_pairs(eng, projection, sequence, last)


NH, NKV, HD = 16, 4, 128
GRP = NH // NKV
SE = 361
ET = (SE + P - 1) // P
EREM = SE - (ET - 1) * P
SCALE = float(HD) ** -0.5


def phase_b(nc, x1, ctx, mask, wq, bq, wk, bk, wv, bv, wo, qn_w, kn_w, x2):
    with ExitStack() as stack:
        m = Memory(nc, stack, "b")
        sb, ps, sem = m.sb, m.ps, m.sem
        wq_sb = sb("wq", [P, KT, NH * HD])
        wk_sb = sb("wk", [P, KT, NKV * HD])
        wv_sb = sb("wv", [P, KT, NKV * HD])
        wo_sb = sb("wo", [P, NH, H])
        bq_sb = sb("bq", [P, NH])
        bk_sb = sb("bk", [P, NKV])
        bv_sb = sb("bv", [P, NKV * HD])
        mask_sb = sb("mask", [T, SE])
        qw = sb("qw", [P, 1])
        kw = sb("kw", [P, 1])
        w_qk = sb("w_qk", [P, 1])
        ident = sb("ident", [P, P])
        ones = sb("ones", [P, P])
        eps5 = sb("eps5", [P, 1])
        eps6 = sb("eps6", [P, 1])
        cell = (sb("cells", [1, CELLS]), list(range(CELLS)))
        xl = sb("xl", [T, 2, H])
        cx = sb("cx", [P, 2, ET, H])
        stats = sb("stats", [T, 6])
        mv = sb("mv", [T, 2])
        lnv = sb("lnv", [T, 1])
        rstd = sb("rstd", [T, 1])
        hn = sb("hn", [T, H])
        hT = sb("hT", [P, KT, T])
        cT = sb("cT", [P, KT, SE])
        kb = sb("kb", [P, 2, SE])
        ksq = sb("ksq", [P, 2, SE])
        rk = sb("rk", [P, 2, SE])
        qb = sb("qb", [P, 2, GRP * T])
        qsq = sb("qsq", [P, 2, GRP * T])
        rq = sb("rq", [P, 2, GRP * T])
        kT = sb("kT", [P, 2, NKV, SE])
        v = sb("v", [P, 2, ET, NKV * HD])
        qT = sb("qT", [P, 2, NH, T])
        nsc = sb("nsc", [T, 2, SE])
        nmx = sb("nmx", [T, 4])
        prob = sb("prob", [T, 4, ET * P])
        tot = sb("tot", [T, 4])
        rin = sb("rin", [T, 4])
        pT = sb("pT", [P, 2, ET, GRP, T])
        aT = sb("aT", [P, NH, T])
        xr = sb("xr", [T, 2, H])
        x2o = sb("x2o", [T, 2, H])

        pj = [ps(f"pj{n}", [P, 512]) for n in range(2)]
        sc = [ps(f"sc{n}", [P, 512]) for n in range(2)]
        tp = [ps(f"tp{n}", [P, 512]) for n in range(2)]
        po = ps("po", [P, 512])
        pout = ps("pout", [P, 512])

        s_w, s_small, s_const, s_prep = sem("weights_loaded"), sem("small_loaded"), sem("const_ready"), sem("prep_ready")
        s_xl = [sem(f"xl_loaded{n}") for n in range(2)]
        s_cx = [sem(f"ctx_loaded{n}") for n in range(2)]
        s_xr = [sem(f"xr_loaded{n}") for n in range(2)]
        s_st = [sem(f"x2_stored{n}") for n in range(2)]
        s_stats, s_mv, s_lnv, s_rstd, s_h = (sem(n) for n in ("stats", "mv", "lnv", "rstd", "h"))
        s_pj, s_hT, s_cT = (sem(n) for n in ("proj_in_psum", "hT", "ctxT"))
        s_kb, s_ksq, s_kln, s_rk, s_kT = (sem(n) for n in ("k_biased", "k_squared", "k_ln", "k_rms", "kT"))
        s_v = sem("v")
        s_qb, s_qsq, s_qln, s_rq, s_qT = (sem(n) for n in ("q_biased", "q_squared", "q_ln", "q_rms", "qT"))
        s_sc, s_tt, s_ex, s_ri, s_pn = (sem(n) for n in ("scores", "masked_max", "exp", "rsum", "probs"))
        s_tp, s_pT, s_pv, s_aT, s_o, s_x2 = (sem(n) for n in ("probs_transposed", "pT", "pv", "aT", "out_proj", "x2"))

        block = stack.enter_context(nc.Block())
        PLAN = [["ln", "c0"], ["c1"], ["c2", "c3"], ["hT", "k0"], ["k1", "ks0"], ["ks1"], ["k2"], ["k3", "ks2"], ["v0", "ks3"], ["v1"],
                ["v2"], ["q0"], ["q1", "qs0"], ["q2", "qs1"], ["q3", "qs2"], ["qs3"]]
        OUT_AT = (0, 1, 2, 5)
        ALL = [i for b in PLAN for i in b]
        USES = [i for i in ALL if i != "ln"]
        UP = len(USES)
        assert UP % 2 == 0

        def use(item, s):
            return UP * s + USES.index(item) + 1

        def bank(item):
            return pj[USES.index(item) % 2]

        def pj_free(eng, item, s):
            n = USES.index(item) - 2
            if n < 0:
                s, n = s - 1, n + UP
                if isinstance(s, int) and s < 0:
                    return
            last = USES[n]
            if last == "hT":
                eng.wait_ge(s_hT, s + 1)
            elif last[0] == "c":
                eng.wait_ge(s_cT, KT * s + int(last[1:]) + 1)
            elif last[0] == "v":
                eng.wait_ge(s_v, ET * s + int(last[1:]) + 1)
            else:
                done = {"k": s_ksq, "ks": s_kln, "q": s_qb, "qs": s_qln}[last.rstrip("0123")]
                eng.wait_ge(done, NKV * s + int(last[-1]) + 1)

        def lagged(s, p, b, lag):
            if b >= lag:
                return s, p, b - lag
            if isinstance(s, int) and s == 0:
                return None
            return s - 1, 1 - p, b - lag + NH

        def over_sequences(eng, projection, head):
            for item in ALL:
                projection(item, 0, 0, 0)

            def one(s, i, p, last=False):
                for b in range(NH):
                    head(s, p, b, i)
                    if not last:
                        for item in PLAN[b]:
                            projection(item, s + 1, i + p, 1 - p)

            one(0, 0, 0)
            one(1, 0, 1)
            with eng.Fori(1, B // 2 - 1) as i:
                one(2 * i, i, 0)
                one(2 * i + 1, i, 1)
            n = B // 2 - 1
            one(B - 2, n, 0)
            one(B - 1, n, 1, last=True)
            for b in range(8):
                head(B, 0, b, n + 1)

        def live(s):
            return not (isinstance(s, int) and s == B)

        @block.sync
        def _(eng):
            eng.dma_start(wk_sb[:, :, :], wk.rearrange("(k p) n -> p k n", p=P)).then_inc(s_w, 16)
            eng.dma_start(wv_sb[:, :, :], wv.rearrange("(k p) n -> p k n", p=P)).then_inc(s_w, 16)
            eng.dma_start(wq_sb[:, :, :], wq.rearrange("(k p) n -> p k n", p=P)).then_inc(s_w, 16)
            eng.dma_start(wo_sb[:, :, :], wo.rearrange("(k p) n -> p k n", p=P)).then_inc(s_w, 16)

            def projection(item, s, i, p):
                if item == "ln":
                    at_least(eng, s_h, s - 1)
                    eng.dma_start(xl[:, p, :], x1[bass.ds(s, 1)].rearrange("a t d -> t (a d)")).then_inc(s_xl[p], 16)
                    at_least(eng, s_pj, use("c3", s - 2))
                    eng.dma_start(cx[:, p, 0:ET - 1, :], ctx[bass.ds(s, 1), 0:P * (ET - 1), :].rearrange("a (e p) d -> p (a e) d", p=P)).then_inc(s_cx[p], 16)
                    eng.dma_start(cx[0:EREM, p, ET - 1, :], ctx[bass.ds(s, 1), P * (ET - 1):SE, :].rearrange("a e d -> e (a d)")).then_inc(s_cx[p], 16)

            def head(s, p, b, i):
                if b == 0 and live(s):
                    at_least(eng, s_x2, s - 1)
                    eng.dma_start(xr[:, p, :], x1[bass.ds(s, 1)].rearrange("a t d -> t (a d)")).then_inc(s_xr[p], 16)
                if b == 6 and not (isinstance(s, int) and s == 0):
                    eng.wait_ge(s_x2, s)
                    eng.dma_start(x2[bass.ds(s - 1, 1)].rearrange("a t d -> t (a d)"), x2o[:, 1 - p, :]).then_inc(s_st[1 - p], 16)

            over_sequences(eng, projection, head)
            eng.wait_ge(s_st[0], 16 * (B // 2))
            eng.wait_ge(s_st[1], 16 * (B // 2))

        @block.gpsimd
        def _(eng):
            for dst, src in ((bq_sb, bq), (bk_sb, bk), (qw, qn_w), (kw, kn_w)):
                eng.dma_start(dst[:, :], src.rearrange("(h p) -> p h", p=P), allow_slow_non_contiguous=True).then_inc(s_small, 16)
            eng.dma_start(bv_sb[:, :], bv.rearrange("(a n) -> a n", a=1).to_broadcast([P, NKV * HD])).then_inc(s_small, 16)
            eng.dma_start(mask_sb[:, :], mask.rearrange("a t e -> (a t) e")).then_inc(s_small, 16)
            eng.memset(ident[:, :], 0.0).then_inc(s_const, 1)
            eng.memset(ones[:, :], 1.0).then_inc(s_const, 1)
            eng.memset(prob[:, :, :], 0.0).then_inc(s_const, 1)
            eng.memset(eps5[:, :], 1e-5).then_inc(s_const, 1)
            eng.memset(eps6[:, :], 1e-6).then_inc(s_const, 1)
            eng.wait_ge(s_const, 5)
            eng.affine_select(out=ident[:, :], in_=ident[:, :], compare_op=ALU.not_equal, fill=1.0, base=0,
                              pattern=[[-1, P]], channel_multiplier=1).then_inc(s_const, 1)

            def projection(item, s, i, p):
                if item.startswith("ks"):
                    n = int(item[2:])
                    k = NKV * s + n
                    eng.wait_ge(s_rk, k + 1)
                    at_least(eng, s_sc, NH * (s - 1))
                    eng.tensor_tensor(kT[:, p, n, :], kb[:, n % 2, :], rk[:, n % 2, :], ALU.mult).then_inc(s_kT, 1)

            over_sequences(eng, projection, lambda *a: None)

        @block.scalar
        def _(eng):
            eng.preload_act_table_set(TABLES)
            eng.wait_ge(s_const, 6)
            eng.wait_ge(s_small, 96)

            def projection(item, s, i, p):
                if item == "ln":
                    eng.wait_ge(s_mv, s + 1)
                    eng.activation(lnv[:, :], mv[:, 1:2], ACT.Ln, bias=eps5[0:T, :]).then_inc(s_lnv, 1)
                    eng.wait_ge(s_lnv, s + 1)
                    eng.activation(rstd[:, :], lnv[:, :], ACT.Exp, scale=-0.5).then_inc(s_rstd, 1)
                elif item == "hT":
                    eng.wait_ge(s_pj, use(item, s))
                    eng.copy(hT[:, :, :], bank(item)[:, 0:KT * T].rearrange("p (k t) -> p k t", k=KT)).then_inc(s_hT, 1)
                elif item.startswith("c"):
                    eng.wait_ge(s_pj, use(item, s))
                    eng.copy(cT[:, int(item[1:]), :], bank(item)[:, 0:SE]).then_inc(s_cT, 1)
                elif item.startswith("ks") or item.startswith("qs"):
                    n = int(item[2:])
                    k = NKV * s + n
                    r, ln, done, cols = (rk, s_kln, s_rk, SE) if item[0] == "k" else (rq, s_qln, s_rq, GRP * T)
                    eng.wait_ge(s_pj, use(item, s))
                    at_least(eng, s_kT if item[0] == "k" else s_qT, k - 1)
                    eng.activation(r[:, n % 2, :], bank(item)[:, 0:cols], ACT.Ln, scale=1.0 / HD, bias=eps6[:, :]).then_inc(ln, 1)
                    eng.wait_ge(ln, k + 1)
                    eng.activation(r[:, n % 2, :], r[:, n % 2, :], ACT.Exp, scale=-0.5).then_inc(done, 1)
                elif item[0] == "k":
                    n = int(item[1:])
                    k = NKV * s + n
                    eng.wait_ge(s_pj, use(item, s))
                    at_least(eng, s_kT, k - 1)
                    eng.activation(kb[:, n % 2, :], bank(item)[:, 0:SE], ACT.Identity, bias=bk_sb[:, n:n + 1]).then_inc(s_kb, 1)
                    eng.activation(ksq[:, n % 2, :], bank(item)[:, 0:SE], ACT.Square, bias=bk_sb[:, n:n + 1]).then_inc(s_ksq, 1)
                elif item[0] == "q":
                    n = int(item[1:])
                    k = NKV * s + n
                    eng.wait_ge(s_qb, k + 1)
                    eng.activation(qsq[:, n % 2, :], qb[:, n % 2, :], ACT.Square).then_inc(s_qsq, 1)

            def head(s, p, b, i):
                if live(s):
                    n = NH * s + b
                    eng.wait_ge(s_tt, n + 1)
                    at_least(eng, s_tp, n - 3)
                    eng.activation(prob[:, b % 4, 0:SE], nsc[:, b % 2, :], ACT.Exp, scale=-1.0, bias=nmx[:, b % 4:b % 4 + 1],
                                   accum_out=tot[:, b % 4:b % 4 + 1]).then_inc(s_ex, 1)
                at = lagged(s, p, b, 3)
                if at and b < 3 or at and live(s):
                    s_, p_, h = at
                    n = NH * s_ + h
                    eng.wait_ge(s_tp, n + 1)
                    if h % 4 == 0:
                        at_least(eng, s_pv, NKV * s_ + h // 4 - 1)
                    eng.copy(pT[:, (h // 4) % 2, :, h % 4, :], tp[h % 2][:, 0:ET * T].rearrange("p (e t) -> p e t", e=ET)).then_inc(s_pT, 1)
                if b % 4 == 0 and (live(s) or b < 8):
                    at = lagged(s, p, b, 8)
                    if at:
                        s_, p_, h = at
                        n = h // 4
                        eng.wait_ge(s_pv, NKV * s_ + n + 1)
                        if n == 0:
                            at_least(eng, s_o, s_)
                        eng.copy(aT[:, 4 * n:4 * n + 4, :], po[:, 0:GRP * T].rearrange("p (h t) -> p h t", h=GRP)).then_inc(s_aT, 1)

            over_sequences(eng, projection, head)

        @block.vector
        def _(eng):
            eng.wait_ge(s_small, 96)
            eng.scalar_tensor_tensor(out=w_qk[:, :], in0=qw[:, :], scalar=SCALE, in1=kw[:, :], op0=ALU.mult, op1=ALU.mult).then_inc(s_prep, 1)
            eng.wait_ge(s_prep, 1)

            def projection(item, s, i, p):
                if item == "ln":
                    eng.wait_ge(s_xl[p], 16 * (i + 1))
                    eng.bn_stats(stats[:, :], xl[:, p, :]).then_inc(s_stats, 1)
                    eng.wait_ge(s_stats, s + 1)
                    hold_vector(eng, cell)
                    eng.bn_aggr(mv[:, :], stats[:, :]).then_inc(s_mv, 1)
                elif item == "hT":
                    eng.wait_ge(s_rstd, s + 1)
                    at_least(eng, s_hT, s)
                    eng.tensor_scalar(hn[:, :], xl[:, p, :], mv[:, 0:1], rstd[:, 0:1], ALU.subtract, ALU.mult).then_inc(s_h, 1)
                elif item[0] == "v":
                    e = int(item[1:])
                    rows = P if e < ET - 1 else EREM
                    eng.wait_ge(s_pj, use(item, s))
                    at_least(eng, s_pv, NKV * (s - 1))
                    eng.tensor_tensor(v[0:rows, p, e, :], bank(item)[0:rows, :], bv_sb[0:rows, :], ALU.add).then_inc(s_v, 1)
                elif item.startswith("qs"):
                    n = int(item[2:])
                    k = NKV * s + n
                    eng.wait_ge(s_rq, k + 1)
                    at_least(eng, s_sc, NH * (s - 1))
                    eng.scalar_tensor_tensor(out=qT[:, p, GRP * n:GRP * n + GRP, :].rearrange("p h t -> p (h t)"), in0=qb[:, n % 2, :],
                                             scalar=w_qk[:, 0:1], in1=rq[:, n % 2, :], op0=ALU.mult, op1=ALU.mult).then_inc(s_qT, 1)
                elif item[0] == "q":
                    n = int(item[1:])
                    eng.wait_ge(s_pj, use(item, s))
                    at_least(eng, s_qT, NKV * s + n - 1)
                    eng.tensor_tensor(qb[:, n % 2, :].rearrange("p (h t) -> p h t", h=GRP), bank(item)[:, 0:GRP * T].rearrange("p (h t) -> p h t", h=GRP),
                                      bq_sb[:, GRP * n:GRP * n + GRP].rearrange("p (h a) -> p h a", a=1).to_broadcast([P, GRP, T]), ALU.add).then_inc(s_qb, 1)

            def head(s, p, b, i):
                if live(s):
                    n = NH * s + b
                    eng.wait_ge(s_sc, n + 1)
                    at_least(eng, s_ex, n - 1)
                    hold_vector(eng, cell)
                    eng.tensor_tensor_reduce(out=nsc[:, b % 2, :], in0=sc[b % 2][0:T, 0:SE], in1=mask_sb[:, :], scale=-1.0, scalar=3.0e38,
                                             op0=ALU.add, op1=ALU.min, accum_out=nmx[:, b % 4:b % 4 + 1]).then_inc(s_tt, 1)
                at = lagged(s, p, b, 1)
                if at and (live(s) or b < 1):
                    s_, p_, h = at
                    n = NH * s_ + h
                    eng.wait_ge(s_ex, n + 1)
                    eng.reciprocal(rin[:, h % 4:h % 4 + 1], tot[:, h % 4:h % 4 + 1]).then_inc(s_ri, 1)
                    eng.wait_ge(s_ri, n + 1)
                    eng.tensor_scalar(prob[:, h % 4, 0:SE], prob[:, h % 4, 0:SE], rin[:, h % 4:h % 4 + 1], None, ALU.mult).then_inc(s_pn, 1)
                if b == 6 and not (isinstance(s, int) and s == 0):
                    q = 1 - p
                    n = i - 1 if p == 0 else i
                    eng.wait_ge(s_o, s)
                    eng.wait_ge(s_xr[q], 16 * (n + 1))
                    at_least(eng, s_st[q], 16 * n)
                    eng.tensor_tensor(x2o[:, q, :], pout[0:T, :], xr[:, q, :], ALU.add).then_inc(s_x2, 1)

            over_sequences(eng, projection, head)

        @block.tensor
        def _(eng):
            eng.wait_ge(s_const, 6)
            eng.wait_ge(s_w, 64)

            def projection(item, s, i, p):
                if item == "ln":
                    return
                if item == "hT":
                    eng.wait_ge(s_h, s + 1)
                    pj_free(eng, item, s)
                    for k in range(KT):
                        mm = eng.transpose(bank(item)[:, T * k:T * k + T], hn[:, P * k:P * k + P], ident[0:T, 0:T])
                elif item[0] == "c":
                    k = int(item[1:])
                    if k == 0:
                        eng.wait_ge(s_cx[p], 32 * (i + 1))
                    pj_free(eng, item, s)
                    for e in range(ET):
                        rows = P if e < ET - 1 else EREM
                        mm = eng.transpose(bank(item)[:, P * e:P * e + rows], cx[0:rows, p, e, P * k:P * k + P], ident[0:rows, 0:rows])
                elif item.startswith("ks"):
                    n = int(item[2:])
                    eng.wait_ge(s_ksq, NKV * s + n + 1)
                    pj_free(eng, item, s)
                    mm = eng.matmul(bank(item)[:, 0:SE], ones[:, :], ksq[:, n % 2, :], start=True, stop=True)
                elif item.startswith("qs"):
                    n = int(item[2:])
                    eng.wait_ge(s_qsq, NKV * s + n + 1)
                    pj_free(eng, item, s)
                    mm = eng.matmul(bank(item)[:, 0:GRP * T], ones[:, :], qsq[:, n % 2, :], start=True, stop=True)
                elif item[0] == "k":
                    n = int(item[1:])
                    if n == 0:
                        eng.wait_ge(s_cT, KT * s + KT)
                    pj_free(eng, item, s)
                    for k in range(KT):
                        mm = eng.matmul(bank(item)[:, 0:SE], wk_sb[:, k, HD * n:HD * n + HD], cT[:, k, :], start=(k == 0), stop=(k == KT - 1))
                elif item[0] == "v":
                    e = int(item[1:])
                    rows = P if e < ET - 1 else EREM
                    pj_free(eng, item, s)
                    for k in range(KT):
                        mm = eng.matmul(bank(item)[0:rows, :], cT[:, k, P * e:P * e + rows], wv_sb[:, k, :], start=(k == 0), stop=(k == KT - 1))
                elif item[0] == "q":
                    n = int(item[1:])
                    if n == 0:
                        eng.wait_ge(s_hT, s + 1)
                    pj_free(eng, item, s)
                    for h in range(GRP):
                        c = HD * (GRP * n + h)
                        for k in range(KT):
                            mm = eng.matmul(bank(item)[:, T * h:T * h + T], wq_sb[:, k, c:c + HD], hT[:, k, :], start=(k == 0), stop=(k == KT - 1))
                mm.then_inc(s_pj, 1)

            def head(s, p, b, i):
                if live(s):
                    n = NH * s + b
                    if b % 4 == 0:
                        eng.wait_ge(s_kT, NKV * s + b // 4 + 1)
                        eng.wait_ge(s_qT, NKV * s + b // 4 + 1)
                    at_least(eng, s_tt, n - 1)
                    eng.matmul(sc[b % 2][0:T, 0:SE], qT[:, p, b, :], kT[:, p, b // 4, :], start=True, stop=True).then_inc(s_sc, 1)
                at = lagged(s, p, b, 2)
                if at and (live(s) or b < 2):
                    s_, p_, h = at
                    n = NH * s_ + h
                    eng.wait_ge(s_pn, n + 1)
                    at_least(eng, s_pT, n - 1)
                    for e in range(ET):
                        mm = eng.transpose(tp[h % 2][:, T * e:T * e + T], prob[:, h % 4, P * e:P * e + P], ident[0:T, 0:T])
                    mm.then_inc(s_tp, 1)
                if b % 4 == 3:
                    at = lagged(s, p, b, 7)
                    if at and (live(s) or b < 7):
                        s_, p_, h = at
                        n = h // 4
                        eng.wait_ge(s_pT, NH * s_ + h + 4)
                        if n == 0:
                            eng.wait_ge(s_v, ET * s_ + ET)
                        at_least(eng, s_aT, NKV * s_ + n)
                        for e in range(ET):
                            rows = P if e < ET - 1 else EREM
                            mm = eng.matmul(po[:, 0:GRP * T], v[0:rows, p_, e, HD * n:HD * n + HD],
                                            pT[0:rows, n % 2, e, :, :].rearrange("p h t -> p (h t)"), start=(e == 0), stop=(e == ET - 1))
                        mm.then_inc(s_pv, 1)
                if b in OUT_AT and not (isinstance(s, int) and s == 0):
                    n = OUT_AT.index(b)
                    eng.wait_ge(s_aT, NKV * (s - 1) + n + 1)
                    if n == 0:
                        at_least(eng, s_x2, s - 1)
                    for h in range(GRP * n, GRP * n + GRP):
                        mm = eng.matmul(pout[0:T, :], aT[:, h, :], wo_sb[:, h, :], start=(h == 0), stop=(h == NH - 1))
                    if n == NKV - 1:
                        mm.then_inc(s_o, 1)

            over_sequences(eng, projection, head)


TOK = B * T
NT = TOK // P
TG = 5
NG = NT // TG
GT = TG * P
HALF = GT // 2
NE, NI, CAP = 16, 352, 256
NS = 704
NIT = [P, P, NI - 2 * P]
NST = [P] * (NS // P) + [NS % P]
CT2 = CAP // P
SLOTS = NE * CAP


def phase_c(nc, x2, gate_w, w_gate, w_up, w_down, ws_gate, ws_up, ws_down, out):
    h_dram = nc.dram_tensor("h_rows", [TOK, H], F32, kind="Internal").ap()
    slot_dram = nc.dram_tensor("slot_token", [SLOTS, 1], U32, kind="Internal").ap()
    e_dram = nc.dram_tensor("expert_rows", [SLOTS, H], F32, kind="Internal").ap()
    x_rows = x2.rearrange("b t d -> (b t) d")
    out_rows = out.rearrange("b t d -> (b t) d")

    def rows(ap, first, tiles):
        return ap[bass.ds(first, tiles * P), :].rearrange("(t p) d -> p t d", p=P)

    with ExitStack() as stack:
        m = Memory(nc, stack, "c")
        sb, ps, sem = m.sb, m.ps, m.sem
        acc = sb("acc", [P, NT, H])
        wts = sb("wts", [P, NT, 2])
        place = sb("place", [P, NT, 2], U32)
        ident = sb("ident", [P, P])
        pool_cells = sb("pool_cells", [1, 3])
        s_const, s_held = sem("const_ready"), sem("pool_held")
        wsg = sb("wsg", [P, KT, NS])
        wsu = sb("wsu", [P, KT, NS])
        wsd = sb("wsd", [P, len(NST), H])
        gw = sb("gw", [NE, H])
        gwT = sb("gwT", [P, KT, NE])
        upper = sb("upper", [P, P], BF16)
        ones = sb("ones", [P, P], BF16)
        iota16 = sb("iota16", [P, TG, NE])
        zero = sb("zero", [P, SLOTS // P], U32)
        eps = sb("eps", [P, 1])
        cell = (sb("cells", [1, CELLS]), list(range(CELLS)))
        tokf = sb("tokf", [P, TG])
        tok = sb("tok", [P, TG], U32)
        stats = sb("stats", [P, TG, 6])
        mv = sb("mv", [P, TG, 2])
        lnv = sb("lnv", [P, TG])
        rstd = sb("rstd", [P, TG])
        hn = sb("hn", [P, TG, H])
        hT = sb("hT", [P, KT, GT])
        mx = sb("mx", [P, TG])
        lg = sb("lg", [P, TG, NE])
        pr = sb("pr", [P, TG, NE])
        tot = sb("tot", [P, TG])
        rtot = sb("rtot", [P, TG])
        m8 = sb("m8", [P, TG, 8])
        i8 = sb("i8", [P, TG, 8], U32)
        idx = sb("idx", [P, 2, TG])
        oh = sb("oh", [P, 2, TG, NE])
        msk = sb("msk", [P, TG, NE], BF16)
        carry = sb("carry", [P, NE])
        pos = sb("pos", [P, TG, NE])
        ohp = sb("ohp", [P, 2, TG, NE])
        pk = sb("pk", [P, 2, TG])
        over = sb("over", [P, 2, TG])
        slot = sb("slot", [P, 2, TG])
        dsl = sb("dsl", [P, 2, TG], U32)
        sg = sb("sg", [P, 2, HALF])
        gs = sb("gs", [P, 2, HALF])
        aT = sb("aT", [P, len(NST), GT])

        tr = [ps(f"tr{n}", [P, 512]) for n in range(2)]
        rt = ps("rt", [P, 512])
        pz = ps("pz", [P, 512])
        pg = [ps(f"pg{n}", [P, 512]) for n in range(2)]
        pu = [ps(f"pu{n}", [P, 512]) for n in range(2)]

        s_w, s_x, s_zero, s_mem = sem("weights_loaded"), sem("x_loaded"), sem("slots_zeroed"), sem("memsets")
        s_hst, s_scat = sem("h_stored"), sem("scattered")
        s_gwt, s_gw = sem("gate_in_psum"), sem("gate_T")
        s_stats, s_mv, s_lnv, s_rstd, s_h = (sem(n) for n in ("stats", "mv", "lnv", "rstd", "h"))
        s_tr, s_hT, s_lg, s_pos, s_down = sem("h_in_psum"), sem("hT"), sem("logits"), sem("positions"), sem("down")
        s_r, s_ex, s_disp = sem("route_step"), sem("route_exp"), sem("slots")
        s_gu, s_se, s_sm, s_sl, s_ss, s_gs, s_aT, s_acc = (sem(n) for n in (
            "gate_up", "silu_exp", "silu_min", "silu_ln", "silu_sigm", "silu", "aT", "acc"))
        R_MAX, R_SUB, R_SUM, R_REC, R_PROB = 0, 1, 2, 3, 4
        R_TOP = 5
        R_IDX = R_TOP + TG
        R_CVT = R_IDX + TG
        R_OH = R_CVT + 3
        R_MSK = R_OH + 2
        R_POS, R_CARRY = R_MSK + 1, R_MSK + 2
        R_OHP = R_CARRY + 1
        R_PK = R_OHP + 2
        R_OVER, R_MIN, R_SLOT, R_PLACE, R_OUT, R_NEXT = (R_PK + n for n in (1, 2, 3, 4, 5, 6))
        NR = R_NEXT + 1

        NIS = len(NST)
        wgu = sb("wgu", [P, 2, 2, KT, NI])
        wd = sb("wd", [P, 2, len(NIT), H])
        ids = sb("ids", [P, 2, CT2], U32)
        hg = hn[:, 0:2 * CT2, :].rearrange("p (a c) d -> p a c d", a=2)
        hgT = sb("hgT", [P, 2, KT, CAP])
        esg = sb("esg", [P, 2, CAP])
        egs = sb("egs", [P, 2, CAP])
        eaT = sb("eaT", [P, 2, len(NIT), CAP])
        eo = sb("eo", [P, 2, CT2, H])
        gu = [rt, pz, pu[0]]
        dn = pg
        er = wgu[:, :, :, :, :].rearrange("p a b k n -> p (a b k n)")[:, 0:TG * 2 * H].rearrange("p (t k d) -> p t k d", t=TG, k=2)
        s_ew, s_ewd = ([sem(f"{w}_loaded{n}") for n in range(2)] for w in ("gate_up_weights", "down_weights"))
        s_ids = [sem(f"ids_loaded{n}") for n in range(2)]
        s_hg = [sem(f"rows_gathered{n}") for n in range(2)]
        s_es = [sem(f"results_stored{n}") for n in range(2)]
        s_etr, s_ehT, s_egu, s_dn, s_eo = (sem(n) for n in ("rows_in_psum", "rows_T", "expert_gate_up", "expert_down", "results"))
        s_ese, s_esm, s_esl, s_ess, s_egs, s_eaT = (sem("expert_" + n) for n in ("silu_exp", "silu_min", "silu_ln", "silu_sigm", "silu", "aT"))
        s_sum, s_out = sem("summed"), sem("out_stored")
        s_er = [sem(f"result_rows{t}") for t in range(TG)]
        NIE = len(NIT)

        block = stack.enter_context(nc.Block())

        def over_groups(eng, group):
            group(0)
            with eng.Fori(1, NG - 1) as g:
                group(g)

        def over_experts(eng, expert):
            expert(0, 0, 0)
            expert(1, 0, 1)
            with eng.Fori(1, NE // 2) as i:
                expert(2 * i, i, 0)
                expert(2 * i + 1, i, 1)

        BEHIND = {n: (2 * n - 4, 2 * n - 3) for n in range(2, 2 * NIS)}

        @block.sync
        def _(eng):
            for g in range(NG):
                at_least(eng, s_x, 16 * g)
                eng.dma_start(acc[:, TG * g:TG * g + TG, :], rows(x_rows, GT * g, TG)).then_inc(s_x, 16)
                if g == 0:
                    eng.dma_start(gw[:, :], gate_w).then_inc(s_w, 16)
                    eng.dma_start(wsg[:, :, :], ws_gate.rearrange("(k p) n -> p k n", p=P)).then_inc(s_w, 16)
                    eng.dma_start(wsu[:, :, :], ws_up.rearrange("(k p) n -> p k n", p=P)).then_inc(s_w, 16)
                    n = P * (NIS - 1)
                    eng.dma_start(wsd[:, 0:NIS - 1, :], ws_down[0:n].rearrange("(k p) n -> p k n", p=P)).then_inc(s_w, 16)
                    eng.dma_start(wsd[0:NST[-1], NIS - 1, :], ws_down[n:NS]).then_inc(s_w, 16)
            eng.wait_ge(s_mem, 3)
            eng.dma_start(slot_dram.rearrange("(p n) a -> p (n a)", p=P), zero[:, :]).then_inc(s_zero, 16)

            def store_h(g):
                eng.wait_ge(s_h, TG * g + TG)
                eng.dma_start(rows(h_dram, GT * g, TG), hn[:, :, :]).then_inc(s_hst, 16)

            over_groups(eng, store_h)
            store_h(NG - 1)

            def expert(e, i, p):
                at_least(eng, s_egu, NIE * (e - 1))
                for n, w in ((0, w_gate), (1, w_up)):
                    eng.dma_start(wgu[:, p, n, :, :], w[bass.ds(e, 1)].rearrange("a (k p) n -> p (a k) n", p=P)).then_inc(s_ew[p], 16)
                if isinstance(e, int) and e == 0:
                    eng.wait_ge(s_scat, 160 * NG)
                at_least(eng, s_etr, CT2 * (e - 1))
                eng.dma_start(ids[:, p, :], slot_dram[bass.ds(CAP * e, CAP), :].rearrange("(c p) a -> p (c a)", p=P),
                              allow_slow_non_contiguous=True).then_inc(s_ids[p], 16)
                at_least(eng, s_dn, CT2 * (e - 1))
                n = P * (NIE - 1)
                eng.dma_start(wd[:, p, 0:NIE - 1, :], w_down[bass.ds(e, 1), 0:n, :].rearrange("a (k p) n -> p (a k) n", p=P)).then_inc(s_ewd[p], 16)
                eng.dma_start(wd[0:NIT[-1], p, NIE - 1, :], w_down[bass.ds(e, 1), n:NI, :].rearrange("a k n -> k (a n)")).then_inc(s_ewd[p], 16)

            over_experts(eng, expert)
            for g in range(NG):
                eng.wait_ge(s_sum, 2 * TG * g + 2 * TG)
                eng.dma_start(rows(out_rows, GT * g, TG), acc[:, TG * g:TG * g + TG, :]).then_inc(s_out, 16)
            eng.wait_ge(s_out, 16 * NG)
            eng.wait_ge(s_hst, 16 * NG)
            eng.wait_ge(s_zero, 16)

        @block.gpsimd
        def _(eng):
            eng.memset(ident[:, :], 0.0).then_inc(s_const, 1)
            eng.memset(pool_cells[:, :], 1.0).then_inc(s_const, 1)
            eng.memset(upper[:, :], 1.0).then_inc(s_const, 1)
            eng.memset(ones[:, :], 1.0).then_inc(s_const, 1)
            eng.iota(iota16[:, :, :], pattern=[[0, TG], [1, NE]], base=0, channel_multiplier=0, allow_small_or_imprecise_dtypes=True).then_inc(s_const, 1)
            eng.iota(tokf[:, :], pattern=[[P, TG]], base=0, channel_multiplier=1, allow_small_or_imprecise_dtypes=True).then_inc(s_const, 1)
            eng.wait_ge(s_const, 6)
            eng.affine_select(out=ident[:, :], in_=ident[:, :], compare_op=ALU.not_equal, fill=1.0, base=0,
                              pattern=[[-1, P]], channel_multiplier=1).then_inc(s_const, 1)
            eng.affine_select(out=upper[:, :], in_=upper[:, :], compare_op=ALU.is_gt, fill=0.0, base=0,
                              pattern=[[1, P]], channel_multiplier=-1).then_inc(s_const, 1)
            eng.wait_ge(s_zero, 16)

            def scatter(g):
                eng.wait_ge(s_disp, g + 1)
                hold_pool(eng, pool_cells, s_held, g)
                for k in range(2):
                    for t in range(TG):
                        eng.indirect_dma_start(out=slot_dram, out_offset=bass.IndirectOffsetOnAxis(ap=dsl[:, k, t:t + 1], axis=0),
                                               in_=tok[:, t:t + 1], in_offset=None, bounds_check=SLOTS - 1, oob_is_err=False).then_inc(s_scat, 16)

            over_groups(eng, scatter)
            scatter(NG - 1)
            eng.wait_ge(s_hst, 16 * NG)
            eng.wait_ge(s_tr, TG * NG)

            def expert(e, i, p):
                eng.wait_ge(s_ids[p], 16 * (i + 1))
                at_least(eng, s_etr, CT2 * (e - 1))
                hold_pool(eng, pool_cells, s_held, NG + e)
                for c in range(CT2):
                    eng.indirect_dma_start(out=hg[:, p, c, :], out_offset=None, in_=h_dram,
                                           in_offset=bass.IndirectOffsetOnAxis(ap=ids[:, p, c:c + 1], axis=0)).then_inc(s_hg[p], 16)

            over_experts(eng, expert)
            for p in range(2):
                eng.wait_ge(s_es[p], 16 * (NE // 2))
            eng.wait_ge(s_dn, CT2 * NE)
            for n in range(NT):
                at_least(eng, s_sum, 2 * (n - TG) + 2)
                for k in range(2):
                    eng.indirect_dma_start(out=er[:, n % TG, k, :], out_offset=None, in_=e_dram,
                                           in_offset=bass.IndirectOffsetOnAxis(ap=place[:, n, k:k + 1], axis=0)).then_inc(s_er[n % TG], 16)

        @block.scalar
        def _(eng):
            eng.preload_act_table_set(TABLES)
            eng.wait_ge(s_gwt, 1)
            eng.copy(gwT[:, :, :], rt[:, 0:KT * NE].rearrange("p (k e) -> p k e", k=KT)).then_inc(s_gw, 1)
            eng.wait_ge(s_mem, 3)

            def norm(g):
                eng.wait_ge(s_mv, TG * g + TG)
                eng.activation(lnv[:, :], mv[:, :, 1], ACT.Ln, bias=eps[:, :]).then_inc(s_lnv, 1)
                eng.wait_ge(s_lnv, g + 1)
                eng.activation(rstd[:, :], lnv[:, :], ACT.Exp, scale=-0.5).then_inc(s_rstd, 1)

            def transposed(g):
                at_least(eng, s_gu, 2 * NIS * g)
                for t in range(TG):
                    eng.wait_ge(s_tr, TG * g + t + 1)
                    eng.copy(hT[:, :, P * t:P * t + P], tr[t % 2][:, :].rearrange("p (k t) -> p k t", k=KT)).then_inc(s_hT, 1)

            def softmax(g):
                eng.wait_ge(s_r, NR * g + R_SUB + 1)
                eng.activation(pr[:, :, :], lg[:, :, :], ACT.Exp).then_inc(s_ex, 1)

            def silu(g, n):
                r = NST[n // 2]
                at = 2 * NIS * g + n
                eng.wait_ge(s_gu, at + 1)
                at_least(eng, s_gs, at - 1 if n >= 2 else 2 * NIS * g)
                eng.activation(sg[0:r, n % 2, :], pg[n % 2][0:r, 0:HALF], ACT.Exp, scale=-1.0).then_inc(s_se, 1)
                eng.wait_ge(s_sm, at + 1)
                eng.activation(sg[0:r, n % 2, :], sg[0:r, n % 2, :], ACT.Ln, bias=1.0).then_inc(s_sl, 1)
                eng.wait_ge(s_sl, at + 1)
                eng.activation(sg[0:r, n % 2, :], sg[0:r, n % 2, :], ACT.Exp, scale=-1.0).then_inc(s_ss, 1)

            def group(g):
                softmax(g)
                for n in range(2 * NIS):
                    silu(g, n)
                    if n == 5:
                        norm(g + 1)
                transposed(g + 1)

            norm(0)
            transposed(0)
            over_groups(eng, group)
            softmax(NG - 1)

            def results(e, p, i):
                at_least(eng, s_es[p], 16 * i)
                for c in range(CT2):
                    eng.wait_ge(s_dn, CT2 * e + c + 1)
                    eng.copy(eo[:, p, c, :], dn[c][:, :]).then_inc(s_eo, 1)
                eng.wait_ge(s_eo, CT2 * e + CT2)
                eng.dma_start(rows(e_dram, CAP * e, CT2), eo[:, p, :, :]).then_inc(s_es[p], 16)

            def expert(e, i, p):
                at_least(eng, s_egu, NIE * (e - 1))
                for c in range(CT2):
                    eng.wait_ge(s_etr, CT2 * e + c + 1)
                    eng.copy(hgT[:, p, :, P * c:P * c + P], tr[c][:, :].rearrange("p (k t) -> p k t", k=KT)).then_inc(s_ehT, 1)
                for n in range(NIE):
                    at, r = NIE * e + n, NIT[n]
                    q = (p + n) % 2
                    eng.wait_ge(s_egu, at + 1)
                    at_least(eng, s_egs, at - 1)
                    eng.activation(esg[0:r, q, :], gu[n][0:r, 0:CAP], ACT.Exp, scale=-1.0).then_inc(s_ese, 1)
                    eng.wait_ge(s_esm, at + 1)
                    eng.activation(esg[0:r, q, :], esg[0:r, q, :], ACT.Ln, bias=1.0).then_inc(s_esl, 1)
                    eng.wait_ge(s_esl, at + 1)
                    eng.activation(esg[0:r, q, :], esg[0:r, q, :], ACT.Exp, scale=-1.0).then_inc(s_ess, 1)
                if not (isinstance(e, int) and e == 0):
                    results(e - 1, 1 - p, i if p else i - 1)

            over_experts(eng, expert)
            results(NE - 1, 1, NE // 2 - 1)
            for n in range(2 * NIS):
                silu(NG - 1, n)

        @block.vector
        def _(eng):
            eng.memset(zero[:, :], 0).then_inc(s_mem, 1)
            eng.memset(eps[:, :], 1e-5).then_inc(s_mem, 1)
            eng.memset(carry[:, :], 0.0).then_inc(s_mem, 1)
            eng.wait_ge(s_mem, 3)
            eng.wait_ge(s_const, 8)

            def bc(ap):
                return ap.rearrange("p (t a) -> p t a", a=1).to_broadcast([P, TG, NE])

            def token_row(g, t):
                return acc[:, bass.ds(TG * g + t, 1), :].rearrange("p a d -> p (a d)")

            def norm(g):
                eng.wait_ge(s_x, 16 * g + 16)
                for t in range(TG):
                    eng.bn_stats(stats[:, t, :], token_row(g, t)).then_inc(s_stats, 1)
                for t in range(TG):
                    eng.wait_ge(s_stats, TG * g + t + 1)
                    hold_vector(eng, cell)
                    eng.bn_aggr(mv[:, t, :], stats[:, t, :]).then_inc(s_mv, 1)
                eng.wait_ge(s_rstd, g + 1)
                at_least(eng, s_hst, 16 * g)
                at_least(eng, s_tr, TG * g)
                for t in range(TG):
                    eng.tensor_scalar(hn[:, t, :], token_row(g, t), mv[:, t, 0:1], rstd[:, t:t + 1],
                                      ALU.subtract, ALU.mult).then_inc(s_h, 1)

            def add_down(g, t):
                eng.wait_ge(s_down, TG * g + t + 1)
                eng.tensor_tensor(token_row(g, t), tr[(TG + t) % 2][:, :], token_row(g, t), ALU.add).then_inc(s_acc, 1)

            def route_step(g, step):
                def done(instruction, name):
                    assert step[0] == name, (step, name)
                    instruction.then_inc(s_r, 1)
                    step[0] += 1

                def after(name):
                    eng.wait_ge(s_r, NR * g + name + 1)

                return done, after

            def route(g):
                step = [0]
                done, after = route_step(g, step)

                def rest(t):
                    if not (isinstance(g, int) and g == 0):
                        add_down(g - 1, t)

                eng.wait_ge(s_lg, g + 1)
                logits = rt[:, 0:TG * NE].rearrange("p (t e) -> p t e", t=TG)
                done(eng.reduce_max(mx[:, :], logits, axis=mybir.AxisListType.X), R_MAX)
                after(R_MAX)
                done(eng.tensor_tensor(lg[:, :, :], logits, bc(mx[:, :]), ALU.subtract), R_SUB)
                rest(0)
                eng.wait_ge(s_ex, g + 1)
                done(eng.reduce_sum(tot[:, :], pr[:, :, :], axis=mybir.AxisListType.X), R_SUM)
                after(R_SUM)
                done(eng.reciprocal(rtot[:, :], tot[:, :]), R_REC)
                after(R_REC)
                done(eng.tensor_tensor(pr[:, :, :], pr[:, :, :], bc(rtot[:, :]), ALU.mult), R_PROB)
                rest(1)
                after(R_PROB)
                hold_vector(eng, cell)
                for t in range(TG):
                    done(eng.max(m8[:, t, :], pr[:, t, :]), R_TOP + t)
                rest(2)
                for t in range(TG):
                    after(R_TOP + t)
                    hold_vector(eng, cell)
                    done(eng.max_index(i8[:, t, :], m8[:, t, :], pr[:, t, :]), R_IDX + t)
                after(R_IDX + TG - 1)
                for k in range(2):
                    done(eng.tensor_copy(idx[:, k, :], i8[:, :, k]), R_CVT + k)
                done(eng.tensor_copy(wts[:, bass.ds(TG * g, TG), :], m8[:, :, 0:2]), R_CVT + 2)
                rest(3)
                for k in range(2):
                    after(R_CVT + k)
                    done(eng.tensor_tensor(oh[:, k, :, :], iota16[:, :, :], bc(idx[:, k, :]), ALU.is_equal), R_OH + k)
                after(R_OH + 1)
                at_least(eng, s_pos, g)
                done(eng.tensor_tensor(msk[:, :, :], oh[:, 0, :, :], oh[:, 1, :, :], ALU.add), R_MSK)
                rest(4)
                return step

            def route_end(g, step):
                done, after = route_step(g, step)
                eng.wait_ge(s_pos, g + 1)
                done(eng.tensor_tensor(pos[:, :, :], pz[:, 0:TG * NE].rearrange("p (t e) -> p t e", t=TG),
                                       carry[:, :].rearrange("p (a e) -> p a e", a=1).to_broadcast([P, TG, NE]), ALU.add), R_POS)
                after(R_POS)
                done(eng.tensor_tensor(carry[:, :], carry[:, :], pz[:, TG * NE:TG * NE + NE], ALU.add), R_CARRY)
                for k in range(2):
                    done(eng.tensor_tensor(ohp[:, k, :, :], oh[:, k, :, :], pos[:, :, :], ALU.mult), R_OHP + k)
                after(R_OHP + 1)
                done(eng.reduce_sum(pk[:, :, :].rearrange("p k t -> p (k t)"), ohp[:, :, :, :].rearrange("p k t e -> p (k t) e"),
                                    axis=mybir.AxisListType.X), R_PK)
                after(R_PK)
                done(eng.tensor_scalar(over[:, :, :], pk[:, :, :], float(CAP), float(4 * SLOTS), ALU.is_ge, ALU.mult), R_OVER)
                done(eng.tensor_scalar(pk[:, :, :], pk[:, :, :], float(CAP - 1), None, ALU.min), R_MIN)
                after(R_MIN)
                done(eng.scalar_tensor_tensor(out=slot[:, :, :], in0=idx[:, :, :], scalar=float(CAP), in1=pk[:, :, :], op0=ALU.mult, op1=ALU.add), R_SLOT)
                after(R_SLOT)
                done(eng.tensor_copy(place[:, bass.ds(TG * g, TG), :].rearrange("p t k -> p k t"), slot[:, :, :]), R_PLACE)
                at_least(eng, s_scat, 160 * g)
                done(eng.tensor_copy(tok[:, :], tokf[:, :]), R_OUT)
                after(R_OUT)
                eng.tensor_tensor(dsl[:, :, :], slot[:, :, :], over[:, :, :], ALU.add).then_inc(s_disp, 1)
                done(eng.tensor_scalar(tokf[:, :], tokf[:, :], float(GT), None, ALU.add), R_NEXT)
                assert step[0] == NR

            def silu(g, n):
                r, c = NST[n // 2], n % 2
                at = 2 * NIS * g + n
                eng.wait_ge(s_se, at + 1)
                eng.tensor_scalar(sg[0:r, c, :], sg[0:r, c, :], E_MAX, None, ALU.min).then_inc(s_sm, 1)
                eng.wait_ge(s_ss, at + 1)
                at_least(eng, s_aT, at - 1 if n >= 2 else 2 * NIS * g)
                eng.tensor_tensor(gs[0:r, c, :], pg[c][0:r, 0:HALF], sg[0:r, c, :], ALU.mult).then_inc(s_gs, 1)
                eng.wait_ge(s_gs, at + 1)
                if n == 0:
                    at_least(eng, s_down, TG * g)
                eng.tensor_tensor(aT[0:r, n // 2, HALF * c:HALF * c + HALF], pu[c][0:r, 0:HALF], gs[0:r, c, :], ALU.mult).then_inc(s_aT, 1)

            def group(g):
                step = route(g)
                for n in range(2 * NIS):
                    silu(g, n)
                    if n == 1:
                        route_end(g, step)
                    if n == 5:
                        norm(g + 1)

            norm(0)
            over_groups(eng, group)
            route_end(NG - 1, route(NG - 1))

            def expert(e, i, p):
                for n in range(NIE):
                    at, r = NIE * e + n, NIT[n]
                    q = (p + n) % 2
                    eng.wait_ge(s_ese, at + 1)
                    eng.tensor_scalar(esg[0:r, q, :], esg[0:r, q, :], E_MAX, None, ALU.min).then_inc(s_esm, 1)
                    eng.wait_ge(s_ess, at + 1)
                    at_least(eng, s_eaT, at - 1)
                    eng.tensor_tensor(egs[0:r, q, :], gu[n][0:r, 0:CAP], esg[0:r, q, :], ALU.mult).then_inc(s_egs, 1)
                    eng.wait_ge(s_egs, at + 1)
                    if n == 0:
                        at_least(eng, s_dn, CT2 * (e - 1))
                    eng.tensor_tensor(eaT[0:r, p, n, :], gu[n][0:r, CAP:2 * CAP], egs[0:r, q, :], ALU.mult).then_inc(s_eaT, 1)

            over_experts(eng, expert)

            def combine(n):
                eng.wait_ge(s_acc, n + 1)
                eng.wait_ge(s_er[n % TG], 32 * (n // TG) + 32)
                for k in range(2):
                    if k:
                        eng.wait_ge(s_sum, 2 * n + 1)
                    eng.scalar_tensor_tensor(out=acc[:, n, :], in0=er[:, n % TG, k, :], scalar=wts[:, n, k:k + 1], in1=acc[:, n, :],
                                             op0=ALU.mult, op1=ALU.add).then_inc(s_sum, 1)

            eng.wait_ge(s_r, NR * NG)
            for n in range(2 * NIS):
                silu(NG - 1, n)
                for tile in BEHIND.get(n, ()):
                    combine(tile)
            for t in range(TG):
                add_down(NG - 1, t)
            for t in range(TG):
                combine(TG * (NG - 1) + t)

        @block.tensor
        def _(eng):
            eng.wait_ge(s_const, 8)
            eng.wait_ge(s_w, 80)
            for k in range(KT):
                mm = eng.transpose(rt[:, NE * k:NE * k + NE], gw[:, P * k:P * k + P], ident[0:NE, 0:NE])
            mm.then_inc(s_gwt, 1)
            eng.wait_ge(s_gw, 1)

            def head(g):
                for t in range(TG):
                    eng.wait_ge(s_h, TG * g + t + 1)
                    if t < 2:
                        at_least(eng, s_acc, TG * (g - 1))
                        at_least(eng, s_hT, TG * g)
                    else:
                        eng.wait_ge(s_hT, TG * g + t - 1)
                    for k in range(KT):
                        mm = eng.transpose(tr[t % 2][:, P * k:P * k + P], hn[:, t, P * k:P * k + P], ident[:, :])
                    mm.then_inc(s_tr, 1)
                at_least(eng, s_r, NR * g)
                for t in range(TG):
                    eng.wait_ge(s_hT, TG * g + t + 1)
                    for k in range(KT):
                        mm = eng.matmul(rt[:, NE * t:NE * t + NE], hT[:, k, P * t:P * t + P], gwT[:, k, :], start=(k == 0), stop=(k == KT - 1))
                mm.then_inc(s_lg, 1)

            def inner(g, n):
                r, c = NST[n // 2], n % 2
                at_least(eng, s_aT, 2 * NIS * g + n - 1 if n >= 2 else 2 * NIS * g)
                for w, dst in ((wsg, pg[c]), (wsu, pu[c])):
                    for k in range(KT):
                        mm = eng.matmul(dst[0:r, 0:HALF], w[:, k, P * (n // 2):P * (n // 2) + r], hT[:, k, HALF * c:HALF * c + HALF],
                                        start=(k == 0), stop=(k == KT - 1))
                mm.then_inc(s_gu, 1)

            def ranks(g):
                eng.wait_ge(s_r, NR * g + R_MSK + 1)
                for t in range(TG + 1):
                    o = pz[:, NE * t:NE * t + NE]
                    parts = [(ones, u) for u in range(min(t, TG))] + ([(upper, t)] if t < TG else [])
                    for n, (w, u) in enumerate(parts):
                        mm = eng.matmul(o, w[:, :], msk[:, u, :], start=(n == 0), stop=(n == len(parts) - 1))
                mm.then_inc(s_pos, 1)

            def down(g):
                eng.wait_ge(s_aT, 2 * NIS * g + 2 * NIS)
                for t in range(TG):
                    if t >= 2:
                        eng.wait_ge(s_acc, TG * g + t - 1)
                    for n in range(NIS):
                        r = NST[n]
                        mm = eng.matmul(tr[(TG + t) % 2][:, :], aT[0:r, n, P * t:P * t + P], wsd[0:r, n, :], start=(n == 0), stop=(n == NIS - 1))
                    mm.then_inc(s_down, 1)

            def group(g):
                for n in range(2 * NIS):
                    inner(g, n)
                    if n == 1:
                        ranks(g)
                head(g + 1)
                down(g)

            head(0)
            over_groups(eng, group)
            ranks(NG - 1)
            eng.wait_ge(s_acc, TG * (NG - 1))
            eng.wait_ge(s_aT, 2 * NIS * (NG - 1))
            eng.wait_ge(s_r, NR * NG)

            def down_expert(e, p, i):
                eng.wait_ge(s_ewd[p], 32 * (i + 1))
                eng.wait_ge(s_eaT, NIE * e + NIE)
                for c in range(CT2):
                    at_least(eng, s_eo, CT2 * (e - 1) + c + 1)
                    for n in range(NIE):
                        r = NIT[n]
                        mm = eng.matmul(dn[c][:, :], eaT[0:r, p, n, P * c:P * c + P], wd[0:r, p, n, :], start=(n == 0), stop=(n == NIE - 1))
                    mm.then_inc(s_dn, 1)

            def expert(e, i, p):
                eng.wait_ge(s_hg[p], 16 * CT2 * (i + 1))
                for c in range(CT2):
                    at_least(eng, s_ehT, CT2 * (e - 1) + c + 1)
                    for k in range(KT):
                        mm = eng.transpose(tr[c][:, P * k:P * k + P], hg[:, p, c, P * k:P * k + P], ident[:, :])
                    mm.then_inc(s_etr, 1)
                eng.wait_ge(s_ehT, CT2 * e + CT2)
                eng.wait_ge(s_ew[p], 32 * (i + 1))
                for n in range(NIE):
                    r = NIT[n]
                    at_least(eng, s_eaT, NIE * (e - 1) + n + 1)
                    for half, w in ((0, 0), (CAP, 1)):
                        for k in range(KT):
                            mm = eng.matmul(gu[n][0:r, half:half + CAP], wgu[:, p, w, k, P * n:P * n + r], hgT[:, p, k, :],
                                            start=(k == 0), stop=(k == KT - 1))
                    mm.then_inc(s_egu, 1)
                if not (isinstance(e, int) and e == 0):
                    down_expert(e - 1, 1 - p, i if p else i - 1)

            over_experts(eng, expert)
            down_expert(NE - 1, 1, NE // 2 - 1)
            eng.wait_ge(s_eo, CT2 * NE)
            eng.wait_ge(s_ehT, CT2 * NE)
            for n in range(2 * NIS):
                inner(NG - 1, n)
            down(NG - 1)


def decoder_kernel(nc, x, ctx_2048, mask, in_proj_w, conv_w, conv_b, a_log, d_skip, dt_bias, norm_w, out_proj_w,
                   wq, bq, wk, bk, wv, bv, wo, qn_w, kn_w, gate_w, w_gate, w_up, w_down, ws_gate, ws_up, ws_down, out):
    x1 = nc.dram_tensor("x1", [B, T, H], F32, kind="Internal").ap()
    x2 = nc.dram_tensor("x2", [B, T, H], F32, kind="Internal").ap()
    phase_a(nc, x, in_proj_w, conv_w, conv_b, a_log, d_skip, dt_bias, norm_w, out_proj_w, x1)
    phase_b(nc, x1, ctx_2048, mask, wq, bq, wk, bk, wv, bv, wo, qn_w, kn_w, x2)
    phase_c(nc, x2, gate_w, w_gate, w_up, w_down, ws_gate, ws_up, ws_down, out)


_INS = ['x', 'ctx_2048', 'mask_1xSxS2_ff0', 'L0_attn_in_proj_w', 'L0_attn_conv_w', 'L0_attn_conv_b', 'L0_attn_A_log', 'L0_attn_D',
        'L0_attn_dt_bias', 'L0_attn_norm_w', 'L0_attn_out_proj_w', 'L0_xattn_Wq', 'L0_xattn_bq', 'L0_xattn_Wk', 'L0_xattn_bk',
        'L0_xattn_Wv', 'L0_xattn_bv', 'L0_xattn_Wo', 'L0_xattn_qn_w', 'L0_xattn_kn_w', 'L0_ffn_gate_w', 'L0_ffn_w_gate',
        'L0_ffn_w_up', 'L0_ffn_w_down', 'L0_ffn_ws_gate', 'L0_ffn_ws_up', 'L0_ffn_ws_down']
_OUTS = [((32, 100, 512), 'float32')]


def kernel(**inputs):
    import numpy as _np
    import concourse.bacc as _bacc
    from concourse import mybir as _mybir
    from concourse.bass_utils import run_bass_kernel_spmd as _run

    nc = _bacc.Bacc("TRN2", target_bir_lowering=False, num_devices=1)
    arrays, args = {}, []
    for name in _INS:
        a = _np.ascontiguousarray(inputs[name])
        arrays[f"in_{name}_dram"] = a
        args.append(nc.dram_tensor(f"in_{name}_dram", a.shape, _mybir.dt.from_np(a.dtype), kind="ExternalInput").ap())
    for i, (shape, dtype) in enumerate(_OUTS):
        dt = _mybir.dt.from_np(_np.dtype(dtype))
        args.append(nc.dram_tensor(f"out_{i}_dram", shape, dt, kind="ExternalOutput").ap())
    decoder_kernel(nc, *args)
    r = _run(nc, [arrays], core_ids=[0])
    got = tuple(r.results[0][f"out_{i}_dram"] for i in range(len(_OUTS)))
    return got[0]
```

```python
from contextlib import ExitStack

import concourse.bass as bass
from concourse import mybir

F32 = mybir.dt.float32
BF16 = mybir.dt.bfloat16
FR = mybir.dt.float32r
I32 = mybir.dt.int32
U32 = mybir.dt.uint32
ALU = mybir.AluOpType
ACT = mybir.ActivationFunctionType

P = 128
B = 32
T = 100
H = 512
KT = H // P


TABLES = "natural_log_exp_and_others"

E_MAX = 2.0 ** 63


def at_least(eng, sem, value):
    if not isinstance(value, int) or value > 0:
        eng.wait_ge(sem, value)


PARTS = ((0, 0), (0, 1), (1, 0))

CELLS = 16


def hold_vector(eng, cells):
    n = cells[1].pop(0)
    cells[1].append(n)
    eng.memset(cells[0][0:1, n:n + 1], 0.0)


def hold_pool(eng, cells, held, times):
    at_least(eng, held, times)
    eng.tensor_tensor(cells[0:1, 2:3], cells[0:1, 0:1], cells[0:1, 1:2], ALU.add).then_inc(held, 1)


class Memory:

    def __init__(self, nc, stack, tag):
        self.nc, self.stack, self.tag, self.sems = nc, stack, tag, []
        stack.callback(self.clear)

    def clear(self):
        if self.sems:
            self.nc.clear_and_free_semaphores(self.sems)
            self.nc.all_engine_barrier()

    def sb(self, name, shape, dt=F32):
        return self.stack.enter_context(self.nc.sbuf_tensor(f"{self.tag}_{name}", shape, dt))

    def ps(self, name, shape, dt=F32):
        return self.stack.enter_context(self.nc.psum_tensor(f"{self.tag}_{name}", shape, dt))

    def sem(self, name):
        self.sems.append(self.nc.alloc_semaphore(name=f"{self.tag}_{name}"))
        return self.sems[-1]


INTER = 1024
NSTATE = 128
HEADS = 64
PD = INTER // HEADS
CONV = INTER + 2 * NSTATE
CT = CONV // P
XT = INTER // P
HH = HEADS // 2
PAIRS = B // 2
HB = 4
NBLK = HEADS // HB
LAG = 3
W2 = 2 * T


def phase_a(nc, x, w_in, conv_w, conv_b, a_log, d_skip, dt_bias, norm_w, w_out, x1):
    with ExitStack() as stack:
        m = Memory(nc, stack, "a")
        sb, ps, sem = m.sb, m.ps, m.sem
        win = sb("win", [P, KT, 2 * INTER + 2 * NSTATE + HEADS])
        wdt = sb("wdt", [P, KT, 2, 3, HH])
        wout = sb("wout", [P, XT, H])
        ident = sb("ident", [P, P])
        eye4 = sb("eye4", [T, HB, T])
        sel = sb("sel", [96, HH, T], BF16)
        cw = sb("cw", [P, CT, 4])
        cb = sb("cb", [P, CT])
        nw = sb("nw", [P, XT])
        a_neg = sb("a_neg", [96, 2])
        dtb = sb("dtb", [96, 2])
        dsk = sb("dsk", [T, HEADS])
        eps = sb("eps", [P, 1])
        cell = (sb("cells", [1, CELLS]), list(range(CELLS)))
        xl = sb("xl", [T, 2, 2, H])
        stats = sb("stats", [T, 2, 6])
        mv = sb("mv", [T, 2, 2])
        lnv = sb("lnv", [T, 2])
        rstd = sb("rstd", [T, 2])
        hn = sb("hn", [T, 2, H])
        hT = sb("hT", [P, KT, W2])
        acc = sb("acc", [P, 2, 2, W2])
        sg = sb("sg", [P, 2, 2 * W2])
        xc = sb("xc", [P, 2, CT, W2])
        szt = sb("szt", [T, 2, 512])
        sz = sb("sz", [T, 2, 2, INTER])
        dtu = sb("dtu", [96, 2, W2])
        dtm = sb("dtm", [96, 6, 2 * W2])
        dt = sb("dt", [96, 2, 2, W2])
        da = sb("da", [96, 2, 2, T])
        res = sb("res", [96, 2, 2, T])
        mid = sb("mid", [96, 2, 2, T], BF16)
        das = sb("das", [96, 2, 2, 2, T], BF16)
        gd = sb("gd", [T, 2, T + HEADS])
        xt = sb("xt", [T, INTER])
        dx = sb("dx", [T, 2, INTER])
        dtx = sb("dtx", [T, 2, INTER])
        lmat = sb("lmat", [T, 4, HB * T])
        mmat = sb("mmat", [T, 4, HB, T])
        y1 = sb("y1", [T, INTER])
        ysq = sb("ysq", [T, INTER])
        ss = sb("ss", [T, 2, 3])
        yz = sb("yz", [T, INTER])
        gT = sb("gT", [P, XT, T])
        xr = sb("xr", [T, 2, H])
        x1o = sb("x1o", [T, 2, H])

        pj = [ps(f"pj{n}", [P, 512]) for n in range(2)]
        sp_ = [ps(f"sp{n}", [P, 512]) for n in range(2)]
        bc = [ps(f"bc{n}", [P, 512]) for n in range(2)]
        yp = ps("yp", [P, 2, 512])

        s_win_dt, s_win_conv, s_win_z, s_wout, s_small = (sem(n + "_loaded") for n in ("win_dt", "win_conv", "win_z", "wout", "small"))
        s_const, s_prep, s_aneg = sem("const_ready"), sem("prep_ready"), sem("a_neg_ready")
        s_wout_ready, s_wdt = sem("wout_ready"), sem("wdt_ready")
        s_xl = [sem("xl_loaded0"), sem("xl_loaded1")]
        s_xr = [sem("xr_loaded0"), sem("xr_loaded1")]
        s_st = [sem("x1_stored0"), sem("x1_stored1")]
        s_stats, s_mv, s_lnv, s_rstd, s_h = sem("stats"), sem("mv"), sem("lnv"), sem("rstd"), sem("h")
        s_pj, s_hT = sem("proj_in_psum"), sem("hT")
        s_tap0, s_taps, s_exp, s_e1, s_cl, s_rec, s_xc = (sem(n) for n in ("tap0", "taps", "cexp", "cmin", "cln", "csigm", "xc"))
        s_ze, s_z1, s_zl, s_zr, s_sz = (sem(n) for n in ("zexp", "zmin", "zln", "zsigm", "sz"))
        s_dtu, s_dn, s_dv, s_dw, s_dl, s_dr = (sem(n) for n in ("dt_u", "dt_neg", "dt_exp", "dt_w", "dt_ln", "dt_rec"))
        s_dpre, s_dm, s_dt, s_da, s_da0, s_split = (sem(n) for n in ("dt_pre", "dt_mul", "dt", "da", "da0", "da_split"))
        s_sp, s_gd, s_xt, s_dx, s_dtx = (sem(n) for n in ("ssm_in_psum", "gd", "xt", "dx", "dtx"))
        s_bc, s_L, s_M, s_y = (sem(n) for n in ("decay_bc", "L", "M", "y_heads"))
        s_y1, s_ssq, s_sln, s_rs, s_yz, s_gT, s_x1 = (sem(n) for n in ("y1", "ssq", "sln", "rs", "yz", "gT", "x1"))

        block = stack.enter_context(nc.Block())
        UP = 12
        U_HT, U_DT, U_CV, U_Z = 0, 2, 3, 8
        NCV = CT // 2

        def pj_free(eng, g, n):
            if n < 2:
                g, n = g - 1, n + UP
                if isinstance(g, int) and g < 0:
                    return
            u = n - 2
            if u < U_DT:
                eng.wait_ge(s_hT, 2 * g + u + 1)
            elif u == U_DT:
                eng.wait_ge(s_dtu, 2 * g + 2)
            elif u < U_Z:
                eng.wait_ge(s_taps, 6 * (NCV * g + u - U_CV) + 6)
            else:
                eng.wait_ge(s_sz, 4 * g + u - U_Z + 1)

        US = 6

        def sp_free(eng, s, n):
            if n < 2:
                s, n = s - 1, n + US
                if isinstance(s, int) and s < 0:
                    return
            u = n - 2
            if u == 0:
                eng.wait_ge(s_gd, s + 1)
            elif u in (1, 2):
                eng.wait_ge(s_dtx, 2 * s + u)
            elif u in (3, 4):
                at_least(eng, s_gT, 2 * (s - 1) + u - 2)
            else:
                at_least(eng, s_x1, s)

        PLAN = {(0, 1): ["ln"], (0, 3): ["hT"], (0, 4): ["dt"], (0, 6): ["dt2"], (0, 7): ["cv0", "dt3"], (0, 9): ["cw0"],
                (0, 10): ["dtr", "cx0"], (0, 11): ["cv1"], (0, 12): ["dt4"], (0, 13): ["cw1"], (0, 14): ["cx1", "cv2", "dt5"],
                (0, 15): ["cw2"], (1, 0): ["cx2"], (1, 1): ["cv3"], (1, 2): ["cw3"], (1, 3): ["cx3"], (1, 4): ["cv4"], (1, 5): ["cw4"],
                (1, 6): ["cx4"], (1, 7): ["z0"], (1, 9): ["zz0", "z1"], (1, 10): ["zz1"], (1, 11): ["z2"], (1, 12): ["zz2"],
                (1, 13): ["z3"], (1, 14): ["zz3"]}
        ALL = [i for k in sorted(PLAN) for i in PLAN[k]]

        PROMPT = ("ln", "hT")

        def over_pairs(eng, projection, sequence, tail, late=0):
            for item in ALL:
                projection(item, 0, 0, 0)

            def pair(g, i, p, last=False):
                for j in range(2):
                    def between(b, j=j):
                        if not last:
                            prompt = [n for n in PLAN.get((j, b), []) if n in PROMPT]
                            others = [n for n in PLAN.get(divmod(NBLK * j + b - late, NBLK), []) if n not in PROMPT]
                            for item in prompt + others:
                                projection(item, g + 1, i + p, 1 - p)
                    sequence(g, i, p, j, between)

            pair(0, 0, 0)
            pair(1, 0, 1)
            with eng.Fori(1, PAIRS // 2 - 1) as i:
                pair(2 * i, i, 0)
                pair(2 * i + 1, i, 1)
            n = PAIRS // 2 - 1
            pair(2 * n, n, 0)
            pair(2 * n + 1, n, 1, last=True)
            tail(2 * n + 2, n + 1, 0, 0)

        @block.sync
        def _(eng):
            for r in range(3):
                for src, dst in ((a_log, a_neg), (dt_bias, dtb)):
                    eng.dma_start(dst[HH * r:HH * r + HH, :], src.rearrange("(h r) -> r h", h=2),
                                  allow_slow_non_contiguous=True).then_inc(s_small, 16)
            eng.dma_start(cw[:, :, :], conv_w.rearrange("(c p) k -> p c k", p=P), allow_slow_non_contiguous=True).then_inc(s_small, 16)
            eng.dma_start(cb[:, :], conv_b.rearrange("(c p) -> p c", p=P), allow_slow_non_contiguous=True).then_inc(s_small, 16)
            eng.dma_start(nw[:, :], norm_w.rearrange("(c p) -> p c", p=P), allow_slow_non_contiguous=True).then_inc(s_small, 16)
            eng.dma_start(dsk[:, :], d_skip.rearrange("(a h) -> a h", a=1).to_broadcast([T, HEADS]),
                          allow_slow_non_contiguous=True).then_inc(s_small, 16)

            def load_weights():
                n = 2 * INTER + 2 * NSTATE
                eng.dma_start(win[:, :, n:], w_in[:, n:].rearrange("(k p) n -> p k n", p=P), allow_slow_non_contiguous=True).then_inc(s_win_dt, 16)
                eng.dma_start(win[:, :, INTER:n], w_in[:, INTER:n].rearrange("(k p) n -> p k n", p=P)).then_inc(s_win_conv, 16)
                eng.dma_start(win[:, :, 0:INTER], w_in[:, 0:INTER].rearrange("(k p) n -> p k n", p=P)).then_inc(s_win_z, 16)
                eng.dma_start(wout[:, :, :], w_out.rearrange("(k p) n -> p k n", p=P)).then_inc(s_wout, 16)

            def projection(item, g, i, p):
                if item == "ln":
                    at_least(eng, s_h, 2 * (g - 1))
                    eng.dma_start(xl[:, p, :, :], x[bass.ds(2 * g, 2)].rearrange("j t d -> t j d")).then_inc(s_xl[p], 16)
                    if isinstance(g, int) and g == 0:
                        load_weights()

            def tail(g, i, p, j):
                q = 1 - j
                s = 2 * g + j - 1
                eng.wait_ge(s_x1, s + 1)
                eng.dma_start(x1[bass.ds(s, 1)].rearrange("a t d -> t (a d)"), x1o[:, q, :]).then_inc(s_st[q], 16)

            def sequence(g, i, p, j, between):
                s = 2 * g + j
                at_least(eng, s_x1, s - 1)
                eng.dma_start(xr[:, j, :], x[bass.ds(s, 1)].rearrange("a t d -> t (a d)")).then_inc(s_xr[j], 16)
                for b in range(NBLK):
                    between(b)
                    if b == 7 and not (isinstance(s, int) and s == 0):
                        tail(g, i, p, j)

            over_pairs(eng, projection, sequence, tail)
            eng.wait_ge(s_st[0], 16 * (B // 2))
            eng.wait_ge(s_st[1], 16 * (B // 2))

        @block.gpsimd
        def _(eng):
            eng.memset(ident[:, :], 0.0).then_inc(s_const, 1)
            eng.memset(eye4[:, :, :], 0.0).then_inc(s_const, 1)
            eng.memset(sel[:, :, :], 0.0).then_inc(s_const, 1)
            eng.wait_ge(s_const, 3)
            eng.affine_select(out=ident[:, :], in_=ident[:, :], compare_op=ALU.not_equal, fill=1.0, base=0,
                              pattern=[[-1, P]], channel_multiplier=1).then_inc(s_const, 1)
            eng.affine_select(out=eye4[:, :, :], in_=eye4[:, :, :], compare_op=ALU.not_equal, fill=1.0, base=0,
                              pattern=[[0, HB], [-1, T]], channel_multiplier=1).then_inc(s_const, 1)
            for r in range(3):
                if r:
                    eng.wait_ge(s_const, 5 + r)
                eng.affine_select(out=sel[:, :, :], in_=sel[:, :, :], compare_op=ALU.not_equal, fill=1.0,
                                  base=-HH * r, pattern=[[-1, HH], [0, T]], channel_multiplier=1).then_inc(s_const, 1)
            eng.wait_ge(s_win_dt, 16)
            for h in range(2):
                for r in range(3):
                    eng.tensor_copy(wdt[:, :, h, r, :], win[:, :, 2 * INTER + 2 * NSTATE + HH * h:][:, :, 0:HH]).then_inc(s_wdt, 1)

            def projection(item, g, i, p):
                if item == "dt3":
                    eng.wait_ge(s_dw, 3 * g + 3)
                    eng.tensor_tensor(dtm[:, 3, :], dtm[:, 3, :], dtm[:, 4, :], ALU.add).then_inc(s_dpre, 1)
                    eng.wait_ge(s_dl, g + 1)
                    eng.tensor_tensor(dtm[:, 4, :], dtm[:, 5, :], dtm[:, 4, :], ALU.add).then_inc(s_dpre, 1)
                    eng.wait_ge(s_dpre, 2 * g + 2)
                    eng.tensor_tensor(dtm[:, 4, :], dtm[:, 4, :], dtm[:, 1, :], ALU.mult).then_inc(s_dm, 1)
                elif item == "dtr":
                    eng.wait_ge(s_dm, 2 * g + 1)
                    eng.wait_ge(s_dr, g + 1)
                    eng.tensor_tensor(dtm[:, 4, :], dtm[:, 4, :], dtm[:, 3, :], ALU.mult).then_inc(s_dm, 1)
                elif item.startswith("cx"):
                    c = int(item[2:])
                    k = NCV * g + c
                    q = (p + c) % 2
                    eng.wait_ge(s_rec, k + 1)
                    at_least(eng, s_sp, US * 2 * (g - 1))
                    eng.tensor_tensor(xc[:, p, 2 * c:2 * c + 2, :].rearrange("p a b -> p (a b)"),
                                      acc[:, q, :, :].rearrange("p a b -> p (a b)"), sg[:, q, :], ALU.mult).then_inc(s_xc, 1)

            def sequence(g, i, p, j, between):
                s = 2 * g + j
                for c in range(2):
                    eng.wait_ge(s_xt, 2 * s + c + 1)
                    at_least(eng, s_y1, s - 1)
                    eng.tensor_tensor(dx[:, j, 512 * c:512 * c + 512].rearrange("t (h q) -> t h q", q=PD),
                                      xt[:, 512 * c:512 * c + 512].rearrange("t (h q) -> t h q", q=PD),
                                      dsk[:, 32 * c:32 * c + 32].rearrange("t (h a) -> t h a", a=1).to_broadcast([T, 32, PD]), ALU.mult).then_inc(s_dx, 1)
                for b in range(NBLK):
                    n = NBLK * s + b
                    eng.wait_ge(s_L, n + 1)
                    at_least(eng, s_y, n - 3)
                    eng.tensor_tensor(mmat[:, b % 4, :, :], lmat[:, b % 4, :].rearrange("s (h t) -> s h t", h=HB),
                                      gd[:, j, 0:T].rearrange("s (a t) -> s a t", a=1).to_broadcast([T, HB, T]), ALU.mult).then_inc(s_M, 1)
                    if b == 1 and not (isinstance(s, int) and s == 0):
                        gate(g, i, p, j)
                    between(b)

            def gate(g, i, p, j):
                s = 2 * g + j - 1
                eng.wait_ge(s_y1, s + 1)
                at_least(eng, s_gT, 2 * s)
                eng.tensor_tensor(yz[:, :], y1[:, :], sz[:, p if j else 1 - p, 1 - j, :], ALU.mult).then_inc(s_yz, 1)

            eng.wait_ge(s_small, 160)
            over_pairs(eng, projection, sequence, gate, late=1)

        @block.scalar
        def _(eng):
            eng.preload_act_table_set(TABLES)
            eng.wait_ge(s_small, 160)
            eng.activation(a_neg[:, :], a_neg[:, :], ACT.Exp).then_inc(s_aneg, 1)
            eng.wait_ge(s_aneg, 1)
            eng.mul(a_neg[:, :], a_neg[:, :], -1.0).then_inc(s_aneg, 1)
            eng.wait_ge(s_aneg, 2)
            eng.wait_ge(s_prep, 3)

            def projection(item, g, i, p):
                if item == "ln":
                    eng.wait_ge(s_mv, 2 * g + 2)
                    eng.activation(lnv[:, :], mv[:, :, 1], ACT.Ln, bias=eps[0:T, :]).then_inc(s_lnv, 1)
                    eng.wait_ge(s_lnv, g + 1)
                    eng.activation(rstd[:, :], lnv[:, :], ACT.Exp, scale=-0.5).then_inc(s_rstd, 1)
                elif item == "hT":
                    at_least(eng, s_pj, UP * g)
                    for j in range(2):
                        eng.wait_ge(s_pj, UP * g + j + 1)
                        eng.copy(hT[:, :, T * j:T * j + T], pj[j][:, 0:KT * T].rearrange("p (k t) -> p k t", k=KT)).then_inc(s_hT, 1)
                elif item == "dt2":
                    eng.wait_ge(s_dn, g + 1)
                    eng.activation(dtm[:, 1, :], dtm[:, 0, :], ACT.Exp).then_inc(s_dv, 1)
                elif item == "dt3":
                    eng.wait_ge(s_dw, 3 * g + 1)
                    eng.activation(dtm[:, 5, :], dtm[:, 2, :], ACT.Ln).then_inc(s_dl, 1)
                elif item == "dt4":
                    eng.wait_ge(s_dt, g + 1)
                    at_least(eng, s_split, 5 * g)
                    for h in range(2):
                        eng.activation(da[:, h, :, :].rearrange("p j t -> p (j t)"), dt[:, p, h, :], ACT.Exp, scale=a_neg[:, h:h + 1]).then_inc(s_da, 1)
                elif item.startswith("cv"):
                    c = int(item[2:])
                    k = NCV * g + c
                    q = (p + c) % 2
                    eng.wait_ge(s_pj, UP * g + U_CV + c + 1)
                    at_least(eng, s_xc, k - 1)
                    for a in range(2):
                        t = 2 * c + a
                        eng.activation(acc[:, q, a, :], pj[(U_CV + c) % 2][:, W2 * a:W2 * a + W2], ACT.Identity,
                                       scale=cw[:, t, 3:4], bias=cb[:, t:t + 1]).then_inc(s_tap0, 1)
                elif item.startswith("cw"):
                    c = int(item[2:])
                    k = NCV * g + c
                    q = (p + c) % 2
                    eng.wait_ge(s_taps, 6 * k + 6)
                    eng.activation(sg[:, q, :], acc[:, q, :, :].rearrange("p a b -> p (a b)"), ACT.Exp, scale=-1.0).then_inc(s_exp, 1)
                elif item.startswith("cx"):
                    c = int(item[2:])
                    k = NCV * g + c
                    q = (p + c) % 2
                    eng.wait_ge(s_e1, k + 1)
                    eng.activation(sg[:, q, :], sg[:, q, :], ACT.Ln, bias=1.0).then_inc(s_cl, 1)
                    eng.wait_ge(s_cl, k + 1)
                    eng.activation(sg[:, q, :], sg[:, q, :], ACT.Exp, scale=-1.0).then_inc(s_rec, 1)
                elif item.startswith("zz"):
                    c = int(item[2:])
                    k = 4 * g + c
                    eng.wait_ge(s_z1, k + 1)
                    eng.activation(szt[:, c % 2, :], szt[:, c % 2, :], ACT.Ln, bias=1.0).then_inc(s_zl, 1)
                    eng.wait_ge(s_zl, k + 1)
                    eng.activation(szt[:, c % 2, :], szt[:, c % 2, :], ACT.Exp, scale=-1.0).then_inc(s_zr, 1)
                elif item[0] == "z":
                    c = int(item[1:])
                    k = 4 * g + c
                    eng.wait_ge(s_pj, UP * g + U_Z + c + 1)
                    at_least(eng, s_sz, k - 1)
                    eng.activation(szt[:, c % 2, :], pj[(U_Z + c) % 2][0:T, :], ACT.Exp, scale=-0.25).then_inc(s_ze, 1)

            def tail(g, i, p, j):
                s = 2 * g + j - 1
                for c in range(2):
                    eng.wait_ge(s_sp, US * (s + 1) + 3 + c + 1)
                    eng.copy(gT[:, 4 * c:4 * c + 4, :], sp_[(3 + c) % 2][:, 0:4 * T].rearrange("p (k t) -> p k t", k=4)).then_inc(s_gT, 1)

            def sequence(g, i, p, j, between):
                s = 2 * g + j
                eng.wait_ge(s_sp, US * s + 1)
                at_least(eng, s_M, NBLK * (s - 1))
                eng.copy(gd[:, j, :], sp_[0][0:T, 0:T + HEADS]).then_inc(s_gd, 1)
                for c in range(2):
                    eng.wait_ge(s_sp, US * s + c + 2)
                    at_least(eng, s_dx, 2 * s)
                    eng.copy(xt[:, 512 * c:512 * c + 512], sp_[(1 + c) % 2][0:T, :]).then_inc(s_xt, 1)
                for b in range(NBLK):
                    if b == 1 and not (isinstance(s, int) and s == 0):
                        norm(g, i, p, j)
                    if b == 4 and not (isinstance(s, int) and s == 0):
                        tail(g, i, p, j)
                    between(b)

            def norm(g, i, p, j):
                s = 2 * g + j - 1
                q = 1 - j
                eng.wait_ge(s_y1, s + 1)
                eng.activation(ysq[:, :], y1[:, :], ACT.Square, accum_out=ss[:, q, 0:1]).then_inc(s_ssq, 1)
                eng.wait_ge(s_ssq, s + 1)
                eng.activation(ss[:, q, 1:2], ss[:, q, 0:1], ACT.Ln, scale=1.0 / INTER, bias=eps[0:T, :]).then_inc(s_sln, 1)
                eng.wait_ge(s_sln, s + 1)
                at_least(eng, s_x1, s - 1)
                eng.activation(ss[:, q, 2:3], ss[:, q, 1:2], ACT.Exp, scale=-0.5).then_inc(s_rs, 1)

            def last(g, i, p, j):
                norm(g, i, p, j)
                tail(g, i, p, j)

            over_pairs(eng, projection, sequence, last)

        @block.vector
        def _(eng):
            eng.memset(eps[:, :], 1e-5).then_inc(s_prep, 1)
            eng.wait_ge(s_small, 160)
            eng.tensor_scalar(cw[:, :, :], cw[:, :, :], 0.5, None, ALU.mult).then_inc(s_prep, 1)
            eng.memset(ss[:, :, :], 0.0).then_inc(s_prep, 1)
            eng.wait_ge(s_prep, 3)

            def projection(item, g, i, p):
                if item == "ln":
                    eng.wait_ge(s_xl[p], 16 * (i + 1))
                    for j in range(2):
                        eng.bn_stats(stats[:, j, :], xl[:, p, j, :]).then_inc(s_stats, 1)
                    for j in range(2):
                        eng.wait_ge(s_stats, 2 * g + j + 1)
                        hold_vector(eng, cell)
                        eng.bn_aggr(mv[:, j, :], stats[:, j, :]).then_inc(s_mv, 1)
                elif item == "hT":
                    eng.wait_ge(s_rstd, g + 1)
                    at_least(eng, s_hT, 2 * g)
                    for j in range(2):
                        eng.tensor_scalar(hn[:, j, :], xl[:, p, j, :], mv[:, j, 0:1], rstd[:, j:j + 1], ALU.subtract, ALU.mult).then_inc(s_h, 1)
                elif item == "dt":
                    eng.wait_ge(s_pj, UP * g + U_DT + 1)
                    for h in range(2):
                        eng.tensor_scalar(dtu[:, h, :], pj[U_DT % 2][0:96, W2 * h:W2 * h + W2], dtb[:, h:h + 1], None, ALU.add).then_inc(s_dtu, 1)
                    eng.wait_ge(s_dtu, 2 * g + 2)
                    u = dtu[:, :, :].rearrange("p h t -> p (h t)")
                    at_least(eng, s_dm, 2 * g)
                    eng.scalar_tensor_tensor(out=dtm[:, 0, :], in0=u, scalar=-1.0, in1=u, op0=ALU.mult, op1=ALU.min).then_inc(s_dn, 1)
                elif item == "dt3":
                    eng.wait_ge(s_dv, g + 1)
                    eng.tensor_scalar(dtm[:, 2, :], dtm[:, 1, :], 1.0, None, ALU.add).then_inc(s_dw, 1)
                    eng.wait_ge(s_dw, 3 * g + 1)
                    eng.tensor_scalar(dtm[:, 3, :], dtm[:, 2, :], -1.0, None, ALU.add).then_inc(s_dw, 1)
                    eng.wait_ge(s_dw, 3 * g + 2)
                    eng.tensor_scalar(dtm[:, 4, :], dtm[:, 3, :], 0.0, None, ALU.is_equal).then_inc(s_dw, 1)
                elif item == "dtr":
                    eng.wait_ge(s_dpre, 2 * g + 1)
                    eng.reciprocal(dtm[:, 3, :], dtm[:, 3, :]).then_inc(s_dr, 1)
                elif item == "dt4":
                    eng.wait_ge(s_dm, 2 * g + 2)
                    at_least(eng, s_sp, US * 2 * (g - 1))
                    eng.scalar_tensor_tensor(out=dt[:, p, :, :].rearrange("p h t -> p (h t)"), in0=dtu[:, :, :].rearrange("p h t -> p (h t)"),
                                             scalar=0.0, in1=dtm[:, 4, :], op0=ALU.max, op1=ALU.add).then_inc(s_dt, 1)
                elif item == "dt5":
                    eng.wait_ge(s_da, 2 * g + 2)
                    eng.memset(da[:, :, :, 0:1], 0.0).then_inc(s_da0, 1)
                    eng.wait_ge(s_da0, g + 1)
                    at_least(eng, s_bc, NBLK * 2 * (g - 1))
                    eng.tensor_copy(das[:, p, :, :, :], da[:, :, :, :]).then_inc(s_split, 1)
                    eng.wait_ge(s_split, 5 * g + 1)
                    eng.tensor_tensor(res[:, :, :, :], da[:, :, :, :], das[:, p, :, :, :], ALU.subtract).then_inc(s_split, 1)
                    eng.wait_ge(s_split, 5 * g + 2)
                    eng.tensor_copy(mid[:, :, :, :], res[:, :, :, :]).then_inc(s_split, 1)
                    eng.wait_ge(s_split, 5 * g + 3)
                    eng.tensor_copy(das[32:64, p, :, :, :], mid[32:64, :, :, :]).then_inc(s_split, 1)
                    eng.tensor_tensor(das[64:96, p, :, :, :], res[64:96, :, :, :], mid[64:96, :, :, :], ALU.subtract).then_inc(s_split, 1)
                elif item.startswith("cv"):
                    c = int(item[2:])
                    k = NCV * g + c
                    q = (p + c) % 2
                    eng.wait_ge(s_tap0, 2 * k + 2)
                    n = 0
                    for d in (1, 2, 3):
                        for a in range(2):
                            if n >= 2:
                                eng.wait_ge(s_taps, 6 * k + n - 1)
                            o = acc[:, q, a, :].rearrange("p (j t) -> p j t", j=2)[:, :, d:T]
                            src = pj[(U_CV + c) % 2][:, W2 * a:W2 * a + W2].rearrange("p (j t) -> p j t", j=2)[:, :, 0:T - d]
                            eng.scalar_tensor_tensor(out=o, in0=src, scalar=cw[:, 2 * c + a, 3 - d:4 - d], in1=o,
                                                     op0=ALU.mult, op1=ALU.add).then_inc(s_taps, 1)
                            n += 1
                elif item.startswith("cw"):
                    c = int(item[2:])
                    k = NCV * g + c
                    q = (p + c) % 2
                    eng.wait_ge(s_exp, k + 1)
                    eng.tensor_scalar(sg[:, q, :], sg[:, q, :], E_MAX, None, ALU.min).then_inc(s_e1, 1)
                elif item[0] == "z" and item[1] != "z":
                    c = int(item[1:])
                    k = 4 * g + c
                    eng.wait_ge(s_ze, k + 1)
                    eng.tensor_scalar(szt[:, c % 2, :], szt[:, c % 2, :], E_MAX, None, ALU.min).then_inc(s_z1, 1)
                elif item.startswith("zz"):
                    c = int(item[2:])
                    k = 4 * g + c
                    eng.wait_ge(s_zr, k + 1)
                    at_least(eng, s_yz, 2 * (g - 1))
                    eng.scalar_tensor_tensor(out=sz[:, p, c // 2, 512 * (c % 2):512 * (c % 2) + 512], in0=pj[(U_Z + c) % 2][0:T, :],
                                             scalar=0.25, in1=szt[:, c % 2, :], op0=ALU.mult, op1=ALU.mult).then_inc(s_sz, 1)

            def tail(g, i, p, j):
                s = 2 * g + j - 1
                q = 1 - j
                eng.wait_ge(s_sp, US * (s + 1) + 6)
                eng.wait_ge(s_rs, s + 1)
                done = (s - q) // 2 if isinstance(s, int) else g - 1 if j == 0 else g
                eng.wait_ge(s_xr[q], 16 * (done + 1))
                at_least(eng, s_st[q], 16 * done)
                eng.scalar_tensor_tensor(out=x1o[:, q, :], in0=sp_[5 % 2][0:T, :], scalar=ss[:, q, 2:3], in1=xr[:, q, :],
                                         op0=ALU.mult, op1=ALU.add).then_inc(s_x1, 1)

            def sequence(g, i, p, j, between):
                s = 2 * g + j
                if isinstance(s, int) and s == 0:
                    eng.wait_ge(s_wout, 16)
                    for c in range(XT):
                        eng.tensor_scalar(wout[:, c, :], wout[:, c, :], nw[:, c:c + 1], None, ALU.mult).then_inc(s_wout_ready, 1)
                eng.wait_ge(s_gd, s + 1)
                for c in range(2):
                    eng.wait_ge(s_xt, 2 * s + c + 1)
                    at_least(eng, s_y, NBLK * (s - 1))
                    eng.tensor_tensor(dtx[:, j, 512 * c:512 * c + 512].rearrange("t (h q) -> t h q", q=PD),
                                      sp_[(1 + c) % 2][0:T, :].rearrange("t (h q) -> t h q", q=PD),
                                      gd[:, j, T + 32 * c:T + 32 * c + 32].rearrange("t (h a) -> t h a", a=1).to_broadcast([T, 32, PD]), ALU.mult).then_inc(s_dtx, 1)
                for b in range(NBLK):
                    n = NBLK * s + b
                    eng.wait_ge(s_bc, n + 1)
                    at_least(eng, s_M, n - 3)
                    eng.tensor_tensor_scan(lmat[:, b % 4, :], bc[b % 2][0:T, 0:HB * T], eye4[:, :, :].rearrange("s h t -> s (h t)"),
                                           0.0, ALU.mult, ALU.add).then_inc(s_L, 1)
                    if b == 1 and not (isinstance(s, int) and s == 0):
                        add_skip(g, i, p, j)
                    between(b)
                    if b == 10 and not (isinstance(s, int) and s == 0):
                        tail(g, i, p, j)

            def add_skip(g, i, p, j):
                s = 2 * g + j - 1
                eng.wait_ge(s_y, NBLK * s + NBLK)
                eng.wait_ge(s_dx, 2 * s + 2)
                at_least(eng, s_yz, s)
                at_least(eng, s_ssq, s)
                eng.tensor_tensor(y1[:, :], yp[0:T, :, :].rearrange("t a b -> t (a b)"), dx[:, 1 - j, :], ALU.add).then_inc(s_y1, 1)

            def last(g, i, p, j):
                add_skip(g, i, p, j)
                tail(g, i, p, j)

            over_pairs(eng, projection, sequence, last, late=1)

        @block.tensor
        def _(eng):
            eng.wait_ge(s_const, 8)

            def projection(item, g, i, p):
                if item == "hT":
                    for j in range(2):
                        eng.wait_ge(s_h, 2 * g + j + 1)
                        pj_free(eng, g, j)
                        for k in range(KT):
                            mm = eng.transpose(pj[j][:, T * k:T * k + T], hn[:, j, P * k:P * k + P], ident[0:T, 0:T])
                        mm.then_inc(s_pj, 1)
                elif item == "dt":
                    eng.wait_ge(s_hT, 2 * g + 2)
                    if isinstance(g, int) and g == 0:
                        eng.wait_ge(s_wdt, 6)
                    pj_free(eng, g, U_DT)
                    for h in range(2):
                        for k in range(KT):
                            mm = eng.matmul(pj[U_DT % 2][0:96, W2 * h:W2 * h + W2], wdt[:, k, h, :, :].rearrange("p r h -> p (r h)"), hT[:, k, :],
                                            start=(k == 0), stop=(k == KT - 1))
                    mm.then_inc(s_pj, 1)
                elif item.startswith("cv"):
                    c = int(item[2:])
                    if isinstance(g, int) and g == 0:
                        eng.wait_ge(s_win_conv, 16)
                    pj_free(eng, g, U_CV + c)
                    for a in range(2):
                        n = INTER + P * (2 * c + a)
                        for k in range(KT):
                            mm = eng.matmul(pj[(U_CV + c) % 2][:, W2 * a:W2 * a + W2], win[:, k, n:n + P], hT[:, k, :],
                                            start=(k == 0), stop=(k == KT - 1))
                    mm.then_inc(s_pj, 1)
                elif item[0] == "z" and item[1] != "z":
                    c = int(item[1:])
                    j = c // 2
                    if isinstance(g, int) and g == 0:
                        eng.wait_ge(s_win_z, 16)
                    pj_free(eng, g, U_Z + c)
                    for k in range(KT):
                        mm = eng.matmul(pj[(U_Z + c) % 2][0:T, :], hT[:, k, T * j:T * j + T], win[:, k, 512 * (c % 2):512 * (c % 2) + 512],
                                        start=(k == 0), stop=(k == KT - 1))
                    mm.then_inc(s_pj, 1)

            def tail(g, i, p, j, wait=True):
                s = 2 * g + j - 1
                eng.wait_ge(s_yz, s + 1)
                for c in range(2):
                    if wait:
                        sp_free(eng, s + 1, 3 + c)
                    for k in range(4):
                        n = P * (4 * c + k)
                        mm = eng.transpose(sp_[(3 + c) % 2][:, T * k:T * k + T], yz[:, n:n + P], ident[0:T, 0:T])
                    mm.then_inc(s_sp, 1)

            def tail2(g, i, p, j):
                s = 2 * g + j - 1
                eng.wait_ge(s_gT, 2 * s + 2)
                if isinstance(s, int) and s == 0:
                    eng.wait_ge(s_wout_ready, XT)
                for k in range(XT):
                    mm = eng.matmul(sp_[5 % 2][0:T, :], gT[:, k, :], wout[:, k, :], start=(k == 0), stop=(k == XT - 1))
                mm.then_inc(s_sp, 1)

            def sequence(g, i, p, j, between):
                s = 2 * g + j
                first = isinstance(s, int) and s == 0
                cols = slice(T * j, T * j + T)
                eng.wait_ge(s_xc, NCV * g + NCV)
                eng.wait_ge(s_dt, g + 1)
                sp_free(eng, s, 0)
                eng.matmul(sp_[0][0:T, 0:T], xc[:, p, XT, cols], xc[:, p, XT + 1, cols], start=True, stop=True)
                for h in range(2):
                    mm = eng.transpose(sp_[0][0:T, T + HH * h:T + HH * h + HH], dt[0:HH, p, h, cols], ident[0:HH, 0:HH])
                mm.then_inc(s_sp, 1)
                for c in range(2):
                    sp_free(eng, s, 1 + c)
                    for k in range(4):
                        mm = eng.transpose(sp_[(1 + c) % 2][0:T, P * k:P * k + P], xc[:, p, 4 * c + k, cols], ident[:, :])
                    mm.then_inc(s_sp, 1)
                eng.wait_ge(s_split, 5 * g + 5)

                def heads(b):
                    eng.wait_ge(s_M, NBLK * s + b + 1)
                    if b == 0:
                        eng.wait_ge(s_dtx, 2 * s + 2)
                        at_least(eng, s_y1, s)
                    for h in range(HB):
                        n = PD * (HB * b + h)
                        mm = eng.matmul(yp[0:T, n // 512, n % 512:n % 512 + PD], mmat[:, b % 4, h, :], dtx[:, j, n:n + PD], start=True, stop=True)
                    mm.then_inc(s_y, 1)

                for b in range(NBLK):
                    at_least(eng, s_L, NBLK * s + b - 1)
                    for h in range(HB):
                        hd = HB * b + h
                        mm = eng.matmul(bc[b % 2][0:T, T * h:T * h + T], sel[:, hd % HH, :], das[:, p, hd // HH, j, :], start=True, stop=True)
                    mm.then_inc(s_bc, 1)
                    if b >= LAG:
                        heads(b - LAG)
                    if b == 4:
                        if first:
                            eng.nop().then_inc(s_sp, 3)
                        else:
                            tail(g, i, p, j)
                    between(b)
                    if b == 8 and not first:
                        tail2(g, i, p, j)
                for b in range(NBLK - LAG, NBLK):
                    heads(b)

            def last(g, i, p, j):
                eng.wait_ge(s_gT, 2 * B - 2)
                eng.wait_ge(s_x1, B - 1)
                eng.nop().then_inc(s_sp, 3)
                tail(g, i, p, j, False)
                tail2(g, i, p, j)

            over_pairs(eng, projection, sequence, last)


NH, NKV, HD = 16, 4, 128
GRP = NH // NKV
SE = 361
SEP = SE + SE % 2
ET = (SE + P - 1) // P
EREM = SE - (ET - 1) * P
SCALE = float(HD) ** -0.5


def phase_b(nc, x1, ctx, mask, wq, bq, wk, bk, wv, bv, wo, qn_w, kn_w, x2):
    with ExitStack() as stack:
        m = Memory(nc, stack, "b")
        sb, ps, sem = m.sb, m.ps, m.sem
        wq_sb = sb("wq", [P, KT, NH * HD])
        wk_sb = sb("wk", [P, 2, KT, NKV * HD], FR)
        wv_sb = sb("wv", [P, 2, KT, NKV * HD], FR)
        wo_sb = sb("wo", [P, NH, H])
        wk_whole, wv_whole = wo_sb[:, 0:KT, :], wo_sb[:, KT:2 * KT, :]
        bq_sb = sb("bq", [P, NH])
        bk_sb = sb("bk", [P, NKV])
        bv_sb = sb("bv", [P, NKV * HD])
        mask_sb = sb("mask", [T, SE])
        qw = sb("qw", [P, 1])
        kw = sb("kw", [P, 1])
        w_qk = sb("w_qk", [P, 1])
        ident = sb("ident", [P, P])
        ones = sb("ones", [P, P], FR)
        zero = sb("zero", [P, 1])
        eps5 = sb("eps5", [P, 1])
        eps6 = sb("eps6", [P, 1])
        cell = (sb("cells", [1, CELLS]), list(range(CELLS)))
        xl = sb("xl", [T, H])
        cx = sb("cx", [P, ET, H])
        stats = sb("stats", [T, 6])
        mv = sb("mv", [T, 2])
        lnv = sb("lnv", [T, 1])
        rstd = sb("rstd", [T, 1])
        hn = sb("hn", [T, H])
        hT = sb("hT", [P, KT, T])
        cT = sb("cT", [P, 2, KT, SEP], FR)
        kq = sb("kq", [P, 2, GRP * T])
        sq = sb("sq", [P, 2, GRP * T])
        sqp = sb("sqp", [P, 2, 2, GRP * T], FR)
        kT = sb("kT", [P, 2, 2, NKV, SEP], FR)
        v = sb("v", [P, 2, ET, NKV * HD])
        qT = sb("qT", [P, 2, NH, T], FR)
        nmx = sb("nmx", [T, 4])
        prob = sb("prob", [T, 4, ET * P])
        tot = sb("tot", [T, 4])
        rin = sb("rin", [T, 4])
        pT = sb("pT", [P, 2, ET, GRP, T])
        aT = sb("aT", [P, NH, T])
        xr = sb("xr", [T, H])

        pj = [ps(f"pj{n}", [P, 512]) for n in range(2)]
        sc = [ps(f"sc{n}", [P, 512]) for n in range(2)]
        tp = [ps(f"tp{n}", [P, 512]) for n in range(2)]
        po = ps("po", [P, 512])
        pout = ps("pout", [P, 512])

        s_wk, s_wv, s_wq, s_wo, s_small = (sem(n + "_loaded") for n in ("wk", "wv", "wq", "wo", "small"))
        s_const, s_prep = sem("const_ready"), sem("prep_ready")
        s_xl = [sem(f"xl_loaded{n}") for n in range(2)]
        s_cx = [sem(f"ctx_loaded{n}") for n in range(2)]
        s_xr, s_st = sem("xr_loaded"), sem("x2_stored")
        s_stats, s_mv, s_lnv, s_rstd, s_h = (sem(n) for n in ("stats", "mv", "lnv", "rstd", "h"))
        s_pj, s_hT, s_cT, s_cTl = (sem(n) for n in ("proj_in_psum", "hT", "ctxT", "ctxT_low"))
        s_ksplit, s_vsplit, s_ksh, s_ksl, s_qsh, s_qsl = (sem(n) for n in ("wk_split", "wv_split", "k_sq_high", "k_sq_low", "q_sq_high", "q_sq_low"))
        s_kn, s_kh, s_qn, s_qh = (sem(n) for n in ("k_normalised", "k_high", "q_normalised", "q_high"))
        s_kb, s_ksq, s_kln, s_rk, s_kT = (sem(n) for n in ("k_biased", "k_squared", "k_ln", "k_rms", "kT"))
        s_v = sem("v")
        s_qb, s_qsq, s_qln, s_rq, s_qT = (sem(n) for n in ("q_biased", "q_squared", "q_ln", "q_rms", "qT"))
        s_sc, s_tt, s_ex, s_ri, s_pn = (sem(n) for n in ("scores", "masked_max", "exp", "rsum", "probs"))
        s_tp, s_pT, s_pv, s_aT, s_o, s_x2 = (sem(n) for n in ("probs_transposed", "pT", "pv", "aT", "out_proj", "x2"))

        block = stack.enter_context(nc.Block())
        PLAN = [["ln", "c0"], ["c1"], ["c2", "c3"], ["hT", "k0"], ["k1"], ["ks0"], ["ks1", "k2"], ["v0"], ["ks2", "k3"], ["v1"],
                ["q0", "ks3"], ["q1"], ["qs0", "q2", "qs1"], ["q3"], ["qs2", "v2"], ["qs3"]]
        OUT_AT = (0, 1, 2, 5)
        ALL = [i for b in PLAN for i in b]
        USES = [i for i in ALL if i != "ln"]
        UP = len(USES)
        assert UP % 2 == 0

        def use(item, s):
            return UP * s + USES.index(item) + 1

        def bank(item):
            return pj[USES.index(item) % 2]

        def pj_free(eng, item, s):
            n = USES.index(item) - 2
            if n < 0:
                s, n = s - 1, n + UP
                if isinstance(s, int) and s < 0:
                    return
            last = USES[n]
            if last == "hT":
                eng.wait_ge(s_hT, s + 1)
            elif last[0] == "c":
                eng.wait_ge(s_cTl, KT * s + int(last[1:]) + 1)
            elif last[0] == "v":
                eng.wait_ge(s_v, ET * s + int(last[1:]) + 1)
            else:
                done = {"k": s_ksq, "ks": s_kln, "q": s_qb, "qs": s_qln}[last.rstrip("0123")]
                eng.wait_ge(done, NKV * s + int(last[-1]) + 1)

        def lagged(s, p, b, lag):
            if b >= lag:
                return s, p, b - lag
            if isinstance(s, int) and s == 0:
                return None
            return s - 1, 1 - p, b - lag + NH

        def over_sequences(eng, projection, head):
            for item in ALL:
                projection(item, 0, 0, 0)

            def one(s, i, p, last=False):
                for b in range(NH):
                    head(s, p, b, i)
                    if not last:
                        for item in PLAN[b]:
                            projection(item, s + 1, i + p, 1 - p)

            one(0, 0, 0)
            one(1, 0, 1)
            with eng.Fori(1, B // 2 - 1) as i:
                one(2 * i, i, 0)
                one(2 * i + 1, i, 1)
            n = B // 2 - 1
            one(B - 2, n, 0)
            one(B - 1, n, 1, last=True)
            for b in range(8):
                head(B, 0, b, n + 1)

        def live(s):
            return not (isinstance(s, int) and s == B)

        def whole(ap):
            return ap.bitcast(F32)

        def split_weights(eng, w, parts, loaded, split):
            high, low = (parts[:, part, :, :] for part in range(2))
            eng.wait_ge(loaded, 16)
            eng.tensor_copy(high, w).then_inc(split, 1)
            eng.wait_ge(split, 1)
            eng.tensor_tensor(low, w, whole(high), ALU.subtract).then_inc(split, 1)

        def split_squares(eng, n, cols, rounded, split, k):
            eng.tensor_tensor(sqp[:, n % 2, 0, 0:cols], sq[:, n % 2, 0:cols], zero[:, :].to_broadcast([P, cols]), ALU.add).then_inc(rounded, 1)
            eng.wait_ge(rounded, k + 1)
            eng.tensor_tensor(sqp[:, n % 2, 1, 0:cols], sq[:, n % 2, 0:cols], whole(sqp[:, n % 2, 0, 0:cols]), ALU.subtract).then_inc(split, 1)

        @block.sync
        def _(eng):
            for dst, src in ((bq_sb, bq), (bk_sb, bk), (qw, qn_w), (kw, kn_w)):
                eng.dma_start(dst[:, :], src.rearrange("(h p) -> p h", p=P), allow_slow_non_contiguous=True).then_inc(s_small, 16)
            eng.dma_start(bv_sb[:, :], bv.rearrange("(a n) -> a n", a=1).to_broadcast([P, NKV * HD])).then_inc(s_small, 16)
            eng.dma_start(mask_sb[:, :], mask.rearrange("a t e -> (a t) e")).then_inc(s_small, 16)

            def load_weights():
                for w_sb, w, loaded in ((wk_whole, wk, s_wk), (wv_whole, wv, s_wv), (wq_sb[:, :, :], wq, s_wq)):
                    eng.dma_start(w_sb, w.rearrange("(k p) n -> p k n", p=P)).then_inc(loaded, 16)

            def projection(item, s, i, p):
                if item == "ln":
                    at_least(eng, s_h, s)
                    eng.dma_start(xl[:, :], x1[bass.ds(s, 1)].rearrange("a t d -> t (a d)")).then_inc(s_xl[p], 16)
                    at_least(eng, s_pj, use("c3", s - 1))
                    eng.dma_start(cx[:, 0:ET - 1, :], ctx[bass.ds(s, 1), 0:P * (ET - 1), :].rearrange("a (e p) d -> p (a e) d", p=P)).then_inc(s_cx[p], 16)
                    eng.dma_start(cx[0:EREM, ET - 1, :], ctx[bass.ds(s, 1), P * (ET - 1):SE, :].rearrange("a e d -> e (a d)")).then_inc(s_cx[p], 16)
                    if isinstance(s, int) and s == 0:
                        load_weights()

            def head(s, p, b, i):
                if b == 0 and isinstance(s, int) and s == 0:
                    load_residual(s)
                if b == 0 and isinstance(s, int) and s == 0:
                    eng.wait_ge(s_ksplit, 2)
                    eng.wait_ge(s_vsplit, 2)
                    eng.dma_start(wo_sb[:, :, :], wo.rearrange("(k p) n -> p k n", p=P)).then_inc(s_wo, 16)
                if b == 6 and not (isinstance(s, int) and s == 0):
                    eng.wait_ge(s_x2, s)
                    eng.dma_start(x2[bass.ds(s - 1, 1)].rearrange("a t d -> t (a d)"), xr[:, :]).then_inc(s_st, 16)
                    if live(s):
                        eng.wait_ge(s_st, 16 * s)
                        load_residual(s)

            def load_residual(s):
                eng.dma_start(xr[:, :], x1[bass.ds(s, 1)].rearrange("a t d -> t (a d)")).then_inc(s_xr, 16)

            over_sequences(eng, projection, head)
            eng.wait_ge(s_st, 16 * B)

        @block.gpsimd
        def _(eng):
            eng.memset(ident[:, :], 0.0).then_inc(s_const, 1)
            eng.memset(sq[:, 1, 0:2 * KT], 0.0).then_inc(s_const, 1)
            eng.memset(sq[:, 0, 0:P], 1.0).then_inc(s_const, 1)
            eng.memset(prob[:, :, :], 0.0).then_inc(s_const, 1)
            eng.memset(zero[:, :], 0.0).then_inc(s_const, 1)
            eng.memset(eps5[:, :], 1e-5).then_inc(s_const, 1)
            eng.memset(eps6[:, :], 1e-6).then_inc(s_const, 1)
            eng.wait_ge(s_const, 7)
            eng.tensor_copy(ones[:, :], sq[:, 0, 0:P]).then_inc(s_const, 1)
            eng.tensor_copy(cT[:, :, :, SE:SEP], sq[:, 1, 0:2 * KT * (SEP - SE)].rearrange("p (a k n) -> p a k n", a=2, k=KT)).then_inc(s_const, 1)
            eng.affine_select(out=ident[:, :], in_=ident[:, :], compare_op=ALU.not_equal, fill=1.0, base=0,
                              pattern=[[-1, P]], channel_multiplier=1).then_inc(s_const, 1)

            split_weights(eng, wv_whole, wv_sb, s_wv, s_vsplit)

            def projection(item, s, i, p):
                if item.startswith("ks"):
                    n = int(item[2:])
                    k = NKV * s + n
                    eng.wait_ge(s_rk, k + 1)
                    at_least(eng, s_sc, NH * (s - 1))
                    k_ = kq[:, n % 2, 0:SEP]
                    eng.tensor_tensor(k_, k_, sq[:, n % 2, 0:SEP], ALU.mult).then_inc(s_kn, 1)
                    eng.wait_ge(s_kn, k + 1)
                    eng.tensor_tensor(kT[:, p, 0, n, :], k_, zero[:, :].to_broadcast([P, SEP]), ALU.add).then_inc(s_kh, 1)
                    eng.wait_ge(s_kh, k + 1)
                    eng.tensor_tensor(kT[:, p, 1, n, :], k_, whole(kT[:, p, 0, n, :]), ALU.subtract).then_inc(s_kT, 1)
                elif item[0] == "k":
                    n = int(item[1:])
                    eng.wait_ge(s_ksq, NKV * s + n + 1)
                    at_least(eng, s_pj, use(f"ks{n - 2}", s) if n >= 2 else use(f"qs{n + 2}", s - 1))
                    split_squares(eng, n, SEP, s_ksh, s_ksl, NKV * s + n)

            over_sequences(eng, projection, lambda *a: None)

        @block.scalar
        def _(eng):
            eng.preload_act_table_set(TABLES)
            eng.wait_ge(s_const, 10)
            eng.wait_ge(s_small, 96)

            def projection(item, s, i, p):
                if item == "ln":
                    eng.wait_ge(s_mv, s + 1)
                    eng.activation(lnv[:, :], mv[:, 1:2], ACT.Ln, bias=eps5[0:T, :]).then_inc(s_lnv, 1)
                    eng.wait_ge(s_lnv, s + 1)
                    eng.activation(rstd[:, :], lnv[:, :], ACT.Exp, scale=-0.5).then_inc(s_rstd, 1)
                elif item == "hT":
                    eng.wait_ge(s_pj, use(item, s))
                    eng.copy(hT[:, :, :], bank(item)[:, 0:KT * T].rearrange("p (k t) -> p k t", k=KT)).then_inc(s_hT, 1)
                elif item.startswith("c"):
                    eng.wait_ge(s_pj, use(item, s))
                    eng.copy(cT[:, 0, int(item[1:]), 0:SE], bank(item)[:, 0:SE]).then_inc(s_cT, 1)
                elif item.startswith("ks") or item.startswith("qs"):
                    n = int(item[2:])
                    k = NKV * s + n
                    ln, done, cols = (s_kln, s_rk, SEP) if item[0] == "k" else (s_qln, s_rq, GRP * T)
                    eng.wait_ge(s_pj, use(item, s))
                    eng.activation(sq[:, n % 2, 0:cols], bank(item)[:, 0:cols], ACT.Ln, scale=1.0 / HD, bias=eps6[:, :]).then_inc(ln, 1)
                    eng.wait_ge(ln, k + 1)
                    eng.activation(sq[:, n % 2, 0:cols], sq[:, n % 2, 0:cols], ACT.Exp, scale=-0.5).then_inc(done, 1)
                elif item[0] == "k":
                    n = int(item[1:])
                    k = NKV * s + n
                    eng.wait_ge(s_pj, use(item, s))
                    at_least(eng, s_kT, k - 1)
                    if n < 2:
                        at_least(eng, s_qT, NKV * s - 1 + n)
                    eng.activation(kq[:, n % 2, 0:SEP], bank(item)[:, 0:SEP], ACT.Identity, bias=bk_sb[:, n:n + 1]).then_inc(s_kb, 1)
                    eng.activation(sq[:, n % 2, 0:SEP], bank(item)[:, 0:SEP], ACT.Square, bias=bk_sb[:, n:n + 1]).then_inc(s_ksq, 1)
                elif item[0] == "q":
                    n = int(item[1:])
                    k = NKV * s + n
                    eng.wait_ge(s_qb, k + 1)
                    if n < 2:
                        eng.wait_ge(s_kT, NKV * s + 3 + n)
                    eng.activation(sq[:, n % 2, :], kq[:, n % 2, :], ACT.Square).then_inc(s_qsq, 1)

            def head(s, p, b, i):
                if live(s):
                    n = NH * s + b
                    eng.wait_ge(s_tt, n + 1)
                    eng.activation(prob[:, b % 4, 0:SE], prob[:, b % 4, 0:SE], ACT.Exp, scale=-1.0, bias=nmx[:, b % 4:b % 4 + 1],
                                   accum_out=tot[:, b % 4:b % 4 + 1]).then_inc(s_ex, 1)
                at = lagged(s, p, b, 3)
                if at and b < 3 or at and live(s):
                    s_, p_, h = at
                    n = NH * s_ + h
                    eng.wait_ge(s_tp, n + 1)
                    if h % 4 == 0:
                        at_least(eng, s_pv, NKV * s_ + h // 4 - 1)
                    eng.copy(pT[:, (h // 4) % 2, :, h % 4, :], tp[h % 2][:, 0:ET * T].rearrange("p (e t) -> p e t", e=ET)).then_inc(s_pT, 1)
                if b % 4 == 0 and (live(s) or b < 8):
                    at = lagged(s, p, b, 8)
                    if at:
                        s_, p_, h = at
                        n = h // 4
                        eng.wait_ge(s_pv, NKV * s_ + n + 1)
                        if n == 0:
                            at_least(eng, s_o, s_)
                        eng.copy(aT[:, 4 * n:4 * n + 4, :], po[:, 0:GRP * T].rearrange("p (h t) -> p h t", h=GRP)).then_inc(s_aT, 1)

            over_sequences(eng, projection, head)

        @block.vector
        def _(eng):
            eng.wait_ge(s_small, 96)
            eng.wait_ge(s_const, 7)
            eng.scalar_tensor_tensor(out=w_qk[:, :], in0=qw[:, :], scalar=SCALE, in1=kw[:, :], op0=ALU.mult, op1=ALU.mult).then_inc(s_prep, 1)
            eng.wait_ge(s_prep, 1)

            def projection(item, s, i, p):
                if item == "ln":
                    eng.wait_ge(s_xl[p], 16 * (i + 1))
                    eng.bn_stats(stats[:, :], xl[:, :]).then_inc(s_stats, 1)
                    eng.wait_ge(s_stats, s + 1)
                    hold_vector(eng, cell)
                    eng.bn_aggr(mv[:, :], stats[:, :]).then_inc(s_mv, 1)
                elif item == "hT":
                    eng.wait_ge(s_rstd, s + 1)
                    at_least(eng, s_hT, s)
                    eng.tensor_scalar(hn[:, :], xl[:, :], mv[:, 0:1], rstd[:, 0:1], ALU.subtract, ALU.mult).then_inc(s_h, 1)
                elif item[0] == "c":
                    n = int(item[1:])
                    eng.wait_ge(s_cT, KT * s + n + 1)
                    eng.tensor_tensor(cT[:, 1, n, 0:SE], bank(item)[:, 0:SE], whole(cT[:, 0, n, 0:SE]), ALU.subtract).then_inc(s_cTl, 1)
                    if n == KT - 1 and isinstance(s, int) and s == 0:
                        split_weights(eng, wk_whole, wk_sb, s_wk, s_ksplit)
                elif item[0] == "v":
                    e = int(item[1:])
                    rows = P if e < ET - 1 else EREM
                    eng.wait_ge(s_pj, use(item, s))
                    at_least(eng, s_pv, NKV * (s - 1))
                    eng.tensor_tensor(v[0:rows, p, e, :], bank(item)[0:rows, :], bv_sb[0:rows, :], ALU.add).then_inc(s_v, 1)
                elif item.startswith("qs"):
                    n = int(item[2:])
                    if n == NKV - 2:
                        split_queries(s, NKV - 1)
                    if n == NKV - 1:
                        scale_queries(s, p, n - 1)
                        scale_queries(s, p, n)
                elif item[0] == "q":
                    n = int(item[1:])
                    if n:
                        split_queries(s, n - 1)
                    if n >= 2:
                        scale_queries(s, p, n - 2)
                    eng.wait_ge(s_pj, use(item, s))
                    at_least(eng, s_qT, NKV * s + n - 1)
                    if n < 2:
                        eng.wait_ge(s_kT, NKV * s + 3 + n)
                    eng.tensor_tensor(kq[:, n % 2, :].rearrange("p (h t) -> p h t", h=GRP), bank(item)[:, 0:GRP * T].rearrange("p (h t) -> p h t", h=GRP),
                                      bq_sb[:, GRP * n:GRP * n + GRP].rearrange("p (h a) -> p h a", a=1).to_broadcast([P, GRP, T]), ALU.add).then_inc(s_qb, 1)

            def split_queries(s, n):
                eng.wait_ge(s_qsq, NKV * s + n + 1)
                eng.wait_ge(s_pj, use(f"qs{n - 2}" if n >= 2 else f"ks{n + 2}", s))
                split_squares(eng, n, GRP * T, s_qsh, s_qsl, NKV * s + n)

            def scale_queries(s, p, n):
                eng.wait_ge(s_rq, NKV * s + n + 1)
                q_ = kq[:, n % 2, :]
                eng.scalar_tensor_tensor(out=q_, in0=q_, scalar=w_qk[:, 0:1], in1=sq[:, n % 2, :], op0=ALU.mult, op1=ALU.mult).then_inc(s_qn, 1)
                eng.wait_ge(s_qn, NKV * s + n + 1)
                at_least(eng, s_sc, NH * (s - 1) + GRP * (n + 1))
                high, low = (qT[:, part, GRP * n:GRP * n + GRP, :].rearrange("p h t -> p (h t)") for part in range(2))
                eng.tensor_copy(high, q_).then_inc(s_qh, 1)
                eng.wait_ge(s_qh, NKV * s + n + 1)
                eng.tensor_tensor(low, q_, whole(high), ALU.subtract).then_inc(s_qT, 1)

            def head(s, p, b, i):
                if live(s):
                    n = NH * s + b
                    eng.wait_ge(s_sc, n + 1)
                    at_least(eng, s_tp, n - 3)
                    hold_vector(eng, cell)
                    eng.tensor_tensor_reduce(out=prob[:, b % 4, 0:SE], in0=sc[b % 2][0:T, 0:SE], in1=mask_sb[:, :], scale=-1.0, scalar=3.0e38,
                                             op0=ALU.add, op1=ALU.min, accum_out=nmx[:, b % 4:b % 4 + 1]).then_inc(s_tt, 1)
                at = lagged(s, p, b, 1)
                if at and (live(s) or b < 1):
                    s_, p_, h = at
                    n = NH * s_ + h
                    eng.wait_ge(s_ex, n + 1)
                    eng.reciprocal(rin[:, h % 4:h % 4 + 1], tot[:, h % 4:h % 4 + 1]).then_inc(s_ri, 1)
                    eng.wait_ge(s_ri, n + 1)
                    eng.tensor_scalar(prob[:, h % 4, 0:SE], prob[:, h % 4, 0:SE], rin[:, h % 4:h % 4 + 1], None, ALU.mult).then_inc(s_pn, 1)
                if b == 6 and not (isinstance(s, int) and s == 0):
                    eng.wait_ge(s_o, s)
                    eng.wait_ge(s_xr, 16 * s)
                    eng.tensor_tensor(xr[:, :], pout[0:T, :], xr[:, :], ALU.add).then_inc(s_x2, 1)

            over_sequences(eng, projection, head)

        @block.tensor
        def _(eng):
            eng.wait_ge(s_const, 10)

            def projection(item, s, i, p):
                if item == "ln":
                    return
                if isinstance(s, int) and s == 0 and item in ("k0", "v0", "q0"):
                    eng.wait_ge(*{"k": (s_ksplit, 2), "v": (s_vsplit, 2), "q": (s_wq, 16)}[item[0]])
                if item == "hT":
                    eng.wait_ge(s_h, s + 1)
                    pj_free(eng, item, s)
                    for k in range(KT):
                        mm = eng.transpose(bank(item)[:, T * k:T * k + T], hn[:, P * k:P * k + P], ident[0:T, 0:T])
                elif item[0] == "c":
                    k = int(item[1:])
                    if k == 0:
                        eng.wait_ge(s_cx[p], 32 * (i + 1))
                    pj_free(eng, item, s)
                    for e in range(ET):
                        rows = P if e < ET - 1 else EREM
                        mm = eng.transpose(bank(item)[:, P * e:P * e + rows], cx[0:rows, e, P * k:P * k + P], ident[0:rows, 0:rows])
                elif item.startswith("ks"):
                    n = int(item[2:])
                    eng.wait_ge(s_ksl, NKV * s + n + 1)
                    pj_free(eng, item, s)
                    for part in range(2):
                        mm = eng.matmul(bank(item)[:, 0:SEP], ones[:, :], sqp[:, n % 2, part, 0:SEP], start=(part == 0), stop=(part == 1))
                elif item.startswith("qs"):
                    n = int(item[2:])
                    eng.wait_ge(s_qsl, NKV * s + n + 1)
                    pj_free(eng, item, s)
                    for part in range(2):
                        mm = eng.matmul(bank(item)[:, 0:GRP * T], ones[:, :], sqp[:, n % 2, part, :], start=(part == 0), stop=(part == 1))
                elif item[0] == "k":
                    n = int(item[1:])
                    if n == 0:
                        eng.wait_ge(s_cTl, KT * s + KT)
                    pj_free(eng, item, s)
                    for k in range(KT):
                        for a, b in PARTS:
                            mm = eng.matmul(bank(item)[:, 0:SEP], wk_sb[:, a, k, HD * n:HD * n + HD], cT[:, b, k, :],
                                            start=(k == 0 and a == b), stop=(k == KT - 1 and (a, b) == PARTS[-1]))
                elif item[0] == "v":
                    e = int(item[1:])
                    rows = P if e < ET - 1 else EREM
                    pj_free(eng, item, s)
                    for k in range(KT):
                        for a, b in PARTS:
                            mm = eng.matmul(bank(item)[0:rows, :], cT[:, a, k, P * e:P * e + rows], wv_sb[:, b, k, :],
                                            start=(k == 0 and a == b), stop=(k == KT - 1 and (a, b) == PARTS[-1]))
                elif item[0] == "q":
                    n = int(item[1:])
                    if n == 0:
                        eng.wait_ge(s_hT, s + 1)
                    pj_free(eng, item, s)
                    for h in range(GRP):
                        c = HD * (GRP * n + h)
                        for k in range(KT):
                            mm = eng.matmul(bank(item)[:, T * h:T * h + T], wq_sb[:, k, c:c + HD], hT[:, k, :], start=(k == 0), stop=(k == KT - 1))
                mm.then_inc(s_pj, 1)

            def head(s, p, b, i):
                if live(s):
                    n = NH * s + b
                    if b % 4 == 0:
                        eng.wait_ge(s_kT, NKV * s + b // 4 + 1)
                        eng.wait_ge(s_qT, NKV * s + b // 4 + 1)
                    at_least(eng, s_tt, n - 1)
                    for part, (a, c) in enumerate(PARTS):
                        mm = eng.matmul(sc[b % 2][0:T, 0:SEP], qT[:, a, b, :], kT[:, p, c, b // 4, :], start=(part == 0), stop=(part == 2))
                    mm.then_inc(s_sc, 1)
                at = lagged(s, p, b, 2)
                if at and (live(s) or b < 2):
                    s_, p_, h = at
                    n = NH * s_ + h
                    eng.wait_ge(s_pn, n + 1)
                    at_least(eng, s_pT, n - 1)
                    for e in range(ET):
                        mm = eng.transpose(tp[h % 2][:, T * e:T * e + T], prob[:, h % 4, P * e:P * e + P], ident[0:T, 0:T])
                    mm.then_inc(s_tp, 1)
                if b % 4 == 3:
                    at = lagged(s, p, b, 7)
                    if at and (live(s) or b < 7):
                        s_, p_, h = at
                        n = h // 4
                        eng.wait_ge(s_pT, NH * s_ + h + 4)
                        if n == 0:
                            eng.wait_ge(s_v, ET * s_ + ET)
                        at_least(eng, s_aT, NKV * s_ + n)
                        for e in range(ET):
                            rows = P if e < ET - 1 else EREM
                            mm = eng.matmul(po[:, 0:GRP * T], v[0:rows, p_, e, HD * n:HD * n + HD],
                                            pT[0:rows, n % 2, e, :, :].rearrange("p h t -> p (h t)"), start=(e == 0), stop=(e == ET - 1))
                        mm.then_inc(s_pv, 1)
                if b in OUT_AT and not (isinstance(s, int) and s == 0):
                    n = OUT_AT.index(b)
                    eng.wait_ge(s_aT, NKV * (s - 1) + n + 1)
                    if n == 0:
                        at_least(eng, s_x2, s - 1)
                        if isinstance(s, int) and s == 1:
                            eng.wait_ge(s_wo, 16)
                    for h in range(GRP * n, GRP * n + GRP):
                        mm = eng.matmul(pout[0:T, :], aT[:, h, :], wo_sb[:, h, :], start=(h == 0), stop=(h == NH - 1))
                    if n == NKV - 1:
                        mm.then_inc(s_o, 1)

            over_sequences(eng, projection, head)


TOK = B * T
NT = TOK // P
TG = 5
NG = NT // TG
GT = TG * P
HALF = GT // 2
NE, NI, CAP = 16, 352, 256
NS = 704
NIT = [P, P, NI - 2 * P]
NST = [P] * (NS // P) + [NS % P]
CT2 = CAP // P
SLOTS = NE * CAP


def phase_c(nc, x2, gate_w, w_gate, w_up, w_down, ws_gate, ws_up, ws_down, out):
    h_dram = nc.dram_tensor("h_rows", [TOK, H], F32, kind="Internal").ap()
    slot_dram = nc.dram_tensor("slot_token", [SLOTS, 1], U32, kind="Internal").ap()
    e_dram = nc.dram_tensor("expert_rows", [SLOTS, H], F32, kind="Internal").ap()
    x_rows = x2.rearrange("b t d -> (b t) d")
    out_rows = out.rearrange("b t d -> (b t) d")

    def rows(ap, first, tiles):
        return ap[bass.ds(first, tiles * P), :].rearrange("(t p) d -> p t d", p=P)

    with ExitStack() as stack:
        m = Memory(nc, stack, "c")
        sb, ps, sem = m.sb, m.ps, m.sem
        acc = sb("acc", [P, NT, H])
        wts = sb("wts", [P, NT, 2])
        place = sb("place", [P, NT, 2], U32)
        ident = sb("ident", [P, P])
        pool_cells = sb("pool_cells", [1, 3])
        s_const, s_held = sem("const_ready"), sem("pool_held")
        wsg = sb("wsg", [P, KT, NS])
        wsu = sb("wsu", [P, KT, NS])
        wsd = sb("wsd", [P, len(NST), H])
        gw = sb("gw", [NE, H])
        gwT = sb("gwT", [P, KT, NE])
        upper = sb("upper", [P, P], BF16)
        ones = sb("ones", [P, P], BF16)
        iota16 = sb("iota16", [P, TG, NE])
        zero = sb("zero", [P, SLOTS // P], U32)
        eps = sb("eps", [P, 1])
        cell = (sb("cells", [1, CELLS]), list(range(CELLS)))
        tokf = sb("tokf", [P, TG])
        tok = sb("tok", [P, TG], U32)
        stats = sb("stats", [P, TG, 6])
        mv = sb("mv", [P, TG, 2])
        lnv = sb("lnv", [P, TG])
        rstd = sb("rstd", [P, TG])
        hn = sb("hn", [P, TG, H])
        hT = sb("hT", [P, KT, GT])
        mx = sb("mx", [P, TG])
        lg = sb("lg", [P, TG, NE])
        pr = sb("pr", [P, TG, NE])
        tot = sb("tot", [P, TG])
        rtot = sb("rtot", [P, TG])
        m8 = sb("m8", [P, TG, 8])
        i8 = sb("i8", [P, TG, 8], U32)
        idx = sb("idx", [P, 2, TG])
        oh = sb("oh", [P, 2, TG, NE])
        msk = sb("msk", [P, TG, NE], BF16)
        carry = sb("carry", [P, NE])
        pos = sb("pos", [P, TG, NE])
        ohp = sb("ohp", [P, 2, TG, NE])
        pk = sb("pk", [P, 2, TG])
        over = sb("over", [P, 2, TG])
        slot = sb("slot", [P, 2, TG])
        dsl = sb("dsl", [P, 2, TG], U32)
        sg = sb("sg", [P, 2, HALF])
        gs = sb("gs", [P, 2, HALF])
        aT = sb("aT", [P, len(NST), GT])

        tr = [ps(f"tr{n}", [P, 512]) for n in range(2)]
        rt = ps("rt", [P, 512])
        pz = ps("pz", [P, 512])
        pg = [ps(f"pg{n}", [P, 512]) for n in range(2)]
        pu = [ps(f"pu{n}", [P, 512]) for n in range(2)]

        s_w, s_x, s_zero, s_mem = sem("weights_loaded"), sem("x_loaded"), sem("slots_zeroed"), sem("memsets")
        s_hst, s_scat = sem("h_stored"), sem("scattered")
        s_gate, s_gwt, s_gw = sem("gate_loaded"), sem("gate_in_psum"), sem("gate_T")
        s_stats, s_mv, s_lnv, s_rstd, s_h = (sem(n) for n in ("stats", "mv", "lnv", "rstd", "h"))
        s_tr, s_hT, s_lg, s_pos, s_down = sem("h_in_psum"), sem("hT"), sem("logits"), sem("positions"), sem("down")
        s_r, s_ex, s_disp = sem("route_step"), sem("route_exp"), sem("slots")
        s_gu, s_se, s_sm, s_sl, s_ss, s_gs, s_aT, s_acc = (sem(n) for n in (
            "gate_up", "silu_exp", "silu_min", "silu_ln", "silu_sigm", "silu", "aT", "acc"))
        R_MAX, R_SUB, R_SUM, R_REC, R_PROB = 0, 1, 2, 3, 4
        R_TOP = 5
        R_IDX = R_TOP + TG
        R_CVT = R_IDX + TG
        R_OH = R_CVT + 3
        R_MSK = R_OH + 2
        R_POS, R_CARRY = R_MSK + 1, R_MSK + 2
        R_OHP = R_CARRY + 1
        R_PK = R_OHP + 2
        R_OVER, R_MIN, R_SLOT, R_PLACE, R_OUT, R_NEXT = (R_PK + n for n in (1, 2, 3, 4, 5, 6))
        NR = R_NEXT + 1

        NIS = len(NST)
        wgu = sb("wgu", [P, 2, 2, KT, NI])
        wd = sb("wd", [P, 2, len(NIT), H])
        ids = sb("ids", [P, 2, CT2], U32)
        hg = hn[:, 0:2 * CT2, :].rearrange("p (a c) d -> p a c d", a=2)
        hgT = sb("hgT", [P, 2, KT, CAP])
        esg = sb("esg", [P, 2, CAP])
        egs = sb("egs", [P, 2, CAP])
        eaT = sb("eaT", [P, 2, len(NIT), CAP])
        eo = sb("eo", [P, 2, CT2, H])
        gu = [rt, pz, pu[0]]
        dn = pg
        er = wgu[:, :, :, :, :].rearrange("p a b k n -> p (a b k n)")[:, 0:TG * 2 * H].rearrange("p (t k d) -> p t k d", t=TG, k=2)
        s_ew, s_ewd = ([sem(f"{w}_loaded{n}") for n in range(2)] for w in ("gate_up_weights", "down_weights"))
        s_ids = [sem(f"ids_loaded{n}") for n in range(2)]
        s_hg = [sem(f"rows_gathered{n}") for n in range(2)]
        s_es = [sem(f"results_stored{n}") for n in range(2)]
        s_etr, s_ehT, s_egu, s_dn, s_eo = (sem(n) for n in ("rows_in_psum", "rows_T", "expert_gate_up", "expert_down", "results"))
        s_ese, s_esm, s_esl, s_ess, s_egs, s_eaT = (sem("expert_" + n) for n in ("silu_exp", "silu_min", "silu_ln", "silu_sigm", "silu", "aT"))
        s_sum, s_out = sem("summed"), sem("out_stored")
        s_er = [sem(f"result_rows{t}") for t in range(TG)]
        NIE = len(NIT)

        block = stack.enter_context(nc.Block())

        BEFORE = 4

        def over_groups(eng, group):
            group(0)
            with eng.Fori(1, NG - 1) as g:
                group(g)

        def over_experts(eng, expert):
            expert(0, 0, 0)
            expert(1, 0, 1)
            with eng.Fori(1, NE // 2 - 1) as i:
                expert(2 * i, i, 0)
                expert(2 * i + 1, i, 1)
            expert(NE - 2, NE // 2 - 1, 0)
            expert(NE - 1, NE // 2 - 1, 1)

        steps = [n for n in range(BEFORE + 1, 2 * NIS + TG) if n not in (2 * NIS - 2, 2 * NIS - 1)]
        BEHIND = {n: range(0) for n in range(2 * NIS + TG)}
        behind = min(2 * len(steps), NT - TG)
        BEHIND.update((n, range(2 * k, min(2 * k + 2, NT - TG))) for k, n in enumerate(steps))

        @block.sync
        def _(eng):
            for g in range(NG):
                at_least(eng, s_x, 16 * g)
                eng.dma_start(acc[:, TG * g:TG * g + TG, :], rows(x_rows, GT * g, TG)).then_inc(s_x, 16)
                if g == 0:
                    eng.dma_start(gw[:, :], gate_w).then_inc(s_gate, 16)
                    eng.dma_start(wsg[:, :, :], ws_gate.rearrange("(k p) n -> p k n", p=P)).then_inc(s_w, 16)
                    eng.dma_start(wsu[:, :, :], ws_up.rearrange("(k p) n -> p k n", p=P)).then_inc(s_w, 16)
                    n = P * (NIS - 1)
                    eng.dma_start(wsd[:, 0:NIS - 1, :], ws_down[0:n].rearrange("(k p) n -> p k n", p=P)).then_inc(s_w, 16)
                    eng.dma_start(wsd[0:NST[-1], NIS - 1, :], ws_down[n:NS]).then_inc(s_w, 16)
            eng.wait_ge(s_mem, 3)
            eng.dma_start(slot_dram.rearrange("(p n) a -> p (n a)", p=P), zero[:, :]).then_inc(s_zero, 16)

            def store_h(g):
                eng.wait_ge(s_h, TG * g + TG)
                eng.dma_start(rows(h_dram, GT * g, TG), hn[:, :, :]).then_inc(s_hst, 16)

            over_groups(eng, store_h)
            store_h(NG - 1)

            def load_ids(e, p):
                at_least(eng, s_etr, CT2 * (e - 1))
                eng.dma_start(ids[:, p, :], slot_dram[bass.ds(CAP * e, CAP), :].rearrange("(c p) a -> p (c a)", p=P),
                              allow_slow_non_contiguous=True).then_inc(s_ids[p], 16)

            def expert(e, i, p):
                if not (isinstance(e, int) and e < 2):
                    load_ids(e, p)
                at_least(eng, s_egu, NIE * (e - 1))
                for n, w in ((0, w_gate), (1, w_up)):
                    eng.dma_start(wgu[:, p, n, :, :], w[bass.ds(e, 1)].rearrange("a (k p) n -> p (a k) n", p=P)).then_inc(s_ew[p], 16)
                at_least(eng, s_dn, CT2 * (e - 1))
                n = P * (NIE - 1)
                eng.dma_start(wd[:, p, 0:NIE - 1, :], w_down[bass.ds(e, 1), 0:n, :].rearrange("a (k p) n -> p (a k) n", p=P)).then_inc(s_ewd[p], 16)
                eng.dma_start(wd[0:NIT[-1], p, NIE - 1, :], w_down[bass.ds(e, 1), n:NI, :].rearrange("a k n -> k (a n)")).then_inc(s_ewd[p], 16)
                if isinstance(e, int) and e == 1:
                    eng.wait_ge(s_scat, 160 * NG)
                    load_ids(0, 0)
                    load_ids(1, 1)

            over_experts(eng, expert)
            for g in range(NG - 1):
                eng.wait_ge(s_sum, 2 * TG * g + 2 * TG)
                eng.dma_start(rows(out_rows, GT * g, TG), acc[:, TG * g:TG * g + TG, :]).then_inc(s_out, 16)
            for n in range(NT - TG, NT):
                eng.wait_ge(s_sum, 2 * n + 2)
                eng.dma_start(rows(out_rows, P * n, 1), acc[:, n:n + 1, :]).then_inc(s_out, 16)
            eng.wait_ge(s_out, 16 * (NG - 1 + TG))
            eng.wait_ge(s_hst, 16 * NG)
            eng.wait_ge(s_zero, 16)

        @block.gpsimd
        def _(eng):
            eng.memset(ident[:, :], 0.0).then_inc(s_const, 1)
            eng.memset(pool_cells[:, :], 1.0).then_inc(s_const, 1)
            eng.memset(upper[:, :], 1.0).then_inc(s_const, 1)
            eng.memset(ones[:, :], 1.0).then_inc(s_const, 1)
            eng.iota(iota16[:, :, :], pattern=[[0, TG], [1, NE]], base=0, channel_multiplier=0, allow_small_or_imprecise_dtypes=True).then_inc(s_const, 1)
            eng.iota(tokf[:, :], pattern=[[P, TG]], base=0, channel_multiplier=1, allow_small_or_imprecise_dtypes=True).then_inc(s_const, 1)
            eng.wait_ge(s_const, 6)
            eng.affine_select(out=ident[:, :], in_=ident[:, :], compare_op=ALU.not_equal, fill=1.0, base=0,
                              pattern=[[-1, P]], channel_multiplier=1).then_inc(s_const, 1)
            eng.affine_select(out=upper[:, :], in_=upper[:, :], compare_op=ALU.is_gt, fill=0.0, base=0,
                              pattern=[[1, P]], channel_multiplier=-1).then_inc(s_const, 1)
            eng.wait_ge(s_zero, 16)

            def scatter(g):
                eng.wait_ge(s_disp, g + 1)
                hold_pool(eng, pool_cells, s_held, g)
                for k in range(2):
                    for t in range(TG):
                        eng.indirect_dma_start(out=slot_dram, out_offset=bass.IndirectOffsetOnAxis(ap=dsl[:, k, t:t + 1], axis=0),
                                               in_=tok[:, t:t + 1], in_offset=None, bounds_check=SLOTS - 1, oob_is_err=False).then_inc(s_scat, 16)

            over_groups(eng, scatter)
            scatter(NG - 1)
            eng.wait_ge(s_hst, 16 * NG)
            eng.wait_ge(s_tr, TG * NG)

            def expert(e, i, p):
                eng.wait_ge(s_ids[p], 16 * (i + 1))
                at_least(eng, s_etr, CT2 * (e - 1))
                hold_pool(eng, pool_cells, s_held, NG + e)
                for c in range(CT2):
                    eng.indirect_dma_start(out=hg[:, p, c, :], out_offset=None, in_=h_dram,
                                           in_offset=bass.IndirectOffsetOnAxis(ap=ids[:, p, c:c + 1], axis=0)).then_inc(s_hg[p], 16)

            over_experts(eng, expert)
            for p in range(2):
                eng.wait_ge(s_es[p], 16 * (NE // 2))
            eng.wait_ge(s_dn, CT2 * NE)
            for n in range(NT):
                at_least(eng, s_sum, 2 * (n - TG) + 2)
                for k in range(2):
                    eng.indirect_dma_start(out=er[:, n % TG, k, :], out_offset=None, in_=e_dram,
                                           in_offset=bass.IndirectOffsetOnAxis(ap=place[:, n, k:k + 1], axis=0)).then_inc(s_er[n % TG], 16)

        @block.scalar
        def _(eng):
            eng.preload_act_table_set(TABLES)
            eng.wait_ge(s_gwt, 1)
            eng.copy(gwT[:, :, :], rt[:, 0:KT * NE].rearrange("p (k e) -> p k e", k=KT)).then_inc(s_gw, 1)
            eng.wait_ge(s_mem, 3)

            def norm(g):
                eng.wait_ge(s_mv, TG * g + TG)
                eng.activation(lnv[:, :], mv[:, :, 1], ACT.Ln, bias=eps[:, :]).then_inc(s_lnv, 1)
                eng.wait_ge(s_lnv, g + 1)
                eng.activation(rstd[:, :], lnv[:, :], ACT.Exp, scale=-0.5).then_inc(s_rstd, 1)

            def transposed(g):
                at_least(eng, s_gu, 2 * NIS * g)
                for t in range(TG):
                    eng.wait_ge(s_tr, TG * g + t + 1)
                    eng.copy(hT[:, :, P * t:P * t + P], tr[t % 2][:, :].rearrange("p (k t) -> p k t", k=KT)).then_inc(s_hT, 1)

            def softmax(g):
                eng.wait_ge(s_r, NR * g + R_SUB + 1)
                eng.activation(pr[:, :, :], lg[:, :, :], ACT.Exp).then_inc(s_ex, 1)

            def silu(g, n):
                r = NST[n // 2]
                at = 2 * NIS * g + n
                eng.wait_ge(s_gu, at + 1)
                at_least(eng, s_gs, at - 1 if n >= 2 else 2 * NIS * g)
                eng.activation(sg[0:r, n % 2, :], pg[n % 2][0:r, 0:HALF], ACT.Exp, scale=-1.0).then_inc(s_se, 1)
                eng.wait_ge(s_sm, at + 1)
                eng.activation(sg[0:r, n % 2, :], sg[0:r, n % 2, :], ACT.Ln, bias=1.0).then_inc(s_sl, 1)
                eng.wait_ge(s_sl, at + 1)
                eng.activation(sg[0:r, n % 2, :], sg[0:r, n % 2, :], ACT.Exp, scale=-1.0).then_inc(s_ss, 1)

            def group(g):
                softmax(g)
                for n in range(2 * NIS):
                    silu(g, n)
                    if n == 5:
                        norm(g + 1)
                transposed(g + 1)

            norm(0)
            transposed(0)
            over_groups(eng, group)
            softmax(NG - 1)
            for n in range(BEFORE):
                silu(NG - 1, n)

            def results(e, p, i):
                at_least(eng, s_es[p], 16 * i)
                for c in range(CT2):
                    eng.wait_ge(s_dn, CT2 * e + c + 1)
                    eng.copy(eo[:, p, c, :], dn[c][:, :]).then_inc(s_eo, 1)
                eng.wait_ge(s_eo, CT2 * e + CT2)
                eng.dma_start(rows(e_dram, CAP * e, CT2), eo[:, p, :, :]).then_inc(s_es[p], 16)

            def expert(e, i, p):
                for n in range(NIE):
                    at, r = NIE * e + n, NIT[n]
                    q = (p + n) % 2
                    eng.wait_ge(s_egu, at + 1)
                    at_least(eng, s_egs, at - 1)
                    eng.activation(esg[0:r, q, :], gu[n][0:r, 0:CAP], ACT.Exp, scale=-1.0).then_inc(s_ese, 1)
                    eng.wait_ge(s_esm, at + 1)
                    eng.activation(esg[0:r, q, :], esg[0:r, q, :], ACT.Ln, bias=1.0).then_inc(s_esl, 1)
                    eng.wait_ge(s_esl, at + 1)
                    eng.activation(esg[0:r, q, :], esg[0:r, q, :], ACT.Exp, scale=-1.0).then_inc(s_ess, 1)
                if not (isinstance(e, int) and e == NE - 1):
                    gathered(e + 1, 1 - p)
                if not (isinstance(e, int) and e == 0):
                    results(e - 1, 1 - p, i if p else i - 1)

            def gathered(e, p):
                at_least(eng, s_egu, NIE * (e - 1))
                for c in range(CT2):
                    eng.wait_ge(s_etr, CT2 * e + c + 1)
                    eng.copy(hgT[:, p, :, P * c:P * c + P], tr[c][:, :].rearrange("p (k t) -> p k t", k=KT)).then_inc(s_ehT, 1)

            gathered(0, 0)
            over_experts(eng, expert)
            results(NE - 1, 1, NE // 2 - 1)
            for n in range(BEFORE, 2 * NIS):
                silu(NG - 1, n)

        @block.vector
        def _(eng):
            eng.memset(zero[:, :], 0).then_inc(s_mem, 1)
            eng.memset(eps[:, :], 1e-5).then_inc(s_mem, 1)
            eng.memset(carry[:, :], 0.0).then_inc(s_mem, 1)
            eng.wait_ge(s_mem, 3)
            eng.wait_ge(s_const, 8)

            def bc(ap):
                return ap.rearrange("p (t a) -> p t a", a=1).to_broadcast([P, TG, NE])

            def token_row(g, t):
                return acc[:, bass.ds(TG * g + t, 1), :].rearrange("p a d -> p (a d)")

            def moments(g):
                eng.wait_ge(s_x, 16 * g + 16)
                for t in range(TG):
                    eng.bn_stats(stats[:, t, :], token_row(g, t)).then_inc(s_stats, 1)
                for t in range(TG):
                    eng.wait_ge(s_stats, TG * g + t + 1)
                    hold_vector(eng, cell)
                    eng.bn_aggr(mv[:, t, :], stats[:, t, :]).then_inc(s_mv, 1)

            def normalise(g):
                eng.wait_ge(s_rstd, g + 1)
                at_least(eng, s_hst, 16 * g)
                at_least(eng, s_tr, TG * g)
                for t in range(TG):
                    eng.tensor_scalar(hn[:, t, :], token_row(g, t), mv[:, t, 0:1], rstd[:, t:t + 1],
                                      ALU.subtract, ALU.mult).then_inc(s_h, 1)

            def add_down(g, t):
                eng.wait_ge(s_down, TG * g + t + 1)
                eng.tensor_tensor(token_row(g, t), tr[(TG + t) % 2][:, :], token_row(g, t), ALU.add).then_inc(s_acc, 1)

            def route_step(g, step):
                def done(instruction, name):
                    assert step[0] == name, (step, name)
                    instruction.then_inc(s_r, 1)
                    step[0] += 1

                def after(name):
                    eng.wait_ge(s_r, NR * g + name + 1)

                return done, after

            def route(g):
                step = [0]
                done, after = route_step(g, step)

                def rest(t):
                    if not (isinstance(g, int) and g == 0):
                        add_down(g - 1, t)

                eng.wait_ge(s_lg, g + 1)
                logits = rt[:, 0:TG * NE].rearrange("p (t e) -> p t e", t=TG)
                done(eng.reduce_max(mx[:, :], logits, axis=mybir.AxisListType.X), R_MAX)
                after(R_MAX)
                done(eng.tensor_tensor(lg[:, :, :], logits, bc(mx[:, :]), ALU.subtract), R_SUB)
                rest(0)
                eng.wait_ge(s_ex, g + 1)
                done(eng.reduce_sum(tot[:, :], pr[:, :, :], axis=mybir.AxisListType.X), R_SUM)
                after(R_SUM)
                done(eng.reciprocal(rtot[:, :], tot[:, :]), R_REC)
                after(R_REC)
                done(eng.tensor_tensor(pr[:, :, :], pr[:, :, :], bc(rtot[:, :]), ALU.mult), R_PROB)
                rest(1)
                after(R_PROB)
                hold_vector(eng, cell)
                for t in range(TG):
                    done(eng.max(m8[:, t, :], pr[:, t, :]), R_TOP + t)
                rest(2)
                for t in range(TG):
                    after(R_TOP + t)
                    hold_vector(eng, cell)
                    done(eng.max_index(i8[:, t, :], m8[:, t, :], pr[:, t, :]), R_IDX + t)
                after(R_IDX + TG - 1)
                for k in range(2):
                    done(eng.tensor_copy(idx[:, k, :], i8[:, :, k]), R_CVT + k)
                done(eng.tensor_copy(wts[:, bass.ds(TG * g, TG), :], m8[:, :, 0:2]), R_CVT + 2)
                rest(3)
                for k in range(2):
                    after(R_CVT + k)
                    done(eng.tensor_tensor(oh[:, k, :, :], iota16[:, :, :], bc(idx[:, k, :]), ALU.is_equal), R_OH + k)
                after(R_OH + 1)
                at_least(eng, s_pos, g)
                done(eng.tensor_tensor(msk[:, :, :], oh[:, 0, :, :], oh[:, 1, :, :], ALU.add), R_MSK)
                rest(4)
                return step

            def route_end(g, step):
                done, after = route_step(g, step)
                eng.wait_ge(s_pos, g + 1)
                done(eng.tensor_tensor(pos[:, :, :], pz[:, 0:TG * NE].rearrange("p (t e) -> p t e", t=TG),
                                       carry[:, :].rearrange("p (a e) -> p a e", a=1).to_broadcast([P, TG, NE]), ALU.add), R_POS)
                after(R_POS)
                done(eng.tensor_tensor(carry[:, :], carry[:, :], pz[:, TG * NE:TG * NE + NE], ALU.add), R_CARRY)
                for k in range(2):
                    done(eng.tensor_tensor(ohp[:, k, :, :], oh[:, k, :, :], pos[:, :, :], ALU.mult), R_OHP + k)
                after(R_OHP + 1)
                done(eng.reduce_sum(pk[:, :, :].rearrange("p k t -> p (k t)"), ohp[:, :, :, :].rearrange("p k t e -> p (k t) e"),
                                    axis=mybir.AxisListType.X), R_PK)
                after(R_PK)
                done(eng.tensor_scalar(over[:, :, :], pk[:, :, :], float(CAP), float(4 * SLOTS), ALU.is_ge, ALU.mult), R_OVER)
                done(eng.tensor_scalar(pk[:, :, :], pk[:, :, :], float(CAP - 1), None, ALU.min), R_MIN)
                after(R_MIN)
                done(eng.scalar_tensor_tensor(out=slot[:, :, :], in0=idx[:, :, :], scalar=float(CAP), in1=pk[:, :, :], op0=ALU.mult, op1=ALU.add), R_SLOT)
                after(R_SLOT)
                done(eng.tensor_copy(place[:, bass.ds(TG * g, TG), :].rearrange("p t k -> p k t"), slot[:, :, :]), R_PLACE)
                at_least(eng, s_scat, 160 * g)
                done(eng.tensor_copy(tok[:, :], tokf[:, :]), R_OUT)
                after(R_OUT)
                eng.tensor_tensor(dsl[:, :, :], slot[:, :, :], over[:, :, :], ALU.add).then_inc(s_disp, 1)
                done(eng.tensor_scalar(tokf[:, :], tokf[:, :], float(GT), None, ALU.add), R_NEXT)
                assert step[0] == NR

            def silu(g, n):
                r, c = NST[n // 2], n % 2
                at = 2 * NIS * g + n
                eng.wait_ge(s_se, at + 1)
                eng.tensor_scalar(sg[0:r, c, :], sg[0:r, c, :], E_MAX, None, ALU.min).then_inc(s_sm, 1)
                eng.wait_ge(s_ss, at + 1)
                at_least(eng, s_aT, at - 1 if n >= 2 else 2 * NIS * g)
                eng.tensor_tensor(gs[0:r, c, :], pg[c][0:r, 0:HALF], sg[0:r, c, :], ALU.mult).then_inc(s_gs, 1)
                eng.wait_ge(s_gs, at + 1)
                if n == 0:
                    at_least(eng, s_down, TG * g)
                eng.tensor_tensor(aT[0:r, n // 2, HALF * c:HALF * c + HALF], pu[c][0:r, 0:HALF], gs[0:r, c, :], ALU.mult).then_inc(s_aT, 1)

            def group(g):
                step = route(g)
                for n in range(2 * NIS):
                    silu(g, n)
                    if n == 1:
                        route_end(g, step)
                    if n == 4:
                        moments(g + 1)
                    if n == 7:
                        normalise(g + 1)

            moments(0)
            normalise(0)
            over_groups(eng, group)
            route_end(NG - 1, route(NG - 1))
            for n in range(BEFORE):
                silu(NG - 1, n)

            def expert(e, i, p):
                for n in range(NIE):
                    at, r = NIE * e + n, NIT[n]
                    q = (p + n) % 2
                    eng.wait_ge(s_ese, at + 1)
                    eng.tensor_scalar(esg[0:r, q, :], esg[0:r, q, :], E_MAX, None, ALU.min).then_inc(s_esm, 1)
                    eng.wait_ge(s_ess, at + 1)
                    at_least(eng, s_eaT, at - 1)
                    eng.tensor_tensor(egs[0:r, q, :], gu[n][0:r, 0:CAP], esg[0:r, q, :], ALU.mult).then_inc(s_egs, 1)
                    eng.wait_ge(s_egs, at + 1)
                    if n == 0:
                        at_least(eng, s_dn, CT2 * (e - 1))
                    eng.tensor_tensor(eaT[0:r, p, n, :], gu[n][0:r, CAP:2 * CAP], egs[0:r, q, :], ALU.mult).then_inc(s_eaT, 1)

            over_experts(eng, expert)

            def combine(n):
                eng.wait_ge(s_acc, n + 1)
                eng.wait_ge(s_er[n % TG], 32 * (n // TG) + 32)
                for k in range(2):
                    if k:
                        eng.wait_ge(s_sum, 2 * n + 1)
                    eng.scalar_tensor_tensor(out=acc[:, n, :], in0=er[:, n % TG, k, :], scalar=wts[:, n, k:k + 1], in1=acc[:, n, :],
                                             op0=ALU.mult, op1=ALU.add).then_inc(s_sum, 1)

            eng.wait_ge(s_r, NR * NG)
            for n in range(BEFORE, 2 * NIS):
                silu(NG - 1, n)
                for tile in BEHIND.get(n, ()):
                    combine(tile)
            for t in range(TG):
                add_down(NG - 1, t)
                for tile in BEHIND[2 * NIS + t]:
                    combine(tile)
            for n in range(behind, NT):
                combine(n)

        @block.tensor
        def _(eng):
            eng.wait_ge(s_const, 8)
            eng.wait_ge(s_gate, 16)
            for k in range(KT):
                mm = eng.transpose(rt[:, NE * k:NE * k + NE], gw[:, P * k:P * k + P], ident[0:NE, 0:NE])
            mm.then_inc(s_gwt, 1)
            eng.wait_ge(s_gw, 1)

            def head(g):
                for t in range(TG):
                    eng.wait_ge(s_h, TG * g + t + 1)
                    if t < 2:
                        at_least(eng, s_acc, TG * (g - 1))
                        at_least(eng, s_hT, TG * g)
                    else:
                        eng.wait_ge(s_hT, TG * g + t - 1)
                    for k in range(KT):
                        mm = eng.transpose(tr[t % 2][:, P * k:P * k + P], hn[:, t, P * k:P * k + P], ident[:, :])
                    mm.then_inc(s_tr, 1)
                at_least(eng, s_r, NR * g)
                for t in range(TG):
                    eng.wait_ge(s_hT, TG * g + t + 1)
                    for k in range(KT):
                        mm = eng.matmul(rt[:, NE * t:NE * t + NE], hT[:, k, P * t:P * t + P], gwT[:, k, :], start=(k == 0), stop=(k == KT - 1))
                mm.then_inc(s_lg, 1)

            def inner(g, n):
                r, c = NST[n // 2], n % 2
                at_least(eng, s_aT, 2 * NIS * g + n - 1 if n >= 2 else 2 * NIS * g)
                for w, dst in ((wsg, pg[c]), (wsu, pu[c])):
                    for k in range(KT):
                        mm = eng.matmul(dst[0:r, 0:HALF], w[:, k, P * (n // 2):P * (n // 2) + r], hT[:, k, HALF * c:HALF * c + HALF],
                                        start=(k == 0), stop=(k == KT - 1))
                mm.then_inc(s_gu, 1)

            def ranks(g):
                eng.wait_ge(s_r, NR * g + R_MSK + 1)
                for t in range(TG + 1):
                    o = pz[:, NE * t:NE * t + NE]
                    parts = [(ones, u) for u in range(min(t, TG))] + ([(upper, t)] if t < TG else [])
                    for n, (w, u) in enumerate(parts):
                        mm = eng.matmul(o, w[:, :], msk[:, u, :], start=(n == 0), stop=(n == len(parts) - 1))
                mm.then_inc(s_pos, 1)

            def down(g):
                eng.wait_ge(s_aT, 2 * NIS * g + 2 * NIS)
                for t in range(TG):
                    if t >= 2:
                        eng.wait_ge(s_acc, TG * g + t - 1)
                    for n in range(NIS):
                        r = NST[n]
                        mm = eng.matmul(tr[(TG + t) % 2][:, :], aT[0:r, n, P * t:P * t + P], wsd[0:r, n, :], start=(n == 0), stop=(n == NIS - 1))
                    mm.then_inc(s_down, 1)

            def group(g):
                for n in range(2 * NIS):
                    inner(g, n)
                    if n == 1:
                        ranks(g)
                head(g + 1)
                down(g)

            head(0)
            eng.wait_ge(s_w, 64)
            over_groups(eng, group)
            ranks(NG - 1)
            for n in range(BEFORE):
                inner(NG - 1, n)
            eng.wait_ge(s_acc, TG * (NG - 1))
            eng.wait_ge(s_aT, 2 * NIS * (NG - 1) + BEFORE)
            eng.wait_ge(s_r, NR * NG)

            def down_expert(e, p, i):
                eng.wait_ge(s_ewd[p], 32 * (i + 1))
                eng.wait_ge(s_eaT, NIE * e + NIE)
                for c in range(CT2):
                    at_least(eng, s_eo, CT2 * (e - 1) + c + 1)
                    for n in range(NIE):
                        r = NIT[n]
                        mm = eng.matmul(dn[c][:, :], eaT[0:r, p, n, P * c:P * c + P], wd[0:r, p, n, :], start=(n == 0), stop=(n == NIE - 1))
                    mm.then_inc(s_dn, 1)

            def gathered(e, p, i):
                eng.wait_ge(s_hg[p], 16 * CT2 * (i + 1))
                for c in range(CT2):
                    at_least(eng, s_ehT, CT2 * (e - 1) + c + 1)
                    for k in range(KT):
                        mm = eng.transpose(tr[c][:, P * k:P * k + P], hg[:, p, c, P * k:P * k + P], ident[:, :])
                    mm.then_inc(s_etr, 1)

            def expert(e, i, p):
                eng.wait_ge(s_ehT, CT2 * e + CT2)
                eng.wait_ge(s_ew[p], 32 * (i + 1))
                for n in range(NIE):
                    r = NIT[n]
                    at_least(eng, s_eaT, NIE * (e - 1) + n + 1)
                    for half, w in ((0, 0), (CAP, 1)):
                        for k in range(KT):
                            mm = eng.matmul(gu[n][0:r, half:half + CAP], wgu[:, p, w, k, P * n:P * n + r], hgT[:, p, k, :],
                                            start=(k == 0), stop=(k == KT - 1))
                    mm.then_inc(s_egu, 1)
                if not (isinstance(e, int) and e == NE - 1):
                    gathered(e + 1, 1 - p, i + p)
                if not (isinstance(e, int) and e == 0):
                    down_expert(e - 1, 1 - p, i if p else i - 1)

            gathered(0, 0, 0)
            over_experts(eng, expert)
            down_expert(NE - 1, 1, NE // 2 - 1)
            eng.wait_ge(s_eo, CT2 * NE)
            eng.wait_ge(s_ehT, CT2 * NE)
            for n in range(BEFORE, 2 * NIS):
                inner(NG - 1, n)
            down(NG - 1)


def decoder_kernel(nc, x, ctx_2048, mask, in_proj_w, conv_w, conv_b, a_log, d_skip, dt_bias, norm_w, out_proj_w,
                   wq, bq, wk, bk, wv, bv, wo, qn_w, kn_w, gate_w, w_gate, w_up, w_down, ws_gate, ws_up, ws_down, out):
    x1 = nc.dram_tensor("x1", [B, T, H], F32, kind="Internal").ap()
    x2 = nc.dram_tensor("x2", [B, T, H], F32, kind="Internal").ap()
    phase_a(nc, x, in_proj_w, conv_w, conv_b, a_log, d_skip, dt_bias, norm_w, out_proj_w, x1)
    phase_b(nc, x1, ctx_2048, mask, wq, bq, wk, bk, wv, bv, wo, qn_w, kn_w, x2)
    phase_c(nc, x2, gate_w, w_gate, w_up, w_down, ws_gate, ws_up, ws_down, out)


_INS = ['x', 'ctx_2048', 'mask_1xSxS2_ff0', 'L0_attn_in_proj_w', 'L0_attn_conv_w', 'L0_attn_conv_b', 'L0_attn_A_log', 'L0_attn_D',
        'L0_attn_dt_bias', 'L0_attn_norm_w', 'L0_attn_out_proj_w', 'L0_xattn_Wq', 'L0_xattn_bq', 'L0_xattn_Wk', 'L0_xattn_bk',
        'L0_xattn_Wv', 'L0_xattn_bv', 'L0_xattn_Wo', 'L0_xattn_qn_w', 'L0_xattn_kn_w', 'L0_ffn_gate_w', 'L0_ffn_w_gate',
        'L0_ffn_w_up', 'L0_ffn_w_down', 'L0_ffn_ws_gate', 'L0_ffn_ws_up', 'L0_ffn_ws_down']
_OUTS = [((32, 100, 512), 'float32')]


def kernel(**inputs):
    import numpy as _np
    import concourse.bacc as _bacc
    from concourse import mybir as _mybir
    from concourse.bass_utils import run_bass_kernel_spmd as _run

    nc = _bacc.Bacc("TRN2", target_bir_lowering=False, num_devices=1)
    arrays, args = {}, []
    for name in _INS:
        a = _np.ascontiguousarray(inputs[name])
        arrays[f"in_{name}_dram"] = a
        args.append(nc.dram_tensor(f"in_{name}_dram", a.shape, _mybir.dt.from_np(a.dtype), kind="ExternalInput").ap())
    for i, (shape, dtype) in enumerate(_OUTS):
        dt = _mybir.dt.from_np(_np.dtype(dtype))
        args.append(nc.dram_tensor(f"out_{i}_dram", shape, dt, kind="ExternalOutput").ap())
    decoder_kernel(nc, *args)
    r = _run(nc, [arrays], core_ids=[0])
    got = tuple(r.results[0][f"out_{i}_dram"] for i in range(len(_OUTS)))
    return got[0]
```
